# Optimizing a Trainium2 kernel written in Bass

```python
import numpy as np
import jax
import jax.numpy as jnp

def _softmax(x, axis=-1):
    return jax.nn.softmax(x, axis=axis)

def _gelu(x):
    return jax.nn.gelu(x, approximate=True)

def _silu(x):
    return jax.nn.silu(x)

def _sigmoid(x):
    return jax.nn.sigmoid(x)

def _layernorm(x, axis=-1, eps=1e-05):
    m = jnp.mean(x, axis=axis, keepdims=True)
    v = jnp.var(x, axis=axis, keepdims=True)
    return (x - m) / jnp.sqrt(v + eps)

def _scatter_add(tgt, idx, src, axis=0):
    return tgt.at[idx].add(src)

def _segment_sum(src, seg, n):
    return jax.ops.segment_sum(src, seg, n)
kernel_name = 'mk_gnn_resnorm_d4_gnn_r8_61f28d'

def setup_inputs(seed: int=0):
    np.random.seed(seed)
    _w = jnp.asarray

    def _rec_inputs():
        import jax
        import jax.numpy as jnp
        _gk = jax.random.key(seed)
        x = -0.000202 + 1 * jax.random.normal(jax.random.fold_in(_gk, 1), (6250, 128), jnp.float32)
        _s = jax.random.randint(jax.random.fold_in(_gk, 2), (50000,), 0, 6250, jnp.int32)
        _d = jax.random.randint(jax.random.fold_in(_gk, 3), (50000,), 0, 6250, jnp.int32)
        _loop = jnp.arange(6250, dtype=jnp.int32)
        src = jnp.concatenate([_s, _d, _loop])
        dst = jnp.concatenate([_d, _s, _loop])
        _o = jnp.argsort(dst, stable=True)
        src = src[_o]
        dst = dst[_o]
        edge_type_8 = jax.random.randint(jax.random.fold_in(_gk, 12), (106250,), 0, 8, jnp.int32)
        return (x, src, dst, edge_type_8)
    x, src, dst, edge_type_8 = _rec_inputs()

    def _L0_gnn_setup():
        import jax, jax.numpy as jnp
        import numpy as np
        N, E, D = (6250, 75000, 128)
        LN_EPS = 1e-05
        key = jax.random.key(seed)
        ks = jax.random.split(key, 7)
        s = 1.0 / np.sqrt(D)
        x = jax.random.normal(ks[0], (N, D), dtype=jnp.float32)
        edge_index = jax.random.randint(ks[1], (2, E), 0, N, dtype=jnp.int32)
        Wq = jax.random.normal(ks[2], (D, D), dtype=jnp.float32) * s
        Wk = jax.random.normal(ks[3], (D, D), dtype=jnp.float32) * s
        Wv = jax.random.normal(ks[4], (D, D), dtype=jnp.float32) * s
        Wo = jax.random.normal(ks[5], (D, D), dtype=jnp.float32) * s
        bo = jnp.zeros((D,), dtype=jnp.float32)
        gamma = jnp.ones((D,), dtype=jnp.float32)
        beta = jnp.zeros((D,), dtype=jnp.float32)
        return {'x': x, 'edge_index': edge_index, 'Wq': Wq, 'Wk': Wk, 'Wv': Wv, 'Wo': Wo, 'bo': bo, 'gamma': gamma, 'beta': beta}
    _L0_gnn_all = _L0_gnn_setup()
    _L0_gnn_in = {k: v for k, v in _L0_gnn_all.items() if k in ('Wq', 'Wk', 'Wv', 'Wo', 'bo', 'gamma', 'beta')}
    del _L0_gnn_all

    def _L1_gnn_setup():
        import jax, jax.numpy as jnp
        import numpy as np
        N = 12500
        E = 200000
        D_IN = 128
        D_OUT = 128
        HEADS = 4
        C = D_OUT // HEADS
        NEG_SLOPE = 0.2
        EPS_SOFTMAX = 1e-16
        EPS_LN = 1e-05

        def _gat_edge_conv(x, src, dst, W, att_src, att_dst, gat_bias, skip_W, skip_b, ln_g, ln_b):
            n = x.shape[0]
            h = (x @ W).reshape(n, HEADS, C)
            a_s = jnp.einsum('nhc,hc->nh', h, att_src)
            a_d = jnp.einsum('nhc,hc->nh', h, att_dst)
            e = jax.nn.leaky_relu(a_s[src] + a_d[dst], NEG_SLOPE)
            m = jax.ops.segment_max(e, dst, num_segments=n)
            p = jnp.exp(e - m[dst])
            z = jax.ops.segment_sum(p, dst, num_segments=n)
            alpha = p / (z[dst] + EPS_SOFTMAX)
            msg = h[src] * alpha[:, :, None]
            out = jax.ops.segment_sum(msg, dst, num_segments=n)
            out = out.reshape(n, HEADS * C) + gat_bias
            out = out + x @ skip_W + skip_b
            mu = out.mean(-1, keepdims=True)
            var = ((out - mu) ** 2).mean(-1, keepdims=True)
            return (out - mu) * jax.lax.rsqrt(var + EPS_LN) * ln_g + ln_b
        key = jax.random.key(seed)
        ks = jax.random.split(key, 10)
        x = jax.random.normal(ks[0], (N, D_IN), dtype=jnp.float32)
        edge_index = jax.random.randint(ks[1], (2, E), 0, N, dtype=jnp.int64)
        s = 1.0 / np.sqrt(D_IN)
        W = jax.random.normal(ks[2], (D_IN, HEADS * C), dtype=jnp.float32) * s
        att_src = jax.random.normal(ks[3], (HEADS, C), dtype=jnp.float32) * (1.0 / np.sqrt(C))
        att_dst = jax.random.normal(ks[4], (HEADS, C), dtype=jnp.float32) * (1.0 / np.sqrt(C))
        gat_bias = jax.random.normal(ks[5], (D_OUT,), dtype=jnp.float32) * 0.02
        skip_W = jax.random.normal(ks[6], (D_IN, D_OUT), dtype=jnp.float32) * s
        skip_b = jax.random.normal(ks[7], (D_OUT,), dtype=jnp.float32) * 0.02
        ln_g = jnp.ones((D_OUT,), dtype=jnp.float32)
        ln_b = jnp.zeros((D_OUT,), dtype=jnp.float32)
        return {'x': x, 'edge_index': edge_index, 'W': W, 'att_src': att_src, 'att_dst': att_dst, 'gat_bias': gat_bias, 'skip_W': skip_W, 'skip_b': skip_b, 'ln_g': ln_g, 'ln_b': ln_b}
    _L1_gnn_all = _L1_gnn_setup()
    _L1_gnn_in = {k: v for k, v in _L1_gnn_all.items() if k in ('W', 'att_src', 'att_dst', 'gat_bias', 'skip_W', 'skip_b', 'ln_g', 'ln_b')}
    del _L1_gnn_all

    def _L2_gnn_setup():
        import jax, jax.numpy as jnp
        import numpy as np
        N_NODES = 6250
        N_EDGES = 100000
        D = 128

        def _layer_norm(x, gamma, beta, eps=1e-05):
            mu = jnp.mean(x, axis=-1, keepdims=True)
            var = jnp.var(x, axis=-1, keepdims=True)
            return (x - mu) * jax.lax.rsqrt(var + eps) * gamma + beta
        key = jax.random.key(seed)
        ks = jax.random.split(key, 6)
        node_features = jax.random.normal(ks[0], (N_NODES, D), dtype=jnp.float32)
        edge_index = jax.random.randint(ks[1], (2, N_EDGES), 0, N_NODES, dtype=jnp.int64)
        s = 1.0 / np.sqrt(D)
        W1 = jax.random.normal(ks[2], (D, D), dtype=jnp.float32) * s
        b1 = jnp.zeros((D,), dtype=jnp.float32)
        W2 = jax.random.normal(ks[3], (D, D), dtype=jnp.float32) * s
        b2 = jnp.zeros((D,), dtype=jnp.float32)
        eta = jax.random.normal(ks[4], (1, 1), dtype=jnp.float32) * 0.5
        ln_gamma = jnp.ones((D,), dtype=jnp.float32)
        ln_beta = jnp.zeros((D,), dtype=jnp.float32)
        return {'node_features': node_features, 'edge_index': edge_index, 'W1': W1, 'b1': b1, 'W2': W2, 'b2': b2, 'eta': eta, 'ln_gamma': ln_gamma, 'ln_beta': ln_beta}
    _L2_gnn_all = _L2_gnn_setup()
    _L2_gnn_in = {k: v for k, v in _L2_gnn_all.items() if k in ('W1', 'b1', 'W2', 'b2', 'eta', 'ln_gamma', 'ln_beta')}
    del _L2_gnn_all

    def _L3_gnn_setup():
        import jax, jax.numpy as jnp
        import numpy as np
        N = 6250
        E = 200000
        C = 128
        R = 8

        def _rgcn_layer(h, src, dst, et, W, SW, b, activate, residual):
            xw = jnp.einsum('nc,rco->rno', h, W)
            msg = xw[et, src]
            agg = jax.ops.segment_sum(msg, dst, num_segments=N)
            out = h @ SW + agg
            if residual:
                out = out + h
            if activate:
                out = jax.nn.relu(out)
            return out + b
        key = jax.random.key(seed)
        ks = jax.random.split(key, 9)
        scale = 1.0 / np.sqrt(C)
        return {'x': jax.random.normal(ks[0], (N, C), dtype=jnp.float32), 'edge_index': jax.random.randint(ks[1], (2, E), 0, N, dtype=jnp.int32), 'edge_type': jax.random.randint(ks[2], (E,), 0, R, dtype=jnp.int32), 'w1': jax.random.normal(ks[3], (R, C, C), dtype=jnp.float32) * scale, 'sw1': jax.random.normal(ks[4], (C, C), dtype=jnp.float32) * scale, 'b1': jnp.zeros((C,), dtype=jnp.float32), 'w2': jax.random.normal(ks[5], (R, C, C), dtype=jnp.float32) * scale, 'sw2': jax.random.normal(ks[6], (C, C), dtype=jnp.float32) * scale, 'b2': jnp.zeros((C,), dtype=jnp.float32)}
    _L3_gnn_all = _L3_gnn_setup()
    _L3_gnn_in = {k: v for k, v in _L3_gnn_all.items() if k in ('w1', 'sw1', 'b1', 'w2', 'sw2', 'b2')}
    del _L3_gnn_all
    return {'x': x, 'src': src, 'dst': dst, 'edge_type_8': edge_type_8, 'L0_gnn_Wq': _L0_gnn_in['Wq'], 'L0_gnn_Wk': _L0_gnn_in['Wk'], 'L0_gnn_Wv': _L0_gnn_in['Wv'], 'L0_gnn_Wo': _L0_gnn_in['Wo'], 'L0_gnn_bo': _L0_gnn_in['bo'], 'L0_gnn_gamma': _L0_gnn_in['gamma'], 'L0_gnn_beta': _L0_gnn_in['beta'], 'L1_gnn_W': _L1_gnn_in['W'], 'L1_gnn_att_src': _L1_gnn_in['att_src'], 'L1_gnn_att_dst': _L1_gnn_in['att_dst'], 'L1_gnn_gat_bias': _L1_gnn_in['gat_bias'], 'L1_gnn_skip_W': _L1_gnn_in['skip_W'], 'L1_gnn_skip_b': _L1_gnn_in['skip_b'], 'L1_gnn_ln_g': _L1_gnn_in['ln_g'], 'L1_gnn_ln_b': _L1_gnn_in['ln_b'], 'L2_gnn_W1': _L2_gnn_in['W1'], 'L2_gnn_b1': _L2_gnn_in['b1'], 'L2_gnn_W2': _L2_gnn_in['W2'], 'L2_gnn_b2': _L2_gnn_in['b2'], 'L2_gnn_eta': _L2_gnn_in['eta'], 'L2_gnn_ln_gamma': _L2_gnn_in['ln_gamma'], 'L2_gnn_ln_beta': _L2_gnn_in['ln_beta'], 'L3_gnn_w1': _L3_gnn_in['w1'], 'L3_gnn_sw1': _L3_gnn_in['sw1'], 'L3_gnn_b1': _L3_gnn_in['b1'], 'L3_gnn_w2': _L3_gnn_in['w2'], 'L3_gnn_sw2': _L3_gnn_in['sw2'], 'L3_gnn_b2': _L3_gnn_in['b2']}

def reference(x, src, dst, edge_type_8, L0_gnn_Wq, L0_gnn_Wk, L0_gnn_Wv, L0_gnn_Wo, L0_gnn_bo, L0_gnn_gamma, L0_gnn_beta, L1_gnn_W, L1_gnn_att_src, L1_gnn_att_dst, L1_gnn_gat_bias, L1_gnn_skip_W, L1_gnn_skip_b, L1_gnn_ln_g, L1_gnn_ln_b, L2_gnn_W1, L2_gnn_b1, L2_gnn_W2, L2_gnn_b2, L2_gnn_eta, L2_gnn_ln_gamma, L2_gnn_ln_beta, L3_gnn_w1, L3_gnn_sw1, L3_gnn_b1, L3_gnn_w2, L3_gnn_sw2, L3_gnn_b2):
    import jax
    import jax.numpy as jnp

    def _L0_gnn_ref(x, edge_index, Wq, Wk, Wv, Wo, bo, gamma, beta):
        import jax, jax.numpy as jnp
        import numpy as np
        N, E, D = (6250, 75000, 128)
        LN_EPS = 1e-05
        src, dst = (edge_index[0], edge_index[1])
        q = x[dst] @ Wq.T
        k = x[src] @ Wk.T
        v = x[src] @ Wv.T
        logits = jnp.sum(q * k, axis=-1, keepdims=True) / np.sqrt(D)
        msg = jax.nn.sigmoid(logits) * v
        agg = jax.ops.segment_sum(msg, dst, num_segments=N)
        out = agg @ Wo.T + bo
        h = x + out
        mu = jnp.mean(h, axis=-1, keepdims=True)
        var = jnp.mean(jnp.square(h - mu), axis=-1, keepdims=True)
        return (h - mu) * jax.lax.rsqrt(var + LN_EPS) * gamma + beta

    def _L1_gnn_ref(x, edge_index, W, att_src, att_dst, gat_bias, skip_W, skip_b, ln_g, ln_b):
        import jax, jax.numpy as jnp
        import numpy as np
        N = 12500
        E = 200000
        D_IN = 128
        D_OUT = 128
        HEADS = 4
        C = D_OUT // HEADS
        NEG_SLOPE = 0.2
        EPS_SOFTMAX = 1e-16
        EPS_LN = 1e-05

        def _gat_edge_conv(x, src, dst, W, att_src, att_dst, gat_bias, skip_W, skip_b, ln_g, ln_b):
            n = x.shape[0]
            h = (x @ W).reshape(n, HEADS, C)
            a_s = jnp.einsum('nhc,hc->nh', h, att_src)
            a_d = jnp.einsum('nhc,hc->nh', h, att_dst)
            e = jax.nn.leaky_relu(a_s[src] + a_d[dst], NEG_SLOPE)
            m = jax.ops.segment_max(e, dst, num_segments=n)
            p = jnp.exp(e - m[dst])
            z = jax.ops.segment_sum(p, dst, num_segments=n)
            alpha = p / (z[dst] + EPS_SOFTMAX)
            msg = h[src] * alpha[:, :, None]
            out = jax.ops.segment_sum(msg, dst, num_segments=n)
            out = out.reshape(n, HEADS * C) + gat_bias
            out = out + x @ skip_W + skip_b
            mu = out.mean(-1, keepdims=True)
            var = ((out - mu) ** 2).mean(-1, keepdims=True)
            return (out - mu) * jax.lax.rsqrt(var + EPS_LN) * ln_g + ln_b
        n = x.shape[0]
        loops = jnp.arange(n, dtype=edge_index.dtype)
        src = jnp.concatenate([edge_index[0], loops])
        dst = jnp.concatenate([edge_index[1], loops])
        return _gat_edge_conv(x, src, dst, W, att_src, att_dst, gat_bias, skip_W, skip_b, ln_g, ln_b)

    def _L2_gnn_ref(node_features, edge_index, W1, b1, W2, b2, eta, ln_gamma, ln_beta):
        import jax, jax.numpy as jnp
        import numpy as np
        N_NODES = 6250
        N_EDGES = 100000
        D = 128

        def _layer_norm(x, gamma, beta, eps=1e-05):
            mu = jnp.mean(x, axis=-1, keepdims=True)
            var = jnp.var(x, axis=-1, keepdims=True)
            return (x - mu) * jax.lax.rsqrt(var + eps) * gamma + beta
        initial = node_features
        src, dst = (edge_index[0], edge_index[1])
        hu = node_features[src]
        sum_hu = jax.ops.segment_sum(hu, dst, num_segments=node_features.shape[0])
        z = (1.0 + eta) * node_features + sum_hu
        h = jax.nn.relu(z @ W1.T + b1)
        h = jax.nn.relu(h @ W2.T + b2)
        h = jax.nn.relu(h)
        h = _layer_norm(h, ln_gamma, ln_beta)
        return h + initial

    def _L3_gnn_ref(x, edge_index, edge_type, w1, sw1, b1, w2, sw2, b2):
        import jax, jax.numpy as jnp
        import numpy as np
        N = 6250
        E = 200000
        C = 128
        R = 8

        def _rgcn_layer(h, src, dst, et, W, SW, b, activate, residual):
            xw = jnp.einsum('nc,rco->rno', h, W)
            msg = xw[et, src]
            agg = jax.ops.segment_sum(msg, dst, num_segments=N)
            out = h @ SW + agg
            if residual:
                out = out + h
            if activate:
                out = jax.nn.relu(out)
            return out + b
        src, dst = (edge_index[0], edge_index[1])
        h = _rgcn_layer(x, src, dst, edge_type, w1, sw1, b1, activate=True, residual=True)
        h = _rgcn_layer(h, src, dst, edge_type, w2, sw2, b2, activate=False, residual=False)
        return h
    edge_index = jnp.stack([src, dst])
    x = _layernorm(x + _L0_gnn_ref(x, edge_index, L0_gnn_Wq, L0_gnn_Wk, L0_gnn_Wv, L0_gnn_Wo, L0_gnn_bo, L0_gnn_gamma, L0_gnn_beta), axis=-1)
    x = _layernorm(x + _L1_gnn_ref(x, edge_index, L1_gnn_W, L1_gnn_att_src, L1_gnn_att_dst, L1_gnn_gat_bias, L1_gnn_skip_W, L1_gnn_skip_b, L1_gnn_ln_g, L1_gnn_ln_b), axis=-1)
    x = _layernorm(x + _L2_gnn_ref(x, edge_index, L2_gnn_W1, L2_gnn_b1, L2_gnn_W2, L2_gnn_b2, L2_gnn_eta, L2_gnn_ln_gamma, L2_gnn_ln_beta), axis=-1)
    x = _layernorm(x + _L3_gnn_ref(x, edge_index, edge_type_8, L3_gnn_w1, L3_gnn_sw1, L3_gnn_b1, L3_gnn_w2, L3_gnn_sw2, L3_gnn_b2), axis=-1)
    return x

_drawn_inputs = setup_inputs


def setup_inputs(seed=0):
    import zlib

    import numpy as np

    out = dict(_drawn_inputs(seed))
    spreads = {'L0_gnn_bo': (0.0, 0.1),
     'L0_gnn_gamma': (1.0, 0.2),
     'L0_gnn_beta': (0.0, 0.1),
     'L1_gnn_ln_g': (1.0, 0.2),
     'L1_gnn_ln_b': (0.0, 0.1),
     'L2_gnn_b1': (0.0, 0.754),
     'L2_gnn_b2': (0.0, 0.461),
     'L2_gnn_ln_gamma': (1.0, 0.2),
     'L2_gnn_ln_beta': (0.0, 0.1),
     'L3_gnn_b1': (0.0, 0.1),
     'L3_gnn_b2': (0.0, 0.8)}
    factors = {}
    for name, (base, spread) in spreads.items():
        noise = np.random.default_rng([zlib.crc32(name.encode()), seed]).standard_normal(out[name].shape)
        drawn = base * np.exp(spread * noise) if base else spread * noise
        out[name] = jnp.asarray(drawn.astype(out[name].dtype))
    for name, factor in factors.items():
        out[name] = (out[name] * factor).astype(out[name].dtype)
    return out
```

```python
import concourse.bass as bass
from concourse import mybir
from contextlib import ExitStack

P = 128
F32 = mybir.dt.float32
I32 = mybir.dt.int32
ALU = mybir.AluOpType
ACT = mybir.ActivationFunctionType
AX = mybir.AxisListType

D = 128
HEADS, HC = 4, 32
HZ = HC + 1
REL = 8
LN_EPS = 1e-05
SOFTMAX_EPS = 1e-16
SLOPE = 0.2
FAR = float(2.0 ** 100)
NO_NODE = 1 << 20

UNIT = 4
RING = 4
ROW1 = HEADS * HZ + HEADS
WIDE1 = ROW1 + HEADS + D
OWN1 = 2 * HEADS + D


class Step:

    def __init__(self, i, s, per):
        self.i, self.s, self.per = i, s, per

    def back(self, lag):
        s = self.s - lag
        return Step(self.i + s // self.per, s % self.per, self.per)

    def at(self, scale=1, offset=0):
        return self.i * (self.per * scale) + (self.s * scale + offset)

    def exists(self, total):
        return not isinstance(self.i, int) or 0 <= self.at() < total


def after(eng, sem, u, back=0, per=1, upto=None):
    value = u.at(per, (upto if upto is not None else per) - back * per)
    if isinstance(value, int) and value <= 0:
        return
    eng.wait_ge(sem, value)


def pipeline(eng, total, per, longest, step, peel=2):
    full = total // per
    for n in range(peel * per):
        step(Step(n // per, n % per, per))
    with eng.Fori(peel, full) as i:
        for s in range(per):
            step(Step(i, s, per))
    for n in range(full * per, total + longest):
        step(Step(n // per, n % per, per))


def stages(total, *parts):
    def step(u):
        for lag, stage in parts:
            v = u.back(lag)
            if v.exists(total):
                stage(v)
    return step


class Memory:

    def __init__(self, nc, ctx, K, name):
        self.nc, self.ctx, self.K, self.name = nc, ctx, K, name

    def sb(self, name, shape, dt=F32):
        return self.ctx.enter_context(self.nc.sbuf_tensor(f"{self.name}_{name}", shape, dt))

    def sem(self, name):
        one = self.nc.alloc_semaphore(f"{self.name}_{name}")
        self.K.semaphores.append(one)
        return one


def bcast(ap, axis, count):
    shape = list(ap.shape)
    ap = ap.unsqueeze(axis)
    shape.insert(axis, count)
    return ap.broadcast_to(shape)


class Graph:

    def __init__(self, nodes, edges):
        self.nodes, self.edges = nodes, edges
        self.blocks = -(-nodes // P)
        self.tail = nodes - (self.blocks - 1) * P
        self.tiles = -(-edges // P)
        self.groups = -(-self.tiles // P)
        body = UNIT * RING
        self.items = -(-(self.tiles + self.blocks - 1) // body) * body
        self.units = self.items // UNIT
        assert self.items <= self.groups * P and nodes * REL < 1 << 24


def build_graph(nc, g, K, src, dst, edge_type):
    G, NB, NI = g.groups, g.blocks, g.items
    NT = G * P
    full = (g.edges // P) % P
    rest = g.edges % P
    with ExitStack() as ctx:
        M = Memory(nc, ctx, K, "prep")
        dst_rows = M.sb("dst_rows", [P, G, P], I32)
        src_rows = M.sb("src_rows", [P, G, P], I32)
        type_rows = M.sb("type_rows", [P, G, P], I32)
        dst_f = M.sb("dst_f", [P, G, P])
        src_f = M.sb("src_f", [P, G, P])
        rel_f = M.sb("rel_f", [P, G, P])
        end_f = M.sb("end_f", [P, G, P])
        start_f = M.sb("start_f", [P, G, P])
        limit = M.sb("limit", [P, NB - 1, 1])
        before = M.sb("before", [P, NB - 1, G])
        tiles_before = M.sb("tiles_before", [P, NB - 1])
        rank = M.sb("rank", [P, 1])
        item_no = M.sb("item_no", [P, NT])
        item_mod = M.sb("item_mod", [P, NT])
        block_past = M.sb("block_past", [P, NT])
        block_of = M.sb("block_of", [P, NT])
        place = M.sb("place", [P, NT])
        pick_own = M.sb("pick_own", [P, NT])
        pick_prev = M.sb("pick_prev", [P, NT])
        change = M.sb("change", [P, NT])
        padded, loaded, consts = M.sem("padded"), M.sem("loaded"), M.sem("consts")
        chain, rank_sum, rank_ready = M.sem("chain"), M.sem("rank_sum"), M.sem("rank_ready")
        mask_ready, blocks_ready, picks_ready = M.sem("mask_ready"), M.sem("blocks_ready"), M.sem("picks_ready")
        table_ready, table_out = M.sem("table_ready"), M.sem("table_out")
        block = ctx.enter_context(nc.Block())
        half = NT // 2
        arrays = [dst_f, src_f, rel_f, end_f, start_f]

        @block.sync
        def _(sp):
            sp.wait_ge(padded, 1)
            for rows, flat in ((dst_rows, dst), (src_rows, src), (type_rows, edge_type)):
                whole = (G - 1) * P * P
                sp.dma_start(rows[:, 0:G - 1, :],
                             flat[0:whole].rearrange("(g r c) -> r g c", r=P, c=P)).then_inc(loaded, 16)
                sp.dma_start(rows[0:full, G - 1, :],
                             flat[whole:whole + full * P].rearrange("(r c) -> r c", c=P)).then_inc(loaded, 16)
                sp.dma_start(rows[full:full + 1, G - 1, 0:rest],
                             flat[whole + full * P:g.edges].rearrange("(r c) -> r c", r=1)).then_inc(loaded, 16)

        @block.gpsimd
        def _(pool):
            nc.gpsimd.iota(limit[:, :, :], [[P, NB - 1]], base=P, channel_multiplier=0,
                           allow_small_or_imprecise_dtypes=True).then_inc(consts, 1)
            nc.gpsimd.iota(item_no[:, :], [[1, NT]], base=0, channel_multiplier=0,
                           allow_small_or_imprecise_dtypes=True).then_inc(consts, 1)
            nc.gpsimd.iota(item_mod[:, :], [[0, G], [1, P]], base=0, channel_multiplier=0,
                           allow_small_or_imprecise_dtypes=True).then_inc(consts, 1)

        @block.vector
        def _(dve):
            link = [0]

            def chained(ins):
                link[0] += 1
                ins.then_inc(chain, 1)
                dve.wait_ge(chain, link[0])

            nc.vector.memset(src_rows[:, G - 1, :], 0)
            nc.vector.memset(type_rows[:, G - 1, :], 0)
            nc.vector.memset(dst_rows[:, G - 1, :], NO_NODE).then_inc(padded, 1)
            dve.wait_ge(loaded, 9 * 16)
            dve.wait_ge(consts, 3)
            dve.wait_ge(padded, 1)
            nc.vector.tensor_copy(dst_f[:, :, :], dst_rows[:, :, :])
            nc.vector.tensor_copy(src_f[:, :, :], src_rows[:, :, :])
            chained(nc.vector.tensor_copy(rel_f[:, :, :], type_rows[:, :, :]))
            chained(nc.vector.tensor_tensor(before[:, :, :], bcast(dst_f[:, :, P - 1], 1, NB - 1),
                                            limit[:, :, :].broadcast_to([P, NB - 1, G]), ALU.is_lt))
            nc.vector.tensor_reduce(tiles_before[:, :], before[:, :, :], AX.X, ALU.add).then_inc(rank_ready, 1)
            chained(nc.vector.scalar_tensor_tensor(rel_f[:, :, :], src_f[:, :, :], float(REL), rel_f[:, :, :],
                                                   ALU.mult, ALU.add))
            nc.vector.memset(end_f[:, :, :], 1.0)
            chained(nc.vector.memset(start_f[:, :, :], -FAR))
            chained(nc.vector.tensor_tensor(end_f[:, :, 0:P - 1], dst_f[:, :, 0:P - 1], dst_f[:, :, 1:P],
                                            ALU.not_equal))
            chained(nc.vector.tensor_scalar(start_f[:, :, 1:P], end_f[:, :, 0:P - 1], -FAR, None, ALU.mult))
            dve.wait_ge(rank_sum, 1)
            chained(nc.vector.tensor_tensor(rank[0:NB - 1, :], K.bank[0][0:NB - 1, 0:1], K.part[0:NB - 1, :],
                                            ALU.add))
            nc.vector.tensor_scalar(block_past[0:NB - 1, :], item_no[0:NB - 1, :], rank[0:NB - 1, :], None,
                                    ALU.is_gt).then_inc(mask_ready, 1)
            dve.wait_ge(blocks_ready, 1)
            for h in range(2):
                last = nc.vector.tensor_copy(block_of[:, h * half:(h + 1) * half], K.bank[1 + h][:, 0:half])
            chained(last)
            nc.vector.tensor_copy(K.block_no[:, :], block_of[0:1, 0:NI])
            chained(nc.vector.tensor_tensor(place[:, :], item_mod[:, :], block_of[:, :], ALU.subtract))
            nc.vector.tensor_scalar(pick_own[:, :], place[:, :], K.part[:, :], None, ALU.is_equal)
            nc.vector.tensor_scalar(pick_prev[:, :], place[:, :], float(P), K.part[:, :], ALU.add,
                                    ALU.is_equal).then_inc(picks_ready, 1)
            nc.vector.memset(change[:, 0:1], -FAR)
            chained(nc.vector.tensor_tensor(change[:, 1:NT], block_of[:, 1:NT], block_of[:, 0:NT - 1],
                                            ALU.not_equal))
            chained(nc.vector.tensor_scalar(change[:, 1:NT], change[:, 1:NT], -FAR, None, ALU.mult))
            cut = K.cut[:, :, :].rearrange("p u (h k) -> p u h k", h=HEADS)
            nc.vector.memset(cut[:, :, :, 0], -FAR)
            for h in range(HEADS):
                nc.vector.tensor_copy(cut[:, :, h, 1:UNIT + 1],
                                      change[:, 0:NI].rearrange("p (u k) -> p u k", k=UNIT))
            for a in range(5):
                dve.wait_ge(table_ready, a + 1)
                lo, hi = K.bank[3 + 2 * (a % 2)], K.bank[4 + 2 * (a % 2)]
                for bank, c0, n in ((lo, 0, half), (hi, half, NI - half)):
                    if a == 0:
                        last = nc.vector.scalar_tensor_tensor(K.node[:, c0:c0 + n], block_of[:, c0:c0 + n], float(-P),
                                                              bank[:, 0:n], ALU.mult, ALU.add)
                    else:
                        into = (K.src_row, K.rel_row, K.ends, K.starts)[a - 1]
                        last = nc.vector.tensor_copy(into[:, c0:c0 + n], bank[:, 0:n])
                last.then_inc(table_out, 1)

        @block.tensor
        def _(pe):
            pe.wait_ge(rank_ready, 1)
            nc.tensor.matmul(K.bank[0][0:NB - 1, 0:1], tiles_before[:, :], K.ones[:, 0:1], start=True,
                             stop=True).then_inc(rank_sum, 1)
            pe.wait_ge(mask_ready, 1)
            for h in range(2):
                last = nc.tensor.matmul(K.bank[1 + h][:, 0:half], K.ones[0:NB - 1, :],
                                        block_past[0:NB - 1, h * half:(h + 1) * half], start=True, stop=True)
            last.then_inc(blocks_ready, 1)
            pe.wait_ge(picks_ready, 1)
            pe.wait_ge(chain, 7)
            for a, rows in enumerate(arrays):
                if a >= 2:
                    pe.wait_ge(table_out, a - 1)
                for q in range(G):
                    for c0, n in ((q * P, min(P, max(0, half - q * P))), (max(q * P, half), min(P, (q + 1) * P - half))):
                        if n <= 0 or c0 >= (q + 1) * P:
                            continue
                        bank, at = (K.bank[3 + 2 * (a % 2)], c0) if c0 < half else (K.bank[4 + 2 * (a % 2)], c0 - half)
                        last = nc.tensor.matmul(bank[:, at:at + n], rows[:, q, :], pick_own[:, c0:c0 + n],
                                                start=True, stop=(q == 0))
                        if q:
                            last = nc.tensor.matmul(bank[:, at:at + n], rows[:, q - 1, :], pick_prev[:, c0:c0 + n],
                                                    start=False, stop=True)
                last.then_inc(table_ready, 1)


def load_and_fold(nc, g, K, W):
    with ExitStack() as ctx:
        M = Memory(nc, ctx, K, "fold")
        part_no = M.sb("part_no", [P, 1], I32)
        col_no = M.sb("col_no", [P, P], I32)
        wq, wk, wv, wo = (M.sb(n, [P, P]) for n in ("wq", "wk", "wv", "wo"))
        wo_t = M.sb("wo_t", [P, P])
        w1, w1_t, att = M.sb("w1", [P, P]), M.sb("w1_t", [P, P]), M.sb("att", [P, 2 * HEADS])
        gin1, gin2 = M.sb("gin1", [P, P]), M.sb("gin2", [P, P])
        skip_b = M.sb("skip_b", [1, D])
        eta = M.sb("eta", [P, 1])
        zeroed, iotas, loaded = M.sem("zeroed"), M.sem("iotas"), M.sem("loaded")
        chain, ident_ready = M.sem("chain"), M.sem("ident_ready")
        turned, turned_out, folded, folded_out = M.sem("turned"), M.sem("turned_out"), M.sem("folded"), M.sem("folded_out")
        loads = [0]
        block = ctx.enter_context(nc.Block())

        @block.sync
        def _(sp):
            def load(out, in_):
                loads[0] += 16
                sp.dma_start(out, in_).then_inc(loaded, 16)

            row = lambda v: v.rearrange("(a d) -> a d", a=1)
            sp.wait_ge(zeroed, 1)
            for t, n in ((wq, "L0_gnn_Wq"), (wk, "L0_gnn_Wk"), (wv, "L0_gnn_Wv"), (wo, "L0_gnn_Wo"), (w1, "L1_gnn_W"),
                         (gin1, "L2_gnn_W1"), (gin2, "L2_gnn_W2")):
                load(t[:, :], W[n])
            for h in range(HEADS):
                for j, n in enumerate(("L1_gnn_att_src", "L1_gnn_att_dst")):
                    load(att[h * HC:(h + 1) * HC, j * HEADS + h:j * HEADS + h + 1],
                         W[n][h:h + 1, :].rearrange("a c -> c a"))
            with sp.Fori(0, g.blocks - 1) as b:
                sp.dma_start(K.x[:, bass.ds(b, 1), :].rearrange("p a d -> p (a d)"),
                             W["x"][bass.ds(b * P, P), :]).then_inc(loaded, 16)
            loads[0] += 16 * (g.blocks - 1)
            load(K.x[0:g.tail, g.blocks - 1, :], W["x"][(g.blocks - 1) * P:g.nodes, :])
            load(K.w1[:, ROW1 + HEADS:], W["L1_gnn_skip_W"])
            load(K.b0[:, :], row(W["L0_gnn_bo"]))
            load(K.b1[:, ROW1 + HEADS:], row(W["L1_gnn_gat_bias"]))
            load(skip_b[:, :], row(W["L1_gnn_skip_b"]))
            load(K.gin_b1[:, :], W["L2_gnn_b1"].rearrange("(d a) -> d a", a=1))
            load(K.gin_b2[:, :], row(W["L2_gnn_b2"]))
            load(eta[:, :], W["L2_gnn_eta"].broadcast_to([P, 1]))
            for t, n in zip(K.affine, ("L0_gnn_gamma", "L0_gnn_beta", "L1_gnn_ln_g", "L1_gnn_ln_b", "L2_gnn_ln_gamma",
                                       "L2_gnn_ln_beta")):
                load(t[:, :], row(W[n]).broadcast_to([P, D]))
            load(K.rel_b1[:, :], row(W["L3_gnn_b1"]).broadcast_to([P, D]))
            load(K.rel_b2[:, :], row(W["L3_gnn_b2"]))
            for t, n, m in ((K.rel_w[0], "L3_gnn_w1", "L3_gnn_sw1"), (K.rel_w[1], "L3_gnn_w2", "L3_gnn_sw2")):
                load(t[:, 0:REL, :], W[n].rearrange("r c o -> c r o"))
                load(t[:, REL, :], W[m])

        @block.gpsimd
        def _(pool):
            nc.gpsimd.iota(part_no[:, :], [[0, 1]], base=0, channel_multiplier=1).then_inc(iotas, 1)
            nc.gpsimd.iota(col_no[:, :], [[1, P]], base=0, channel_multiplier=0).then_inc(iotas, 1)

        @block.vector
        def _(dve):
            nc.vector.memset(K.x[:, g.blocks - 1, :], 0.0)
            nc.vector.memset(K.w1[:, :], 0.0)
            nc.vector.memset(K.b1[:, :], 0.0).then_inc(chain, 1)
            nc.vector.memset(K.ones[:, :], 1.0)
            nc.vector.memset(K.eps[:, :], LN_EPS)
            dve.wait_ge(chain, 1)
            nc.vector.memset(K.b1[:, 0:HEADS * HZ].rearrange("p (h z) -> p h z", h=HEADS)[:, :, HC], 1.0)
            nc.vector.memset(att[:, :], 0.0).then_inc(zeroed, 1)
            dve.wait_ge(iotas, 2)
            nc.vector.tensor_copy(K.col[:, :], col_no[:, :])
            nc.vector.tensor_copy(K.part[:, :], part_no[:, :]).then_inc(chain, 1)
            dve.wait_ge(chain, 2)
            nc.vector.tensor_scalar(K.ident[:, :], K.col[:, :], K.part[:, :], None,
                                    ALU.is_equal).then_inc(ident_ready, 1)
            dve.wait_ge(loaded, loads[0])
            nc.vector.tensor_copy(K.w1[:, 0:HEADS * HZ].rearrange("p (h z) -> p h z", h=HEADS)[:, :, 0:HC],
                                  w1[:, :].rearrange("p (h c) -> p h c", h=HEADS))
            nc.vector.tensor_tensor(K.b1[:, ROW1 + HEADS:], K.b1[:, ROW1 + HEADS:], skip_b[:, :], ALU.add)
            nc.vector.tensor_scalar(K.eta1[:, :], eta[:, :], 1.0, None, ALU.add)
            dve.wait_ge(turned, 1)
            for j, t in enumerate((wo_t, w1_t, K.gin_w1, K.gin_w2)):
                last = nc.vector.tensor_copy(t[:, :], K.bank[0][:, j * P:(j + 1) * P])
            last.then_inc(turned_out, 1)
            dve.wait_ge(folded, 1)
            nc.vector.tensor_scalar(K.qk[:, :], K.bank[1][:, 0:P], float(D) ** -0.5, None, ALU.mult)
            nc.vector.tensor_copy(K.vo[:, :], K.bank[1][:, P:2 * P])
            nc.vector.tensor_copy(K.w1[:, ROW1 - HEADS:ROW1 + HEADS],
                                  K.bank[1][:, 2 * P:2 * P + 2 * HEADS]).then_inc(folded_out, 1)

        @block.tensor
        def _(pe):
            pe.wait_ge(loaded, loads[0])
            pe.wait_ge(ident_ready, 1)
            for j, t in enumerate((wo, w1, gin1, gin2)):
                last = nc.tensor.transpose(K.bank[0][:, j * P:(j + 1) * P], t[:, :], K.ident[:, :])
            last.then_inc(turned, 1)
            nc.tensor.matmul(K.bank[1][:, 0:P], wq[:, :], wk[:, :], start=True, stop=True)
            pe.wait_ge(turned_out, 1)
            nc.tensor.matmul(K.bank[1][:, P:2 * P], wv[:, :], wo_t[:, :], start=True, stop=True)
            nc.tensor.matmul(K.bank[1][:, 2 * P:2 * P + 2 * HEADS], w1_t[:, :], att[:, :], start=True,
                             stop=True).then_inc(folded, 1)


def query_rows(nc, g, K):
    with ExitStack() as ctx:
        M = Memory(nc, ctx, K, "query")
        x_t = M.sb("x_t", [P, RING, P])
        x_u = M.sb("x_u", [P, RING, P])
        brought, taken = M.sem("brought"), M.sem("taken")
        turned, turned_out, made, made_out = M.sem("turned"), M.sem("turned_out"), M.sem("made"), M.sem("made_out")
        block = ctx.enter_context(nc.Block())

        @block.gpsimd
        def _(pool):
            def bring(u):
                after(pool, turned, u, RING)
                pool.sem_inc(taken, 1)
                nc.gpsimd.tensor_copy(x_u[:, u.s, :], blk(K.x, u, D)).then_inc(brought, 1)

            pipeline(pool, g.blocks, RING, 0, stages(g.blocks, (0, bring)))

        @block.tensor
        def _(pe):
            def turn(u):
                after(pe, turned_out, u, 2)
                after(pe, brought, u)
                nc.tensor.transpose(K.bank[u.s % 2][:, 0:P], x_u[:, u.s, :], K.ident[:, :]).then_inc(turned, 1)

            def make(u):
                after(pe, turned_out, u)
                after(pe, made_out, u, 2)
                nc.tensor.matmul(K.bank[2 + u.s % 2][:, 0:P], x_t[:, u.s, :], K.qk[:, :], start=True,
                                 stop=True).then_inc(made, 1)

            pipeline(pe, g.blocks, RING, 1, stages(g.blocks, (0, turn), (1, make)))

        @block.scalar
        def _(act):
            def copy(u):
                after(act, turned, u)
                after(act, made, u, RING)
                nc.scalar.copy(x_t[:, u.s, :], K.bank[u.s % 2][:, 0:P]).then_inc(turned_out, 1)

            pipeline(act, g.blocks, RING, 0, stages(g.blocks, (0, copy)))

        @block.vector
        def _(dve):
            def copy(u):
                after(dve, made, u)
                nc.vector.tensor_copy(blk(K.own, u, D), K.bank[2 + u.s % 2][:, 0:P]).then_inc(made_out, 1)

            pipeline(dve, g.blocks, RING, 0, stages(g.blocks, (0, copy)))


def blk(t, u, n, start=0):
    return t[:, bass.ds(u.at(), 1), start:start + n].rearrange("p a d -> p (a d)")


def block_numbers(nc, engine, K, g, u):
    return nc.values_load_multi_w_load_instructions(
        K.block_no[0:1, bass.ds(u.at(UNIT), UNIT)], engines=(engine,), min_val=0, max_val=g.blocks - 1,
        skip_runtime_bounds_check_because="items are numbered within the blocks")[1]


def at_block(t, b, n, start=0):
    return t[:, bass.ds(b, 1), start:start + n].rearrange("p a d -> p (a d)")


def stage_rows(nc, act, K, g, index, staged, gathered):
    def stage(u):
        if u.at() is not None:
            after_gather(act, gathered, u, RING)
        nc.scalar.copy(K.rows[:, u.s, :], index[:, bass.ds(u.at(UNIT), UNIT)]).then_inc(staged, 1)
    return stage


def after_gather(eng, gathered, u, back=0):
    v = u.back(back)
    value = v.i * (16 * UNIT) + 16 * UNIT
    if isinstance(value, int) and value <= 0:
        return
    eng.wait_ge(gathered[u.s], value)


def gather_rows(nc, pool, K, g, table, width, staged, gathered, used, opened):
    def gather(u):
        after(pool, staged, u)
        after(pool, used, u, RING)
        pool.sem_inc(opened, 1)
        for k in range(UNIT):
            pool.indirect_dma_start(out=K.ring[:, u.s * UNIT + k, 0:width], out_offset=None, in_=table,
                                    in_offset=bass.IndirectOffsetOnAxis(ap=K.rows[:, u.s, k:k + 1], axis=0),
                                    ).then_inc(gathered[u.s], 16)
    return gather


def member(nc, K, u):
    shape = [P, UNIT, P]
    return nc.vector.tensor_tensor(K.member[:, u.s, :, :], bcast(K.col[:, :], 1, UNIT),
                                   K.node[:, bass.ds(u.at(UNIT), UNIT)].unsqueeze(2).broadcast_to(shape), ALU.is_equal)


def attention_items(nc, g, K, x_table):
    with ExitStack() as ctx:
        M = Memory(nc, ctx, K, "attn")
        gathered = [M.sem(f"gathered{s}") for s in range(RING)]
        staged, member_ready, turned, turned_out = (M.sem(n) for n in ("staged", "member", "turned", "turned_out"))
        query_ready, product_ready, logit_ready, gate_ready = (M.sem(n) for n in ("query", "product", "logit", "gate"))
        gated_ready, summed, added, cleared = (M.sem(n) for n in ("gated", "summed", "added", "cleared"))
        member_t = M.sb("member_t", [P, 2, UNIT, P])
        product = M.sb("product", [P, UNIT, P])
        logit, gate = M.sb("logit", [P, 2, UNIT]), M.sb("gate", [P, 2, UNIT])
        gated = M.sb("gated", [P, 2, UNIT, P])
        view = lambda bank: bank[:, :].rearrange("p (k d) -> p k d", k=UNIT)
        bank_t, bank_q, bank_s = K.bank[0:2], K.bank[2:4], K.bank[4:6]
        N = g.units
        opened = M.sem("opened")
        block = ctx.enter_context(nc.Block())

        @block.gpsimd
        def _(pool):
            pipeline(pool, N, RING, 0, stages(N, (0, gather_rows(nc, pool, K, g, x_table, D, staged, gathered, summed,
                                                                 opened))))

        @block.scalar
        def _(act):
            def copy_turned(u):
                after(act, turned, u)
                after(act, query_ready, u, 2)
                nc.scalar.copy(member_t[:, u.s % 2, :, :], view(bank_t[u.s % 2])).then_inc(turned_out, 1)

            def sigmoid(u):
                after(act, logit_ready, u)
                after(act, gated_ready, u, 2)
                nc.scalar.activation(gate[:, u.s % 2, :], logit[:, u.s % 2, :], ACT.Sigmoid).then_inc(gate_ready, 1)

            pipeline(act, N, RING, 3, stages(N, (0, stage_rows(nc, act, K, g, K.src_row, staged, gathered)),
                                             (2, copy_turned), (3, sigmoid)))

        @block.vector
        def _(dve):
            nc.vector.memset(K.acc[:, :, :], 0.0).then_inc(cleared, 1)

            def members(u):
                after(dve, summed, u, RING)
                member(nc, K, u).then_inc(member_ready, 1)

            def logits(u):
                after(dve, query_ready, u)
                after_gather(dve, gathered, u)
                after(dve, logit_ready, u, 1)
                nc.vector.tensor_tensor(product[:, :, :], view(bank_q[u.s % 2]),
                                        K.ring[:, u.s * UNIT:(u.s + 1) * UNIT, 0:D], ALU.mult).then_inc(product_ready, 1)
                after(dve, product_ready, u)
                after(dve, gate_ready, u, 2)
                nc.vector.tensor_reduce(logit[:, u.s % 2, :], product[:, :, :], AX.X, ALU.add).then_inc(logit_ready, 1)

            def gates(u):
                after(dve, gate_ready, u)
                after(dve, summed, u, 2)
                nc.vector.tensor_tensor(gated[:, u.s % 2, :, :], K.member[:, u.s, :, :],
                                        gate[:, u.s % 2, :].unsqueeze(2).broadcast_to([P, UNIT, P]),
                                        ALU.mult).then_inc(gated_ready, 1)

            dve.wait_ge(cleared, 1)
            pipeline(dve, N, RING, 3, stages(N, (0, members), (1, logits), (2, gates),
                                             (3, add_sums(nc, dve, K, g, summed, added, bank_s))))

        @block.tensor
        def _(pe):
            def turn(u):
                after(pe, member_ready, u)
                after(pe, turned_out, u, 2)
                for k in range(UNIT):
                    last = nc.tensor.transpose(bank_t[u.s % 2][:, k * P:(k + 1) * P], K.member[:, u.s, k, :],
                                               K.ident[:, :])
                last.then_inc(turned, 1)

            def queries(u):
                b = block_numbers(nc, mybir.EngineType.PE, K, g, u)
                after(pe, turned_out, u)
                after(pe, product_ready, u, 2)
                for k in range(UNIT):
                    last = nc.tensor.matmul(bank_q[u.s % 2][:, k * P:(k + 1) * P], member_t[:, u.s % 2, k, :],
                                            at_block(K.own, b[k], D), start=True, stop=True)
                last.then_inc(query_ready, 1)

            def sums(u):
                after(pe, gated_ready, u)
                after(pe, added, u, 2, per=UNIT)
                for k in range(UNIT):
                    last = nc.tensor.matmul(bank_s[u.s % 2][:, k * P:(k + 1) * P], gated[:, u.s % 2, k, :],
                                            K.ring[:, u.s * UNIT + k, 0:D], start=True, stop=True)
                last.then_inc(summed, 1)

            pipeline(pe, N, RING, 2, stages(N, (0, turn), (1, queries), (2, sums)))


def add_sums(nc, dve, K, g, summed, added, banks):
    def add(u):
        b = block_numbers(nc, mybir.EngineType.DVE, K, g, u)
        after(dve, summed, u)
        for k in range(UNIT):
            if k:
                after(dve, added, u, per=UNIT, upto=k)
            else:
                after(dve, added, u, 1, per=UNIT)
            into = at_block(K.acc, b[k], D)
            nc.vector.tensor_tensor(into, into, banks[u.s % 2][:, k * P:(k + 1) * P], ALU.add).then_inc(added, 1)
    return add


def sum_items(nc, g, K, name, table, index):
    with ExitStack() as ctx:
        M = Memory(nc, ctx, K, name)
        gathered = [M.sem(f"gathered{s}") for s in range(RING)]
        staged, member_ready, summed, added, cleared = (M.sem(n) for n in ("staged", "member", "summed", "added", "cleared"))
        banks = K.bank[0:2]
        N = g.units
        opened = M.sem("opened")
        block = ctx.enter_context(nc.Block())

        @block.gpsimd
        def _(pool):
            pipeline(pool, N, RING, 0, stages(N, (0, gather_rows(nc, pool, K, g, table, D, staged, gathered, summed,
                                                                 opened))))

        @block.scalar
        def _(act):
            pipeline(act, N, RING, 0, stages(N, (0, stage_rows(nc, act, K, g, index, staged, gathered))))

        @block.vector
        def _(dve):
            nc.vector.memset(K.acc[:, :, :], 0.0).then_inc(cleared, 1)

            def members(u):
                after(dve, summed, u, RING)
                member(nc, K, u).then_inc(member_ready, 1)

            dve.wait_ge(cleared, 1)
            pipeline(dve, N, RING, 1, stages(N, (0, members), (1, add_sums(nc, dve, K, g, summed, added, banks))))

        @block.tensor
        def _(pe):
            def sums(u):
                after(pe, member_ready, u)
                after_gather(pe, gathered, u)
                after(pe, added, u, 2, per=UNIT)
                for k in range(UNIT):
                    last = nc.tensor.matmul(banks[u.s % 2][:, k * P:(k + 1) * P], K.member[:, u.s, k, :],
                                            K.ring[:, u.s * UNIT + k, 0:D], start=True, stop=True)
                last.then_inc(summed, 1)

            pipeline(pe, N, RING, 0, stages(N, (0, sums)))


def softmax_items(nc, g, K, table):
    with ExitStack() as ctx:
        M = Memory(nc, ctx, K, "soft")
        gathered = [M.sem(f"gathered{s}") for s in range(RING)]
        staged, member_ready, turned, turned_out = (M.sem(n) for n in ("staged", "member", "turned", "turned_out"))
        scores_turned, starts_out, run_ready = M.sem("scores_turned"), M.sem("starts_out"), M.sem("run_max")
        run_back, ends_ready, tops_ready = M.sem("run_back"), M.sem("ends"), M.sem("tops")
        chain, max_ready, picked, logit_chain = M.sem("chain"), M.sem("max"), M.sem("picked"), M.sem("logit_chain")
        over_ready, exp_ready, message_ready, summed = M.sem("over"), M.sem("exp"), M.sem("message"), M.sem("summed")
        added, cleared, staged2 = M.sem("added"), M.sem("cleared"), M.sem("starts_staged")
        C = UNIT * HEADS
        member_t = M.sb("member_t", [P, 2, UNIT, P])
        start_u = M.sb("start_u", [P, RING, C])
        score_u = M.sb("score_u", [P, 2, C])
        scores_ready, taken = M.sem("scores"), M.sem("taken")
        starts_t = M.sb("starts_t", [C, 2, P])
        run_max = M.sb("run_max", [C, 2, P])
        run_end = M.sb("run_end", [P, 2, UNIT, HEADS + 1])
        absent = M.sb("absent", [P, UNIT])
        node_own = M.sb("node_own", [P, 2, HEADS, UNIT])
        tops = M.sb("tops", [P, HEADS, UNIT + 1])
        peak = M.sb("peak", [P, 2, HEADS, UNIT + 1])
        old = M.sb("old", [P, HEADS, UNIT])
        both = M.sb("both", [P, 2, 2, C])
        leaky = M.sb("leaky", [P, 2, 2, C])
        edge_ad = M.sb("edge_ad", [P, UNIT, HEADS])
        over = M.sb("over", [P, 2, 2, C])
        power = M.sb("power", [P, 2, 2, C])
        message = M.sb("message", [P, 2, UNIT, HEADS * HZ])
        scaled = M.sb("scaled", [P, HEADS * HZ])
        view = lambda bank: bank[:, :].rearrange("p (k d) -> p k d", k=UNIT)
        bank_t, bank_s, bank_m = K.bank[0:2], (K.bank[2:4], K.bank[4:6]), K.bank[6:8]
        N = g.units
        W = HEADS * HZ
        RUN, TOP, AD, EDGE = 256, 272, 272 + UNIT * (HEADS + 1), 272 + UNIT * (HEADS + 1) + 2 * C
        top_of = lambda u: bank_m[u.s % 2][:, TOP:AD].rearrange("p (k h) -> p k h", h=HEADS + 1)
        ad_of = lambda u: bank_m[u.s % 2][:, AD:EDGE].rearrange("p (k j h) -> p k j h", k=UNIT, j=2)
        edge_of = lambda u: bank_m[u.s % 2][:, EDGE:EDGE + 2 * C].rearrange("p (k j h) -> p k j h", k=UNIT, j=2)
        sum_of = lambda u, k: bank_s[u.s % 2][k // 3][:, (k % 3) * W:(k % 3 + 1) * W]
        by_kh = lambda a: a.rearrange("p (k h) -> p k h", h=HEADS)
        by_hk = lambda a: a.rearrange("p (h k) -> p h k", h=HEADS)
        opened = M.sem("opened")
        block = ctx.enter_context(nc.Block())

        @block.gpsimd
        def _(pool):
            pipeline(pool, N, RING, 0, stages(N, (0, gather_rows(nc, pool, K, g, table, ROW1, staged, gathered,
                                                                 message_ready, opened))))

        @block.scalar
        def _(act):
            rows = stage_rows(nc, act, K, g, K.src_row, staged, gathered)

            def inputs(u):
                rows(u)
                after(act, scores_turned, u, RING)
                nc.scalar.copy(by_kh(start_u[:, u.s, :]), K.starts[:, bass.ds(u.at(UNIT), UNIT)].unsqueeze(2)
                               .broadcast_to([P, UNIT, HEADS])).then_inc(staged2, 1)

            def copy_scores(u):
                after_gather(act, gathered, u)
                after(act, scores_turned, u, 2)
                nc.scalar.copy(by_kh(score_u[:, u.s % 2, :]),
                               K.ring[:, u.s * UNIT:(u.s + 1) * UNIT, W:W + HEADS]).then_inc(scores_ready, 1)

            def copy_starts(u):
                after(act, scores_turned, u)
                after(act, run_ready, u, 2)
                nc.scalar.copy(starts_t[:, u.s % 2, :], bank_m[u.s % 2][0:C, P:2 * P]).then_inc(starts_out, 1)

            def exponent(u):
                after(act, over_ready, u)
                after(act, added, u, 2, per=2 * UNIT)
                nc.scalar.activation(power[:, u.s % 2, :, :], over[:, u.s % 2, :, :], ACT.Exp).then_inc(exp_ready, 1)

            def copy_turned(u):
                after(act, turned, u)
                after(act, picked, u, 2)
                nc.scalar.copy(member_t[:, u.s % 2, :, :], view(bank_t[u.s % 2])).then_inc(turned_out, 1)

            pipeline(act, N, RING, 4, stages(N, (0, inputs), (4, copy_starts), (4, exponent), (3, copy_turned), (3, copy_scores)), peel=3)



        @block.tensor
        def _(pe):
            def turn_scores(u):
                after(pe, scores_ready, u)
                after(pe, staged2, u)
                after(pe, over_ready, u, 2)
                bank = bank_m[u.s % 2]
                nc.tensor.transpose(bank[0:C, 0:P], score_u[:, u.s % 2, :], K.ident[:, :])
                nc.tensor.transpose(bank[0:C, P:2 * P], start_u[:, u.s, :],
                                    K.ident[:, :]).then_inc(scores_turned, 1)

            def turn_runs(u):
                after(pe, run_ready, u)
                pe.sem_inc(taken, 1)
                nc.tensor.transpose(bank_m[u.s % 2][:, RUN:TOP], run_max[:, u.s % 2, :],
                                    K.ident[0:C, 0:C]).then_inc(run_back, 1)

            def item_tops(u):
                b = block_numbers(nc, mybir.EngineType.PE, K, g, u)
                after(pe, ends_ready, u, per=2)
                after(pe, member_ready, u)
                for k in range(UNIT):
                    nc.tensor.matmul(top_of(u)[:, k, :], K.member[:, u.s, k, :], run_end[:, u.s % 2, k, :],
                                     start=True, stop=True)
                for k in range(UNIT):
                    last = nc.tensor.matmul(ad_of(u)[:, k, :, :], K.ident[:, :], at_block(K.own, b[k], 2 * HEADS),
                                            start=True, stop=True)
                last.then_inc(tops_ready, 1)
                return b

            def pick(u, b):
                after(pe, max_ready, u)
                after(pe, turned_out, u)
                for k in range(UNIT):
                    nc.tensor.matmul(edge_of(u)[:, k, 0, :], member_t[:, u.s % 2, k, :], at_block(K.own, b[k], HEADS, HEADS),
                                     start=True, stop=True)
                    last = nc.tensor.matmul(edge_of(u)[:, k, 1, :], member_t[:, u.s % 2, k, :],
                                            peak[:, u.s % 2, :, k + 1], start=True, stop=True)
                last.then_inc(picked, 1)

            def maxima(u):
                turn_scores(u)
                turn_runs(u)
                pick(u, item_tops(u))

            def turn(u):
                after(pe, member_ready, u)
                after(pe, turned_out, u, 2)
                for k in range(UNIT):
                    last = nc.tensor.transpose(bank_t[u.s % 2][:, k * P:(k + 1) * P], K.member[:, u.s, k, :],
                                               K.ident[:, :])
                last.then_inc(turned, 1)

            def sums(u):
                after(pe, message_ready, u)
                after(pe, added, u, 2, per=2 * UNIT)
                for k in range(UNIT):
                    last = nc.tensor.matmul(sum_of(u, k), K.member[:, u.s, k, :], message[:, u.s % 2, k, :],
                                            start=True, stop=True)
                last.then_inc(summed, 1)

            pipeline(pe, N, RING, 1, stages(N, (1, maxima), (0, turn), (1, sums)))

        @block.vector
        def _(dve):
            def run_maxima(u):
                after(dve, scores_turned, u)
                after(dve, starts_out, u)
                after(dve, run_back, u, 2)
                nc.vector.tensor_tensor_scan(run_max[:, u.s % 2, :], starts_t[:, u.s % 2, :],
                                             bank_m[u.s % 2][0:C, 0:P], -FAR, ALU.add, ALU.max).then_inc(run_ready, 1)

            def run_ends(u):
                ends = K.ends[:, bass.ds(u.at(UNIT), UNIT)]
                after(dve, tops_ready, u, 2)
                nc.vector.tensor_copy(run_end[:, u.s % 2, :, HEADS], ends).then_inc(ends_ready, 1)
                after(dve, run_back, u)
                nc.vector.tensor_tensor(run_end[:, u.s % 2, :, 0:HEADS], by_kh(bank_m[u.s % 2][:, RUN:TOP]),
                                        ends.unsqueeze(2).broadcast_to([P, UNIT, HEADS]),
                                        ALU.mult).then_inc(ends_ready, 1)

            def new_maxima(u):
                after(dve, tops_ready, u)
                nc.vector.tensor_scalar(absent[:, :], top_of(u)[:, :, HEADS], FAR, -FAR, ALU.mult,
                                        ALU.add).then_inc(chain, 1)
                nc.vector.tensor_copy(tops[:, :, 0], peak[:, 1 - u.s % 2, :, UNIT]).then_inc(chain, 1)
                nc.vector.tensor_copy(node_own[:, :, :, :], ad_of(u).rearrange("p k j h -> p j h k")).then_inc(chain, 1)
                after(dve, chain, u, per=8, upto=1)
                nc.vector.tensor_tensor(tops[:, :, 1:UNIT + 1], top_of(u)[:, :, 0:HEADS].rearrange("p k h -> p h k"),
                                        bcast(absent[:, :], 1, HEADS), ALU.add).then_inc(chain, 1)
                after(dve, chain, u, per=8, upto=4)
                nc.vector.tensor_tensor(tops[:, :, 1:UNIT + 1], tops[:, :, 1:UNIT + 1], node_own[:, 0, :, :],
                                        ALU.max).then_inc(chain, 1)
                after(dve, chain, u, per=8, upto=5)
                after(dve, picked, u, 2)
                nc.vector.tensor_tensor_scan(peak[:, u.s % 2, :, :].rearrange("p h k -> p (h k)"),
                                             K.cut[:, bass.ds(u.at(), 1), :].rearrange("p a c -> p (a c)"),
                                             tops[:, :, :].rearrange("p h k -> p (h k)"), -FAR, ALU.add,
                                             ALU.max).then_inc(max_ready, 1)
                after(dve, max_ready, u)
                nc.vector.tensor_tensor(old[:, :, :], peak[:, u.s % 2, :, 0:UNIT],
                                        K.cut[:, bass.ds(u.at(), 1), :].rearrange("p a (h k) -> p (a h) k", h=HEADS)
                                        [:, :, 1:UNIT + 1], ALU.add).then_inc(chain, 1)
                after(dve, chain, u, per=8, upto=6)
                nc.vector.tensor_tensor(old[:, :, :], old[:, :, :], node_own[:, 0, :, :], ALU.max).then_inc(chain, 1)
                after(dve, chain, u, per=8, upto=7)
                ad = node_own[:, 1, :, :]
                nc.vector.tensor_tensor(by_hk(both[:, 0, 0, :]), old[:, :, :], ad, ALU.add)
                nc.vector.tensor_tensor(by_hk(both[:, 0, 1, :]), peak[:, u.s % 2, :, 1:UNIT + 1], ad,
                                        ALU.add).then_inc(chain, 1)

            def overs(u):
                after(dve, picked, u)
                edge = edge_of(u)
                nc.vector.tensor_copy(edge_ad[:, :, :], edge[:, :, 0, :]).then_inc(logit_chain, 1)
                after(dve, logit_chain, u, per=4, upto=1)
                nc.vector.tensor_tensor(by_kh(both[:, 1, 0, :]), K.ring[:, u.s * UNIT:(u.s + 1) * UNIT, W:W + HEADS],
                                        edge_ad[:, :, :], ALU.add)
                nc.vector.tensor_tensor(by_kh(both[:, 1, 1, :]), edge[:, :, 1, :], edge_ad[:, :, :],
                                        ALU.add).then_inc(logit_chain, 1)
                after(dve, chain, u, per=8)
                after(dve, logit_chain, u, per=4, upto=2)
                nc.vector.tensor_tensor(both[:, 1, 0, :], both[:, 1, 0, :], both[:, 1, 1, :],
                                        ALU.min).then_inc(logit_chain, 1)
                after(dve, logit_chain, u, per=4, upto=3)
                nc.vector.scalar_tensor_tensor(leaky[:, :, :, :], both[:, :, :, :], SLOPE, both[:, :, :, :], ALU.mult,
                                               ALU.max).then_inc(logit_chain, 1)
                after(dve, logit_chain, u, per=4, upto=4)
                after(dve, exp_ready, u, 2)
                nc.vector.tensor_tensor(over[:, u.s % 2, :, :], leaky[:, :, 0, :], leaky[:, :, 1, :],
                                        ALU.subtract).then_inc(over_ready, 1)

            def messages(u):
                after(dve, exp_ready, u)
                after(dve, summed, u, 2)
                nc.vector.tensor_tensor(
                    message[:, u.s % 2, :, :].rearrange("p k (h z) -> p k h z", h=HEADS),
                    K.ring[:, u.s * UNIT:(u.s + 1) * UNIT, 0:W].rearrange("p k (h z) -> p k h z", h=HEADS),
                    by_kh(power[:, u.s % 2, 1, :]).unsqueeze(3).broadcast_to([P, UNIT, HEADS, HZ]),
                    ALU.mult).then_inc(message_ready, 1)

            def add(u, items):
                if items[0] == 0:
                    add.b = block_numbers(nc, mybir.EngineType.DVE, K, g, u)
                    after(dve, summed, u)
                for k in items:
                    into = at_block(K.acc, add.b[k], W)
                    heads = lambda a: a.rearrange("p (h z) -> p h z", h=HEADS)
                    after(dve, added, u, back=0 if k else 1, per=2 * UNIT, upto=2 * k if k else None)
                    nc.vector.tensor_tensor(heads(scaled[:, :]), heads(into), by_hk(power[:, u.s % 2, 0, :])[:, :, k]
                                            .unsqueeze(2).broadcast_to([P, HEADS, HZ]), ALU.mult).then_inc(added, 1)
                    after(dve, added, u, per=2 * UNIT, upto=2 * k + 1)
                    nc.vector.tensor_tensor(into, scaled[:, :], sum_of(u, k), ALU.add).then_inc(added, 1)

            def members(u):
                after(dve, summed, u, RING)
                member(nc, K, u).then_inc(member_ready, 1)

            def spread(u):
                v = u.back(1)
                late = v.exists(N)
                if u.exists(N):
                    run_maxima(u)
                if late:
                    add(v, (0,))
                if u.exists(N):
                    run_ends(u)
                if late:
                    add(v, (1,))
                if u.exists(N):
                    new_maxima(u)
                    nxt = u.back(-1)
                    if nxt.exists(N):
                        members(nxt)
                    overs(u)
                if late:
                    add(v, (2, 3))
                if u.exists(N):
                    messages(u)

            nc.vector.memset(peak[:, 1, :, :], -FAR).then_inc(cleared, 1)
            dve.wait_ge(cleared, 1)
            members(Step(0, 0, RING))

            def step(u):
                v = u.back(1)
                if v.exists(N + 1):
                    spread(v)
            pipeline(dve, N, RING, 2, step)


ATTENTION, SOFTMAX, GIN, RELATIONS, LAST = range(5)


def node_pass(nc, g, K, kind, name, table, affine=None):
    with ExitStack() as ctx:
        M = Memory(nc, ctx, K, name)
        N = g.blocks
        inner = kind in (ATTENTION, GIN)
        tables = kind in (ATTENTION, GIN, RELATIONS)
        first = kind in (ATTENTION, SOFTMAX, GIN)
        second = kind != RELATIONS
        rel_w = K.rel_w[0 if kind == GIN else 1]
        width = ROW1 if kind == ATTENTION else REL * D
        S = {n: M.sem(n) for n in ("input", "turned", "turned_out", "product", "hidden", "product2", "layer", "stats1",
                                   "root1", "norm1", "joined", "stats2", "root2", "norm2", "row_turned",
                                   "row_turned_out", "rows", "rows_act", "rows_dve", "kept",
                                   "begun")
             if not (n.endswith("1") and not first)}
        stored = [M.sem("stored0"), M.sem("stored1")]
        taken, taken_pool, taken_sp = M.sem("taken"), M.sem("taken_pool"), M.sem("taken_sp")
        joins = {ATTENTION: 3, SOFTMAX: 3, GIN: 4}.get(kind, 1)
        row_stored = [M.sem(f"row_stored{s}") for s in range(RING)] if kind in (LAST, SOFTMAX) else None
        uses = lambda u: u.i * 2 + u.s // 2
        z_in = M.sb("z_in", [P, RING, D])
        z_t = M.sb("z_t", [P, 2, D])
        hidden = M.sb("hidden", [P, 2, D])
        layer = M.sb("layer", [P, RING, D])
        norm = M.sb("norm", [P, RING, D])
        joined = M.sb("joined", [P, RING, D])
        fresh = M.sb("fresh", [P, RING, D])
        stats = [M.sb(f"stats{j}", [P, RING, 6]) for j in range(2)]
        moments = [M.sb(f"moments{j}", [P, RING, 2]) for j in range(2)]
        root = [M.sb(f"root{j}", [P, RING, 1]) for j in range(2)]
        scale = [M.sb(f"scale{j}", [P, RING, 1]) for j in range(2)]
        inv_z = M.sb("inv_z", [P, RING, 2, HEADS])
        x_t = M.sb("x_t", [P, 2, D])
        rows = M.sb("rows", [P, 2, width])
        block = ctx.enter_context(nc.Block())

        def after_stored(eng, u):
            value = uses(u) * 16
            if not (isinstance(value, int) and value <= 0):
                eng.wait_ge(stored[u.s % 2], value)

        def moments_of(dve, j, src, u):
            sem = S[f"stats{j + 1}"]
            after(dve, S[f"norm{j + 1}"], u, RING, per=2)
            after(dve, S[f"root{j + 1}"], u, RING)
            nc.vector.bn_stats(stats[j][:, u.s, :], src).then_inc(sem, 1)
            after(dve, sem, u, per=2, upto=1)
            dve.sem_inc(taken, 1)
            nc.vector.bn_aggr(moments[j][:, u.s, :], stats[j][:, u.s, :]).then_inc(sem, 1)

        def root_of(act, j, u):
            after(act, S[f"stats{j + 1}"], u, per=2)
            after(act, S[f"norm{j + 1}"], u, RING, per=2)
            nc.scalar.activation(root[j][:, u.s, :], moments[j][:, u.s, 1:2], ACT.Sqrt,
                                 bias=K.eps[:, :]).then_inc(S[f"root{j + 1}"], 1)

        def normalize(dve, j, out, src, u):
            sem = S[f"norm{j + 1}"]
            after(dve, S[f"root{j + 1}"], u)
            nc.vector.reciprocal(scale[j][:, u.s, :], root[j][:, u.s, :]).then_inc(sem, 1)
            after(dve, sem, u, per=2, upto=1)
            nc.vector.tensor_scalar(out, src, moments[j][:, u.s, 0:1], scale[j][:, u.s, :], ALU.subtract,
                                    ALU.mult).then_inc(sem, 1)

        @block.vector
        def _(dve):
            def enter(u):
                if kind == GIN:
                    after(dve, S["turned"], u, RING)
                    nc.vector.scalar_tensor_tensor(z_in[:, u.s, :], blk(K.x, u, D), K.eta1[:, :], blk(K.acc, u, D),
                                                   ALU.mult, ALU.add).then_inc(S["input"], 1)
                if kind == SOFTMAX:
                    after(dve, S["layer"], u, RING, per=2)
                    z = K.acc[:, bass.ds(u.at(), 1), 0:HEADS * HZ].rearrange("p a (h z) -> p (a h) z", h=HEADS)[:, :, HC]
                    nc.vector.tensor_scalar(inv_z[:, u.s, 0, :], z, SOFTMAX_EPS, None, ALU.add).then_inc(S["input"], 1)
                    after(dve, S["input"], u, per=2, upto=1)
                    nc.vector.reciprocal(inv_z[:, u.s, 1, :], inv_z[:, u.s, 0, :]).then_inc(S["input"], 1)
                if kind == RELATIONS:
                    after(dve, S["layer"], u, RING)
                    nc.vector.tensor_tensor(joined[:, u.s, :], blk(K.acc, u, D), blk(K.own, u, D),
                                            ALU.add).then_inc(S["input"], 1)
                if kind == LAST:
                    after(dve, S["norm2"], u, RING, per=2)
                    nc.vector.tensor_tensor(joined[:, u.s, :], blk(K.acc, u, D), blk(K.own, u, D),
                                            ALU.add).then_inc(S["joined"], 1)

            def make_layer(u):
                if kind == ATTENTION:
                    after(dve, S["product"], u)
                    nc.vector.tensor_tensor(layer[:, u.s, :], K.bank[1 + u.s % 2][:, 0:D], blk(K.x, u, D),
                                            ALU.add).then_inc(S["layer"], 1)
                    after(dve, S["layer"], u)
                if kind == SOFTMAX:
                    after(dve, S["input"], u, per=2)
                    acc = K.acc[:, bass.ds(u.at(), 1), 0:HEADS * HZ].rearrange("p a (h z) -> p (a h) z", h=HEADS)
                    nc.vector.tensor_tensor(z_in[:, u.s, :].rearrange("p (h c) -> p h c", h=HEADS), acc[:, :, 0:HC],
                                            inv_z[:, u.s, 1, :].unsqueeze(2).broadcast_to([P, HEADS, HC]),
                                            ALU.mult).then_inc(S["layer"], 1)
                    after(dve, S["layer"], u, per=2, upto=1)
                    nc.vector.tensor_tensor(layer[:, u.s, :], z_in[:, u.s, :], blk(K.own, u, D, 2 * HEADS),
                                            ALU.add).then_inc(S["layer"], 1)
                    after(dve, S["layer"], u, per=2)
                if kind == GIN:
                    after(dve, S["layer"], u)
                if first:
                    moments_of(dve, 0, layer[:, u.s, :], u)
                if kind == RELATIONS:
                    after(dve, S["input"], u)
                    after(dve, S["row_turned"], u, RING)
                    nc.vector.scalar_tensor_tensor(z_in[:, u.s, :], joined[:, u.s, :], 0.0, K.rel_b1[:, :], ALU.max,
                                                   ALU.add).then_inc(S["layer"], 1)

            def norm_first(u):
                if first:
                    after(dve, S["joined"], u, RING, per=joins)
                    normalize(dve, 0, norm[:, u.s, :], layer[:, u.s, :], u)

            def stats_second(u):
                if second:
                    after(dve, S["joined"], u, per=joins)
                    moments_of(dve, 1, joined[:, u.s, :], u)

            def norm_second(u):
                if second:
                    if row_stored:
                        after_row_stored(dve, u)
                    if kind != LAST:
                        after(dve, S["kept"], u, RING)
                    if tables:
                        after(dve, S["row_turned"], u, RING)
                    if kind == GIN:
                        after(dve, S["rows_dve"], u, RING, per=2)
                    normalize(dve, 1, fresh[:, u.s, :], joined[:, u.s, :], u)

            def after_row_stored(eng, u):
                value = u.i * 16
                if not (isinstance(value, int) and value <= 0):
                    eng.wait_ge(row_stored[u.s], value)

            def copy_rows(u):
                if kind in (GIN, RELATIONS):
                    after(dve, S["rows"], u, per=3)
                    after_stored(dve, u)
                    nc.vector.tensor_copy(rows[:, u.s % 2, 4 * D:8 * D], K.bank[5][:, :]).then_inc(S["rows_dve"], 1)
                    nc.vector.tensor_tensor(blk(K.own, u, D), K.bank[6 + u.s % 2][:, 0:D],
                                            fresh[:, u.s, :] if kind == GIN else blk(K.x, u, D),
                                            ALU.add).then_inc(S["rows_dve"], 1)

            pipeline(dve, N, RING, 4, stages(N, (0, enter), (3, stats_second), (2, make_layer), (3, norm_second),
                                             (2, norm_first), (4, copy_rows)))


        @block.gpsimd
        def _(pool):
            def join(u):
                j = S["joined"]
                after(pool, S["norm1"], u, per=2)
                after(pool, S["stats2"], u, RING, per=2)
                after(pool, S["norm2"], u, RING, per=2)
                o = joined[:, u.s, :]
                nc.gpsimd.tensor_tensor(o, norm[:, u.s, :], affine[0][:, :], ALU.mult).then_inc(j, 1)
                after(pool, j, u, per=joins, upto=1)
                nc.gpsimd.tensor_tensor(o, o, affine[1][:, :], ALU.add).then_inc(j, 1)
                for n in range(2, joins):
                    after(pool, j, u, per=joins, upto=n)
                    pool.sem_inc(taken_pool, 1)
                    nc.gpsimd.tensor_tensor(o, o, blk(K.x, u, D), ALU.add).then_inc(j, 1)

            def bring(u):
                if kind == ATTENTION:
                    after(pool, S["turned"], u, RING)
                    pool.sem_inc(taken_pool, 1)
                    nc.gpsimd.tensor_copy(z_in[:, u.s, :], blk(K.acc, u, D)).then_inc(S["input"], 1)

            def keep(u):
                after(pool, S["norm2"], u, per=2)
                if kind == ATTENTION:
                    after(pool, S["layer"], u)
                pool.sem_inc(taken_pool, 1)
                nc.gpsimd.tensor_copy(blk(K.x, u, D), fresh[:, u.s, :]).then_inc(S["kept"], 1)

            def begin(u):
                if kind == ATTENTION:
                    after(pool, S["rows_act"], u, per=2, upto=1)
                    pool.sem_inc(taken_pool, 1)
                    nc.gpsimd.tensor_copy(blk(K.acc, u, HEADS * HZ),
                                          rows[:, u.s % 2, 0:HEADS * HZ]).then_inc(S["begun"], 1)

            if first:
                pipeline(pool, N, RING, 4, stages(N, (0, bring), (2, join), (4, keep), (4, begin)))

        @block.scalar
        def _(act):
            def copy_turned(u):
                if inner:
                    after(act, S["turned"], u)
                    after(act, S["product"], u, 2)
                    nc.scalar.copy(z_t[:, u.s % 2, :], K.bank[0][:, 0:D]).then_inc(S["turned_out"], 1)

            def hide(u):
                if kind == GIN:
                    after(act, S["product"], u)
                    after(act, S["product2"], u, 2)
                    nc.scalar.activation(hidden[:, u.s % 2, :], K.bank[1][:, 0:D], ACT.Relu,
                                         bias=K.gin_b1[:, :]).then_inc(S["hidden"], 1)

            def show(u):
                if kind == GIN:
                    after(act, S["product2"], u)
                    after(act, S["norm1"], u, RING, per=2)
                    nc.scalar.activation(layer[:, u.s, :], K.bank[2][:, 0:D], ACT.Relu).then_inc(S["layer"], 1)

            def root_first(u):
                if first:
                    root_of(act, 0, u)

            def root_second(u):
                if second:
                    root_of(act, 1, u)

            def copy_row(u):
                if tables:
                    after(act, S["row_turned"], u)
                    after(act, S["rows"], u, 2, per=3 if kind != ATTENTION else 1)
                    nc.scalar.copy(x_t[:, u.s % 2, :], K.bank[3][:, 0:D]).then_inc(S["row_turned_out"], 1)

            def copy_rows(u):
                if kind == ATTENTION:
                    bank = K.bank[4 + u.s % 2]
                    after(act, S["rows"], u)
                    after_stored(act, u)
                    after(act, S["begun"], u, 2)
                    nc.scalar.copy(rows[:, u.s % 2, :], bank[:, 0:ROW1]).then_inc(S["rows_act"], 1)
                    nc.scalar.copy(blk(K.own, u, OWN1), bank[:, ROW1 - HEADS:WIDE1]).then_inc(S["rows_act"], 1)
                elif tables:
                    after(act, S["rows"], u, per=3, upto=1)
                    after_stored(act, u)
                    nc.scalar.copy(rows[:, u.s % 2, 0:4 * D], K.bank[4][:, :]).then_inc(S["rows_act"], 1)

            pipeline(act, N, RING, 4, stages(N, (1, copy_turned), (3, root_second), (4, copy_row), (2, root_first),
                                             (1, hide), (4, copy_rows), (1, show)))

        @block.tensor
        def _(pe):
            def turn(u):
                if inner:
                    after(pe, S["input"], u)
                    after(pe, S["turned_out"], u, 1)
                    nc.tensor.transpose(K.bank[0][:, 0:D], z_in[:, u.s, :], K.ident[:, :]).then_inc(S["turned"], 1)

            def multiply(u):
                if kind == ATTENTION:
                    after(pe, S["turned_out"], u)
                    after(pe, S["layer"], u, 2)
                    out = K.bank[1 + u.s % 2][:, 0:D]
                    nc.tensor.matmul(out, z_t[:, u.s % 2, :], K.vo[:, :], start=True, stop=False)
                    nc.tensor.matmul(out, K.ones[0:1, :], K.b0[:, :], start=False, stop=True).then_inc(S["product"], 1)
                if kind == GIN:
                    after(pe, S["turned_out"], u)
                    after(pe, S["hidden"], u, 1)
                    nc.tensor.matmul(K.bank[1][:, 0:D], K.gin_w1[:, :], z_t[:, u.s % 2, :], start=True,
                                     stop=True).then_inc(S["product"], 1)

            def multiply2(u):
                if kind == GIN:
                    after(pe, S["hidden"], u)
                    after(pe, S["layer"], u, 1)
                    nc.tensor.matmul(K.bank[2][:, 0:D], hidden[:, u.s % 2, :], K.gin_w2[:, :], start=True, stop=False)
                    nc.tensor.matmul(K.bank[2][:, 0:D], K.ones[0:1, :], K.gin_b2[:, :], start=False,
                                     stop=True).then_inc(S["product2"], 1)

            def turn_row(u):
                if tables:
                    after(pe, S["layer"] if kind == RELATIONS else S["norm2"], u, per=1 if kind == RELATIONS else 2)
                    after(pe, S["row_turned_out"], u, 1)
                    src = z_in[:, u.s, :] if kind == RELATIONS else fresh[:, u.s, :]
                    nc.tensor.transpose(K.bank[3][:, 0:D], src, K.ident[:, :]).then_inc(S["row_turned"], 1)

            def make_rows(u):
                if kind == ATTENTION:
                    bank = K.bank[4 + u.s % 2]
                    after(pe, S["row_turned_out"], u)
                    after(pe, S["rows_act"], u, 2, per=2)
                    nc.tensor.matmul(bank[:, 0:WIDE1], x_t[:, u.s % 2, :], K.w1[:, :], start=True, stop=False)
                    nc.tensor.matmul(bank[:, 0:WIDE1], K.ones[0:1, :], K.b1[:, :], start=False,
                                     stop=True).then_inc(S["rows"], 1)
                elif tables:
                    after(pe, S["row_turned_out"], u)
                    after(pe, S["rows_act"], u, 1)
                    nc.tensor.matmul(K.bank[4][:, :], x_t[:, u.s % 2, :], rel_w[:, 0:4, :], start=True,
                                     stop=True).then_inc(S["rows"], 1)
                    after(pe, S["rows_dve"], u, 1, per=2)
                    nc.tensor.matmul(K.bank[5][:, :], x_t[:, u.s % 2, :], rel_w[:, 4:8, :], start=True,
                                     stop=True).then_inc(S["rows"], 1)
                    own = K.bank[6 + u.s % 2][:, 0:D]
                    last = nc.tensor.matmul(own, x_t[:, u.s % 2, :], rel_w[:, REL, :], start=True, stop=(kind == GIN))
                    if kind == RELATIONS:
                        last = nc.tensor.matmul(own, K.ones[0:1, :], K.rel_b2[:, :], start=False, stop=True)
                    last.then_inc(S["rows"], 1)

            pipeline(pe, N, RING, 4, stages(N, (1, turn), (4, turn_row), (1, multiply), (4, make_rows), (1, multiply2)))

        @block.sync
        def _(sp):
            def store(u):
                if tables:
                    after(sp, S["rows_act"], u, per=2 if kind == ATTENTION else 1)
                    if kind != ATTENTION:
                        sp.sem_inc(taken_sp, 1)
                        after(sp, S["rows_dve"], u, per=2)
                    sp.sem_inc(taken_sp, 1)
                    sp.dma_start(table[bass.ds(u.at(P), P), :], rows[:, u.s % 2, :]).then_inc(stored[u.s % 2], 16)
                if kind == SOFTMAX:
                    after(sp, S["norm2"], u, per=2)
                    sp.sem_inc(taken_sp, 1)
                    sp.dma_start(table[bass.ds(u.at(P), P), :], fresh[:, u.s, :]).then_inc(row_stored[u.s], 16)
                if kind == LAST:
                    after(sp, S["norm2"], u, per=2)
                    sp.sem_inc(taken_sp, 1)
                    n = g.tail if isinstance(u.i, int) and u.at() == N - 1 else P
                    sp.dma_start(table[bass.ds(u.at(P), n), :], fresh[0:n, u.s, :]).then_inc(row_stored[u.s], 16)

            pipeline(sp, N, RING, 0, stages(N, (0, store)))
            if row_stored:
                for s in range(RING):
                    sp.wait_ge(row_stored[s], 16 * ((N - s + RING - 1) // RING))
            else:
                for s in range(2):
                    sp.wait_ge(stored[s], 16 * ((N - s + 1) // 2))


class Kept:

    def __init__(self, nc, ctx, g):
        def sb(name, shape, dt=F32):
            return ctx.enter_context(nc.sbuf_tensor(name, shape, dt))

        self.semaphores = []
        NB, NI = g.blocks, g.items
        self.bank = [ctx.enter_context(nc.psum_tensor(f"bank{j}", [P, 512], F32)) for j in range(8)]
        self.x = sb("x_nodes", [P, NB, D])
        self.own = sb("own", [P, NB, OWN1])
        self.acc = sb("acc", [P, NB, HEADS * HZ])
        self.node = sb("node", [P, NI])
        self.src_row = sb("src_row", [P, NI], I32)
        self.rel_row = sb("rel_row", [P, NI], I32)
        self.ends = sb("ends", [P, NI])
        self.starts = sb("starts", [P, NI])
        self.cut = sb("cut", [P, g.units, HEADS * (UNIT + 1)])
        self.block_no = sb("block_no", [1, NI], I32)
        self.rows = sb("row_numbers", [P, RING, UNIT], I32)
        self.ring = sb("ring", [P, RING * UNIT, ROW1])
        self.member = sb("member", [P, RING, UNIT, P])
        self.ident, self.col, self.part = sb("ident", [P, P]), sb("col", [P, P]), sb("part", [P, 1])
        self.ones, self.eps = sb("ones", [P, P]), sb("eps", [P, 1])
        self.qk, self.vo = sb("qk", [P, P]), sb("vo", [P, P])
        self.w1, self.b1 = sb("w1", [P, WIDE1]), sb("b1", [1, WIDE1])
        self.b0 = sb("b0", [1, D])
        self.gin_w1, self.gin_w2 = sb("gin_w1", [P, D]), sb("gin_w2", [P, D])
        self.gin_b1, self.gin_b2 = sb("gin_b1", [P, 1]), sb("gin_b2", [1, D])
        self.eta1 = sb("eta1", [P, 1])
        self.affine = [sb(f"affine{j}", [P, D]) for j in range(6)]
        self.rel_w = [sb(f"rel_w{j}", [P, REL + 1, D]) for j in range(2)]
        self.rel_b1, self.rel_b2 = sb("rel_b1", [P, D]), sb("rel_b2", [1, D])


def gnn(nc, W, out, stop=99):
    g = Graph(W["x"].shape[0], W["src"].shape[0])
    rows = g.blocks * P
    with ExitStack() as ctx:
        K = Kept(nc, ctx, g)
        soft_table = nc.dram_tensor("soft_table", (rows, ROW1), F32).ap()
        gin_table = nc.dram_tensor("gin_table", (rows, D), F32).ap()
        rel_tables = [nc.dram_tensor(f"rel_table{j}", (rows, REL * D), F32).ap() for j in range(2)]
        by_relation = lambda t: t.rearrange("n (r c) -> (n r) c", r=REL)
        parts = [
            lambda: load_and_fold(nc, g, K, W),
            lambda: build_graph(nc, g, K, W["src"], W["dst"], W["edge_type_8"]),
            lambda: query_rows(nc, g, K),
            lambda: attention_items(nc, g, K, W["x"]),
            lambda: node_pass(nc, g, K, ATTENTION, "attn_nodes", soft_table, K.affine[0:2]),
            lambda: softmax_items(nc, g, K, soft_table),
            lambda: node_pass(nc, g, K, SOFTMAX, "soft_nodes", gin_table, K.affine[2:4]),
            lambda: sum_items(nc, g, K, "gin", gin_table, K.src_row),
            lambda: node_pass(nc, g, K, GIN, "gin_nodes", rel_tables[0], K.affine[4:6]),
            lambda: sum_items(nc, g, K, "rel1", by_relation(rel_tables[0]), K.rel_row),
            lambda: node_pass(nc, g, K, RELATIONS, "rel1_nodes", rel_tables[1]),
            lambda: sum_items(nc, g, K, "rel2", by_relation(rel_tables[1]), K.rel_row),
            lambda: node_pass(nc, g, K, LAST, "rel2_nodes", out),
        ]
        for part in parts[:stop]:
            part()
            nc.clear_and_free_semaphores(K.semaphores)
            nc.all_engine_barrier()
            K.semaphores = []
        return K


_INS = ["x", "src", "dst", "edge_type_8", "L0_gnn_Wq", "L0_gnn_Wk", "L0_gnn_Wv", "L0_gnn_Wo", "L0_gnn_bo",
        "L0_gnn_gamma", "L0_gnn_beta", "L1_gnn_W", "L1_gnn_att_src", "L1_gnn_att_dst", "L1_gnn_gat_bias",
        "L1_gnn_skip_W", "L1_gnn_skip_b", "L1_gnn_ln_g", "L1_gnn_ln_b", "L2_gnn_W1", "L2_gnn_b1", "L2_gnn_W2",
        "L2_gnn_b2", "L2_gnn_eta", "L2_gnn_ln_gamma", "L2_gnn_ln_beta", "L3_gnn_w1", "L3_gnn_sw1", "L3_gnn_b1",
        "L3_gnn_w2", "L3_gnn_sw2", "L3_gnn_b2"]


def kernel(**inputs):
    import numpy as np
    import concourse.bacc as bacc
    from concourse.bass_utils import run_bass_kernel_spmd

    nc = bacc.Bacc("TRN2", target_bir_lowering=False, num_devices=1)
    arrays, tensors = {}, {}
    for name in _INS:
        a = np.ascontiguousarray(inputs[name])
        arrays[f"in_{name}"] = a
        tensors[name] = nc.dram_tensor(f"in_{name}", a.shape, mybir.dt.from_np(a.dtype), kind="ExternalInput").ap()
    out = nc.dram_tensor("out_nodes", inputs["x"].shape, F32, kind="ExternalOutput").ap()
    gnn(nc, tensors, out)
    return run_bass_kernel_spmd(nc, [arrays], core_ids=[0]).results[0]["out_nodes"]
```

```python
import concourse.bass as bass
from concourse import mybir
from contextlib import ExitStack

P = 128
F32 = mybir.dt.float32
BF16 = mybir.dt.bfloat16
I32 = mybir.dt.int32
ALU = mybir.AluOpType
ACT = mybir.ActivationFunctionType
AX = mybir.AxisListType

D = 128
HEADS, HC = 4, 32
HZ = HC + 1
REL = 8
LN_EPS = 1e-05
SOFTMAX_EPS = 1e-16
SLOPE = 0.2
FAR = float(2.0 ** 100)
NO_NODE = (P - 1) * P

UNIT = 4
RING = 4
LONG_RING = 8
ROW1 = HEADS * HZ + HEADS
WIDE1 = ROW1 + HEADS + D
OWN1 = 2 * HEADS + D


class Step:

    def __init__(self, i, s, per):
        self.i, self.s, self.per = i, s, per

    def back(self, lag):
        s = self.s - lag
        return Step(self.i + s // self.per, s % self.per, self.per)

    def at(self, scale=1, offset=0):
        return self.i * (self.per * scale) + (self.s * scale + offset)

    def exists(self, total):
        return not isinstance(self.i, int) or 0 <= self.at() < total


def after(eng, sem, u, back=0, per=1, upto=None):
    value = u.at(per, (upto if upto is not None else per) - back * per)
    if isinstance(value, int) and value <= 0:
        return
    eng.wait_ge(sem, value)


def pipeline(eng, total, per, longest, step, peel=2):
    full = total // per
    for n in range(peel * per):
        step(Step(n // per, n % per, per))
    with eng.Fori(peel, full) as i:
        for s in range(per):
            step(Step(i, s, per))
    for n in range(full * per, total + longest):
        step(Step(n // per, n % per, per))


def stages(total, *parts):
    def step(u):
        for lag, stage in parts:
            v = u.back(lag)
            if v.exists(total):
                stage(v)
    return step


class Memory:

    def __init__(self, nc, ctx, K, name):
        self.nc, self.ctx, self.K, self.name = nc, ctx, K, name

    def sb(self, name, shape, dt=F32):
        return self.ctx.enter_context(self.nc.sbuf_tensor(f"{self.name}_{name}", shape, dt))

    def within(self, t, taken, shape, dt=F32):
        flat = t[:, :, :].rearrange("p b d -> p (b d)")
        count = 1
        for n in shape[1:]:
            count *= n
        flat = flat[:, taken:taken + count]
        if dt is not F32:
            flat = flat.bitcast(dt)
        return flat if len(shape) == 2 else flat.rearrange("p (g c) -> p g c", c=shape[2])

    def sem(self, name):
        one = self.nc.alloc_semaphore(f"{self.name}_{name}")
        self.K.semaphores.append(one)
        return one


def bcast(ap, axis, count):
    shape = list(ap.shape)
    ap = ap.unsqueeze(axis)
    shape.insert(axis, count)
    return ap.broadcast_to(shape)


class Graph:

    def __init__(self, nodes, edges):
        self.nodes, self.edges = nodes, edges
        self.blocks = -(-nodes // P)
        self.tail = nodes - (self.blocks - 1) * P
        self.tiles = -(-edges // P)
        self.groups = -(-self.tiles // P)
        body = UNIT * RING
        self.items = -(-(self.tiles + self.blocks - 1) // body) * body
        self.units = self.items // UNIT
        assert self.items <= self.groups * P and nodes * REL < 1 << 24 and self.blocks < P


def edge_rows(g, K):
    flat = K.ring[:, :, :].rearrange("p b d -> p (b d)").bitcast(I32)
    n = g.groups * P
    return [flat[:, j * n:(j + 1) * n].rearrange("p (g c) -> p g c", c=P) for j in range(3)]


def order_edges(nc, g, K, src, dst, edge_type, records):
    G = g.groups
    NT = G * P
    full = (g.edges // P) % P
    rest = g.edges % P
    low, high = 4, 3
    with ExitStack() as ctx:
        M = Memory(nc, ctx, K, "order")
        rows = edge_rows(g, K)
        first_dst = M.sb("first_dst", [P, G], I32)
        next_dst = M.sb("next_dst", [P, G], I32)
        bad, bad_sum = M.sb("bad", [P, 2]), M.sb("bad_sum", [P, 1])
        unsorted = M.sb("unsorted", [1, 1], I32)
        place_u = M.sb("place_u", [P, 2, UNIT], I32)
        record_u = M.sb("record_u", [P, 2, UNIT, 3], I32)
        row_f = M.within(K.acc, 0, [P, G, P])
        worse = M.within(K.acc, NT, [P, G, P])
        digit_f, place_f = M.within(K.acc, NT, [P, NT]), M.within(K.acc, 2 * NT, [P, NT])
        digit_i = M.within(K.acc, 3 * NT, [P, NT], I32)
        place_i = digit_i
        record = M.within(K.acc, 4 * NT, [P, NT, 3], I32)
        record_rows = M.within(K.own, 0, [P, G, 3 * P], I32)
        mask, product = K.member[:, 0, :, :], K.member[:, 1, :, :]
        before, carry, count = (K.member[:, 2, j, :] for j in range(3))
        firsts_ready = M.sem("firsts_ready")
        padded, loaded, shifted, chain = M.sem("padded"), M.sem("loaded"), M.sem("shifted"), M.sem("chain")
        bad_ready, bad_summed, flag_ready = M.sem("bad_ready"), M.sem("bad_summed"), M.sem("flag")
        row_ready, turned, masks_ready, ranked = M.sem("row"), M.sem("turned"), M.sem("masks"), M.sem("ranked")
        counted, counts_ready, based, based_out = M.sem("counted"), M.sem("counts"), M.sem("based"), M.sem("based_out")
        staged, sorted_out, reloaded, unpacked = M.sem("staged"), M.sem("sorted_out"), M.sem("reloaded"), M.sem("unpacked")
        scattered = [M.sem(f"scattered{j}") for j in range(2)]
        opened, rank_chain = M.sem("opened"), M.sem("rank_chain")
        units = NT // UNIT
        block = ctx.enter_context(nc.Block())

        def when_unsorted(eng, engine):
            eng.wait_ge(flag_ready, 1)
            flag = nc.values_load_multi_w_load_instructions(
                unsorted[0:1, 0:1], engines=(engine,), min_val=0, max_val=1,
                skip_runtime_bounds_check_because="it is the result of a comparison")[1][0]
            return eng.If(flag > 0)

        @block.sync
        def _(sp):
            sp.wait_ge(padded, 1)
            for into, flat in zip(rows, (dst, src, edge_type)):
                whole = (G - 1) * P * P
                sp.dma_start(into[:, 0:G - 1, :],
                             flat[0:whole].rearrange("(g r c) -> r g c", r=P, c=P)).then_inc(loaded, 16)
                sp.dma_start(into[0:full, G - 1, :],
                             flat[whole:whole + full * P].rearrange("(r c) -> r c", c=P)).then_inc(loaded, 16)
                sp.dma_start(into[full:full + 1, G - 1, 0:rest],
                             flat[whole + full * P:g.edges].rearrange("(r c) -> r c", r=1)).then_inc(loaded, 16)
            sp.wait_ge(firsts_ready, 1)
            sp.dma_start(next_dst[0:P - 1, :], first_dst[1:P, :]).then_inc(shifted, 16)
            sp.dma_start(next_dst[P - 1:P, 0:G - 1], first_dst[0:1, 1:G]).then_inc(shifted, 16)
            with when_unsorted(sp, mybir.EngineType.SP):
                for digit in range(2):
                    sp.wait_ge(sorted_out, digit + 1)
                    sp.dma_start(record_rows[:, :, :], records.rearrange("(g r c) k -> r g (c k)", r=P, c=P)
                                 ).then_inc(reloaded, 16)

        @block.gpsimd
        def _(pool):
            with when_unsorted(pool, mybir.EngineType.Pool):
                for digit in range(2):
                    with pool.Fori(0, units // 2) as i:
                        for s in range(2):
                            pool.wait_ge(staged, i * 2 + (digit * units + s + 1))
                            pool.sem_inc(opened, 1)
                            for k in range(UNIT):
                                pool.indirect_dma_start(
                                    out=records, in_=record_u[:, s, k, :], in_offset=None,
                                    out_offset=bass.IndirectOffsetOnAxis(ap=place_u[:, s, k:k + 1], axis=0),
                                ).then_inc(scattered[s], 16)
                    for s in range(2):
                        pool.wait_ge(scattered[s], (digit + 1) * 16 * UNIT * (units // 2))
                    pool.sem_inc(sorted_out, 1)

        @block.vector
        def _(dve):
            link = [0]

            def chained(ins):
                link[0] += 1
                ins.then_inc(chain, 1)
                dve.wait_ge(chain, link[0])

            nc.vector.memset(next_dst[:, :], NO_NODE)
            nc.vector.memset(rows[1][:, G - 1, :], 0)
            nc.vector.memset(rows[2][:, G - 1, :], 0)
            nc.vector.memset(rows[0][:, G - 1, :], NO_NODE).then_inc(padded, 1)
            dve.wait_ge(padded, 1)
            dve.wait_ge(loaded, 9 * 16)
            nc.vector.tensor_copy(first_dst[:, :], rows[0][:, :, 0]).then_inc(firsts_ready, 1)
            dve.wait_ge(shifted, 2 * 16)
            nc.vector.tensor_tensor(worse[:, :, 0:P - 1], rows[0][:, :, 0:P - 1], rows[0][:, :, 1:P], ALU.is_gt)
            chained(nc.vector.tensor_tensor(worse[:, :, P - 1], rows[0][:, :, P - 1], next_dst[:, :], ALU.is_gt))
            nc.vector.tensor_reduce(bad_sum[:, :], worse.rearrange("p g c -> p (g c)"), AX.X,
                                    ALU.add).then_inc(bad_ready, 1)
            dve.wait_ge(bad_summed, 1)
            nc.vector.tensor_scalar(unsorted[:, :], K.bank[0][0:1, 0:1], 0.0, None, ALU.is_gt).then_inc(flag_ready, 1)
            with when_unsorted(dve, mybir.EngineType.DVE):
                chained(nc.vector.tensor_scalar(before, K.col[:, :], K.part[:, :], None, ALU.is_gt))
                for digit in range(2):
                    for a in range(3):
                        if digit or a:
                            dve.wait_ge(turned, digit * 3 + a)
                        chained(nc.vector.tensor_copy(row_f[:, :, :], rows[a]))
                        dve.sem_inc(row_ready, 1)
                        dve.wait_ge(turned, digit * 3 + a + 1)
                        nc.vector.tensor_copy(record[:, 0:low * P, a], K.bank[0][:, :])
                        chained(nc.vector.tensor_copy(record[:, low * P:NT, a], K.bank[1][:, 0:high * P]))
                    if digit == 0:
                        chained(nc.vector.tensor_scalar(digit_i, record[:, :, 0], P - 1, None, ALU.bitwise_and))
                    else:
                        chained(nc.vector.tensor_scalar(digit_i, record[:, :, 0], P.bit_length() - 1, None,
                                                        ALU.logical_shift_right))
                    nc.vector.tensor_copy(digit_f, digit_i)
                    chained(nc.vector.memset(product, 0.0))
                    each = lambda i: digit_f[:, bass.ds(i * UNIT, UNIT)].unsqueeze(2).broadcast_to([P, UNIT, P])
                    seen, link_0 = masks_ready, digit * 2 * units
                    with dve.Fori(0, units) as i:
                        nc.vector.tensor_tensor(mask, bcast(K.col[:, :], 1, UNIT), each(i), ALU.is_equal).then_inc(seen, 1)
                        dve.wait_ge(seen, i * 2 + (link_0 + 1))
                        nc.vector.tensor_tensor(product, product, mask, ALU.add).then_inc(seen, 1)
                        dve.wait_ge(seen, i * 2 + (link_0 + 2))
                    dve.sem_inc(counted, 1)
                    dve.wait_ge(counts_ready, digit + 1)
                    chained(nc.vector.tensor_copy(count, K.bank[2][:, 0:P]))
                    dve.sem_inc(counted, 1)
                    dve.wait_ge(based, digit + 1)
                    chained(nc.vector.tensor_copy(carry, K.bank[3][:, 0:P]))
                    dve.sem_inc(based_out, 1)
                    with dve.Fori(0, units) as i:
                        rank = i * 4 + digit * 4 * units
                        nc.vector.tensor_tensor(mask, bcast(K.col[:, :], 1, UNIT), each(i), ALU.is_equal
                                                ).then_inc(based_out, 1)
                        dve.wait_ge(ranked, i + (digit * units + 1))
                        nc.vector.tensor_tensor(product, K.bank[2][:, :].rearrange("p (k d) -> p k d", k=UNIT),
                                                bcast(carry, 1, UNIT), ALU.add).then_inc(rank_chain, 1)
                        dve.wait_ge(rank_chain, rank + 1)
                        nc.vector.tensor_tensor(carry, carry, K.bank[3][:, 0:P], ALU.add).then_inc(rank_chain, 1)
                        nc.vector.tensor_tensor(product, product, mask, ALU.mult).then_inc(rank_chain, 1)
                        dve.wait_ge(rank_chain, rank + 3)
                        nc.vector.tensor_reduce(place_f[:, bass.ds(i * UNIT, UNIT)], product, AX.X,
                                                ALU.add).then_inc(rank_chain, 1)
                        dve.wait_ge(rank_chain, rank + 4)
                    chained(nc.vector.tensor_copy(place_i, place_f))

                    def stage(i, s):
                        nc.vector.tensor_copy(place_u[:, s, :], place_i[:, bass.ds(i * (2 * UNIT) + s * UNIT, UNIT)])
                        nc.vector.tensor_copy(record_u[:, s, :, :],
                                              record[:, bass.ds(i * (2 * UNIT) + s * UNIT, UNIT), :]).then_inc(staged, 1)

                    for s in range(2):
                        stage(0, s)
                    with dve.Fori(1, units // 2) as i:
                        for s in range(2):
                            dve.wait_ge(scattered[s], i * (16 * UNIT) + digit * 16 * UNIT * (units // 2))
                            stage(i, s)
                    dve.wait_ge(reloaded, 16 * (digit + 1))
                    for a in range(3):
                        last = nc.vector.tensor_copy(rows[a], record_rows.rearrange("p g (c k) -> p g c k", k=3)[:, :, :, a])
                    chained(last)

        @block.tensor
        def _(pe):
            pe.wait_ge(bad_ready, 1)
            nc.tensor.matmul(K.bank[0][0:1, 0:1], bad_sum[:, :], K.ones[:, 0:1], start=True,
                             stop=True).then_inc(bad_summed, 1)
            with when_unsorted(pe, mybir.EngineType.PE):
                for digit in range(2):
                    for a in range(3):
                        pe.wait_ge(row_ready, digit * 3 + a + 1)
                        for q in range(G):
                            last = nc.tensor.transpose(K.bank[q // low][:, (q % low) * P:(q % low + 1) * P],
                                                       row_f[:, q, :], K.ident[:, :])
                        last.then_inc(turned, 1)
                    pe.wait_ge(counted, 2 * digit + 1)
                    for k in range(UNIT):
                        last = nc.tensor.matmul(K.bank[2][:, 0:P], product[:, k, :], K.ones[:, :], start=(k == 0),
                                                stop=(k == UNIT - 1))
                    last.then_inc(counts_ready, 1)
                    pe.wait_ge(counted, 2 * digit + 2)
                    nc.tensor.matmul(K.bank[3][:, 0:P], count, before, start=True, stop=True).then_inc(based, 1)
                    pe.wait_ge(based_out, digit * (units + 1) + 1)
                    with pe.Fori(0, units) as i:
                        pe.wait_ge(based_out, i + (digit * (units + 1) + 2))
                        nc.tensor.matmul(K.bank[2][:, :], before, mask, start=True, stop=False)
                        for k in range(1, UNIT):
                            last = nc.tensor.matmul(K.bank[2][:, k * P:], K.ones[:, :], mask[:, 0:UNIT - k, :],
                                                    start=False, stop=(k == UNIT - 1))
                        for k in range(UNIT):
                            last = nc.tensor.matmul(K.bank[3][:, 0:P], K.ones[:, :], mask[:, k, :], start=(k == 0),
                                                    stop=(k == UNIT - 1))
                        last.then_inc(ranked, 1)


def build_graph(nc, g, K):
    G, NB, NI = g.groups, g.blocks, g.items
    NT = G * P
    with ExitStack() as ctx:
        M = Memory(nc, ctx, K, "prep")
        dst_rows, src_rows, type_rows = edge_rows(g, K)
        dst_f, src_f, rel_f, end_f, start_f = (M.within(K.acc, j * NT, [P, G, P]) for j in range(5))
        limit = M.sb("limit", [P, NB - 1, 1])
        before = M.sb("before", [P, NB - 1, G])
        tiles_before = M.sb("tiles_before", [P, NB - 1])
        rank = M.sb("rank", [P, 1])
        item_no, item_mod, block_past, block_of, place, pick_own, pick_prev = (
            M.within(K.own, j * NT, [P, NT]) for j in range(7))
        change = item_no
        consts = M.sem("consts")
        chain, rank_sum, rank_ready = M.sem("chain"), M.sem("rank_sum"), M.sem("rank_ready")
        mask_ready, blocks_ready, picks_ready = M.sem("mask_ready"), M.sem("blocks_ready"), M.sem("picks_ready")
        table_ready, table_out = M.sem("table_ready"), M.sem("table_out")
        block = ctx.enter_context(nc.Block())
        half = NT // 2
        arrays = [dst_f, src_f, rel_f, end_f, start_f]

        @block.gpsimd
        def _(pool):
            nc.gpsimd.iota(limit[:, :, :], [[P, NB - 1]], base=P, channel_multiplier=0,
                           allow_small_or_imprecise_dtypes=True).then_inc(consts, 1)
            nc.gpsimd.iota(item_no[:, :], [[1, NT]], base=0, channel_multiplier=0,
                           allow_small_or_imprecise_dtypes=True).then_inc(consts, 1)
            nc.gpsimd.iota(item_mod[:, :], [[0, G], [1, P]], base=0, channel_multiplier=0,
                           allow_small_or_imprecise_dtypes=True).then_inc(consts, 1)

        @block.vector
        def _(dve):
            link = [0]

            def chained(ins):
                link[0] += 1
                ins.then_inc(chain, 1)
                dve.wait_ge(chain, link[0])

            dve.wait_ge(consts, 3)
            nc.vector.tensor_copy(dst_f[:, :, :], dst_rows[:, :, :])
            nc.vector.tensor_copy(src_f[:, :, :], src_rows[:, :, :])
            chained(nc.vector.tensor_copy(rel_f[:, :, :], type_rows[:, :, :]))
            chained(nc.vector.tensor_tensor(before[:, :, :], bcast(dst_f[:, :, P - 1], 1, NB - 1),
                                            limit[:, :, :].broadcast_to([P, NB - 1, G]), ALU.is_lt))
            nc.vector.tensor_reduce(tiles_before[:, :], before[:, :, :], AX.X, ALU.add).then_inc(rank_ready, 1)
            chained(nc.vector.scalar_tensor_tensor(rel_f[:, :, :], src_f[:, :, :], float(REL), rel_f[:, :, :],
                                                   ALU.mult, ALU.add))
            nc.vector.memset(end_f[:, :, :], 1.0)
            chained(nc.vector.memset(start_f[:, :, :], -FAR))
            chained(nc.vector.tensor_tensor(end_f[:, :, 0:P - 1], dst_f[:, :, 0:P - 1], dst_f[:, :, 1:P],
                                            ALU.not_equal))
            chained(nc.vector.tensor_scalar(start_f[:, :, 1:P], end_f[:, :, 0:P - 1], -FAR, None, ALU.mult))
            dve.wait_ge(rank_sum, 1)
            chained(nc.vector.tensor_tensor(rank[0:NB - 1, :], K.bank[0][0:NB - 1, 0:1], K.part[0:NB - 1, :],
                                            ALU.add))
            nc.vector.tensor_scalar(block_past[0:NB - 1, :], item_no[0:NB - 1, :], rank[0:NB - 1, :], None,
                                    ALU.is_gt).then_inc(mask_ready, 1)
            dve.wait_ge(blocks_ready, 1)
            for h in range(2):
                last = nc.vector.tensor_copy(block_of[:, h * half:(h + 1) * half], K.bank[1 + h][:, 0:half])
            chained(last)
            nc.vector.tensor_copy(K.block_no[:, :], block_of[0:1, 0:NI])
            chained(nc.vector.tensor_tensor(place[:, :], item_mod[:, :], block_of[:, :], ALU.subtract))
            nc.vector.tensor_scalar(pick_own[:, :], place[:, :], K.part[:, :], None, ALU.is_equal)
            nc.vector.tensor_scalar(pick_prev[:, :], place[:, :], float(P), K.part[:, :], ALU.add,
                                    ALU.is_equal).then_inc(picks_ready, 1)
            nc.vector.memset(change[:, 0:1], -FAR)
            chained(nc.vector.tensor_tensor(change[:, 1:NT], block_of[:, 1:NT], block_of[:, 0:NT - 1],
                                            ALU.not_equal))
            chained(nc.vector.tensor_scalar(change[:, 1:NT], change[:, 1:NT], -FAR, None, ALU.mult))
            cut = K.cut[:, :, :].rearrange("p u (h k) -> p u h k", h=HEADS)
            nc.vector.memset(cut[:, :, :, 0], -FAR)
            for h in range(HEADS):
                nc.vector.tensor_copy(cut[:, :, h, 1:UNIT + 1],
                                      change[:, 0:NI].rearrange("p (u k) -> p u k", k=UNIT))
            for a in range(5):
                dve.wait_ge(table_ready, a + 1)
                lo, hi = K.bank[3 + 2 * (a % 2)], K.bank[4 + 2 * (a % 2)]
                for bank, c0, n in ((lo, 0, half), (hi, half, NI - half)):
                    if a == 0:
                        last = nc.vector.scalar_tensor_tensor(K.node[:, c0:c0 + n], block_of[:, c0:c0 + n], float(-P),
                                                              bank[:, 0:n], ALU.mult, ALU.add)
                    else:
                        into = (K.src_row, K.rel_row, K.ends, K.starts)[a - 1]
                        last = nc.vector.tensor_copy(into[:, c0:c0 + n], bank[:, 0:n])
                last.then_inc(table_out, 1)

        @block.tensor
        def _(pe):
            pe.wait_ge(rank_ready, 1)
            nc.tensor.matmul(K.bank[0][0:NB - 1, 0:1], tiles_before[:, :], K.ones[:, 0:1], start=True,
                             stop=True).then_inc(rank_sum, 1)
            pe.wait_ge(mask_ready, 1)
            for h in range(2):
                last = nc.tensor.matmul(K.bank[1 + h][:, 0:half], K.ones[0:NB - 1, :],
                                        block_past[0:NB - 1, h * half:(h + 1) * half], start=True, stop=True)
            last.then_inc(blocks_ready, 1)
            pe.wait_ge(picks_ready, 1)
            pe.wait_ge(chain, 7)
            for a, rows in enumerate(arrays):
                if a >= 2:
                    pe.wait_ge(table_out, a - 1)
                for q in range(G):
                    for c0, n in ((q * P, min(P, max(0, half - q * P))), (max(q * P, half), min(P, (q + 1) * P - half))):
                        if n <= 0 or c0 >= (q + 1) * P:
                            continue
                        bank, at = (K.bank[3 + 2 * (a % 2)], c0) if c0 < half else (K.bank[4 + 2 * (a % 2)], c0 - half)
                        last = nc.tensor.matmul(bank[:, at:at + n], rows[:, q, :], pick_own[:, c0:c0 + n],
                                                start=True, stop=(q == 0))
                        if q:
                            last = nc.tensor.matmul(bank[:, at:at + n], rows[:, q - 1, :], pick_prev[:, c0:c0 + n],
                                                    start=False, stop=True)
                last.then_inc(table_ready, 1)


def load_and_fold(nc, g, K, W):
    with ExitStack() as ctx:
        M = Memory(nc, ctx, K, "fold")
        part_no = M.sb("part_no", [P, 1], I32)
        col_no = M.sb("col_no", [P, P], I32)
        wq, wk, wv, wo = (M.sb(n, [P, P]) for n in ("wq", "wk", "wv", "wo"))
        wo_t = M.sb("wo_t", [P, P])
        w1, w1_t, att = M.sb("w1", [P, P]), M.sb("w1_t", [P, P]), M.sb("att", [P, 2 * HEADS])
        gin1, gin2 = M.sb("gin1", [P, P]), M.sb("gin2", [P, P])
        skip_b = M.sb("skip_b", [1, D])
        eta = M.sb("eta", [P, 1])
        zeroed, iotas, loaded = M.sem("zeroed"), M.sem("iotas"), M.sem("loaded")
        chain, ident_ready = M.sem("chain"), M.sem("ident_ready")
        turned, turned_out, folded, folded_out = M.sem("turned"), M.sem("turned_out"), M.sem("folded"), M.sem("folded_out")
        loads = [0]
        block = ctx.enter_context(nc.Block())

        @block.sync
        def _(sp):
            def load(out, in_):
                loads[0] += 16
                sp.dma_start(out, in_).then_inc(loaded, 16)

            row = lambda v: v.rearrange("(a d) -> a d", a=1)
            sp.wait_ge(zeroed, 1)
            for t, n in ((wq, "L0_gnn_Wq"), (wk, "L0_gnn_Wk"), (wv, "L0_gnn_Wv"), (wo, "L0_gnn_Wo"), (w1, "L1_gnn_W"),
                         (gin1, "L2_gnn_W1"), (gin2, "L2_gnn_W2")):
                load(t[:, :], W[n])
            for h in range(HEADS):
                for j, n in enumerate(("L1_gnn_att_src", "L1_gnn_att_dst")):
                    load(att[h * HC:(h + 1) * HC, j * HEADS + h:j * HEADS + h + 1],
                         W[n][h:h + 1, :].rearrange("a c -> c a"))
            with sp.Fori(0, g.blocks - 1) as b:
                sp.dma_start(K.x[:, bass.ds(b, 1), :].rearrange("p a d -> p (a d)"),
                             W["x"][bass.ds(b * P, P), :]).then_inc(loaded, 16)
            loads[0] += 16 * (g.blocks - 1)
            load(K.x[0:g.tail, g.blocks - 1, :], W["x"][(g.blocks - 1) * P:g.nodes, :])
            load(K.w1[:, ROW1 + HEADS:], W["L1_gnn_skip_W"])
            load(K.b0[:, :], row(W["L0_gnn_bo"]))
            load(K.b1[:, ROW1 + HEADS:], row(W["L1_gnn_gat_bias"]))
            load(skip_b[:, :], row(W["L1_gnn_skip_b"]))
            load(K.gin_b1[:, :], W["L2_gnn_b1"].rearrange("(d a) -> d a", a=1))
            load(K.gin_b2[:, :], row(W["L2_gnn_b2"]))
            load(eta[:, :], W["L2_gnn_eta"].broadcast_to([P, 1]))
            for t, n in zip(K.affine, ("L0_gnn_gamma", "L0_gnn_beta", "L1_gnn_ln_g", "L1_gnn_ln_b", "L2_gnn_ln_gamma",
                                       "L2_gnn_ln_beta")):
                load(t[:, :], row(W[n]).broadcast_to([P, D]))
            load(K.rel_b1[:, :], row(W["L3_gnn_b1"]).broadcast_to([P, D]))
            load(K.rel_b2[:, :], row(W["L3_gnn_b2"]))
            for t, n, m in ((K.rel_w[0], "L3_gnn_w1", "L3_gnn_sw1"), (K.rel_w[1], "L3_gnn_w2", "L3_gnn_sw2")):
                load(t[:, 0:REL, :], W[n].rearrange("r c o -> c r o"))
                load(t[:, REL, :], W[m])

        @block.gpsimd
        def _(pool):
            nc.gpsimd.iota(part_no[:, :], [[0, 1]], base=0, channel_multiplier=1).then_inc(iotas, 1)
            nc.gpsimd.iota(col_no[:, :], [[1, P]], base=0, channel_multiplier=0).then_inc(iotas, 1)

        @block.vector
        def _(dve):
            nc.vector.memset(K.x[:, g.blocks - 1, :], 0.0)
            nc.vector.memset(K.w1[:, :], 0.0)
            nc.vector.memset(K.b1[:, :], 0.0).then_inc(chain, 1)
            nc.vector.memset(K.ones[:, :], 1.0)
            nc.vector.memset(K.eps[:, :], LN_EPS)
            dve.wait_ge(chain, 1)
            nc.vector.memset(K.b1[:, 0:HEADS * HZ].rearrange("p (h z) -> p h z", h=HEADS)[:, :, HC], 1.0)
            nc.vector.memset(att[:, :], 0.0).then_inc(zeroed, 1)
            dve.wait_ge(iotas, 2)
            nc.vector.tensor_copy(K.col[:, :], col_no[:, :])
            nc.vector.tensor_copy(K.part[:, :], part_no[:, :]).then_inc(chain, 1)
            dve.wait_ge(chain, 2)
            nc.vector.tensor_scalar(K.ident[:, :], K.col[:, :], K.part[:, :], None,
                                    ALU.is_equal).then_inc(ident_ready, 1)
            nc.vector.tensor_scalar(K.ident_b[:, :], K.col[:, :], K.part[:, :], None, ALU.is_equal)
            dve.wait_ge(loaded, loads[0])
            nc.vector.tensor_copy(K.w1[:, 0:HEADS * HZ].rearrange("p (h z) -> p h z", h=HEADS)[:, :, 0:HC],
                                  w1[:, :].rearrange("p (h c) -> p h c", h=HEADS))
            nc.vector.tensor_tensor(K.b1[:, ROW1 + HEADS:], K.b1[:, ROW1 + HEADS:], skip_b[:, :], ALU.add)
            nc.vector.tensor_scalar(K.eta1[:, :], eta[:, :], 1.0, None, ALU.add)
            dve.wait_ge(turned, 1)
            for j, t in enumerate((wo_t, w1_t, K.gin_w1, K.gin_w2)):
                last = nc.vector.tensor_copy(t[:, :], K.bank[0][:, j * P:(j + 1) * P])
            last.then_inc(turned_out, 1)
            dve.wait_ge(folded, 1)
            nc.vector.tensor_scalar(K.qk[:, :], K.bank[1][:, 0:P], float(D) ** -0.5, None, ALU.mult)
            nc.vector.tensor_copy(K.vo[:, :], K.bank[1][:, P:2 * P])
            nc.vector.tensor_copy(K.w1[:, ROW1 - HEADS:ROW1 + HEADS],
                                  K.bank[1][:, 2 * P:2 * P + 2 * HEADS]).then_inc(folded_out, 1)

        @block.tensor
        def _(pe):
            pe.wait_ge(loaded, loads[0])
            pe.wait_ge(ident_ready, 1)
            for j, t in enumerate((wo, w1, gin1, gin2)):
                last = nc.tensor.transpose(K.bank[0][:, j * P:(j + 1) * P], t[:, :], K.ident[:, :])
            last.then_inc(turned, 1)
            nc.tensor.matmul(K.bank[1][:, 0:P], wq[:, :], wk[:, :], start=True, stop=True)
            pe.wait_ge(turned_out, 1)
            nc.tensor.matmul(K.bank[1][:, P:2 * P], wv[:, :], wo_t[:, :], start=True, stop=True)
            nc.tensor.matmul(K.bank[1][:, 2 * P:2 * P + 2 * HEADS], w1_t[:, :], att[:, :], start=True,
                             stop=True).then_inc(folded, 1)


def query_rows(nc, g, K):
    with ExitStack() as ctx:
        M = Memory(nc, ctx, K, "query")
        x_t = M.sb("x_t", [P, RING, P])
        x_u = M.sb("x_u", [P, RING, P])
        brought, taken = M.sem("brought"), M.sem("taken")
        turned, turned_out, made, made_out = M.sem("turned"), M.sem("turned_out"), M.sem("made"), M.sem("made_out")
        block = ctx.enter_context(nc.Block())

        @block.gpsimd
        def _(pool):
            def bring(u):
                after(pool, turned, u, RING)
                pool.sem_inc(taken, 1)
                nc.gpsimd.tensor_copy(x_u[:, u.s, :], blk(K.x, u, D)).then_inc(brought, 1)

            pipeline(pool, g.blocks, RING, 0, stages(g.blocks, (0, bring)))

        @block.tensor
        def _(pe):
            def turn(u):
                after(pe, turned_out, u, 2)
                after(pe, brought, u)
                nc.tensor.transpose(K.bank[u.s % 2][:, 0:P], x_u[:, u.s, :], K.ident[:, :]).then_inc(turned, 1)

            def make(u):
                after(pe, turned_out, u)
                after(pe, made_out, u, 2)
                nc.tensor.matmul(K.bank[2 + u.s % 2][:, 0:P], x_t[:, u.s, :], K.qk[:, :], start=True,
                                 stop=True).then_inc(made, 1)

            pipeline(pe, g.blocks, RING, 1, stages(g.blocks, (0, turn), (1, make)))

        @block.scalar
        def _(act):
            def copy(u):
                after(act, turned, u)
                after(act, made, u, RING)
                nc.scalar.copy(x_t[:, u.s, :], K.bank[u.s % 2][:, 0:P]).then_inc(turned_out, 1)

            pipeline(act, g.blocks, RING, 0, stages(g.blocks, (0, copy)))

        @block.vector
        def _(dve):
            def copy(u):
                after(dve, made, u)
                nc.vector.tensor_copy(blk(K.own, u, D), K.bank[2 + u.s % 2][:, 0:P]).then_inc(made_out, 1)

            pipeline(dve, g.blocks, RING, 0, stages(g.blocks, (0, copy)))


def blk(t, u, n, start=0):
    return t[:, bass.ds(u.at(), 1), start:start + n].rearrange("p a d -> p (a d)")


def block_numbers(nc, engine, K, g, u):
    return nc.values_load_multi_w_load_instructions(
        K.block_no[0:1, bass.ds(u.at(UNIT), UNIT)], engines=(engine,), min_val=0, max_val=g.blocks - 1,
        skip_runtime_bounds_check_because="items are numbered within the blocks")[1]


def at_block(t, b, n, start=0):
    return t[:, bass.ds(b, 1), start:start + n].rearrange("p a d -> p (a d)")


def stage_rows(nc, act, K, g, index, staged, gathered):
    def stage(u):
        after_gather(act, gathered, u, u.per)
        nc.scalar.copy(K.rows[:, u.s, :], index[:, bass.ds(u.at(UNIT), UNIT)]).then_inc(staged, 1)
    return stage


def after_gather(eng, gathered, u, back=0):
    v = u.back(back)
    value = v.i * (16 * UNIT) + 16 * UNIT
    if isinstance(value, int) and value <= 0:
        return
    eng.wait_ge(gathered[u.s], value)


def gather_rows(nc, pool, K, g, table, width, staged, gathered, used, opened):
    def gather(u):
        after(pool, staged, u)
        after(pool, used, u, u.per)
        pool.sem_inc(opened, 1)
        for k in range(UNIT):
            pool.indirect_dma_start(out=K.ring[:, u.s * UNIT + k, 0:width], out_offset=None, in_=table,
                                    in_offset=bass.IndirectOffsetOnAxis(ap=K.rows[:, u.s, k:k + 1], axis=0),
                                    ).then_inc(gathered[u.s], 16)
    return gather


def member(nc, K, u, out=None):
    shape = [P, UNIT, P]
    return nc.vector.tensor_tensor(K.member[:, u.s % RING, :, :] if out is None else out, bcast(K.col[:, :], 1, UNIT),
                                   K.node[:, bass.ds(u.at(UNIT), UNIT)].unsqueeze(2).broadcast_to(shape), ALU.is_equal)


def attention_items(nc, g, K, x_table):
    with ExitStack() as ctx:
        M = Memory(nc, ctx, K, "attn")
        gathered = [M.sem(f"gathered{s}") for s in range(RING)]
        staged, member_ready, turned, turned_out = (M.sem(n) for n in ("staged", "member", "turned", "turned_out"))
        query_ready, product_ready, logit_ready, gate_ready = (M.sem(n) for n in ("query", "product", "logit", "gate"))
        gated_ready, summed, added, cleared = (M.sem(n) for n in ("gated", "summed", "added", "cleared"))
        member_b = M.sb("member_b", [P, RING, UNIT, P], BF16)
        member_t = M.sb("member_t", [P, 2, UNIT, P])
        product = M.sb("product", [P, UNIT, P])
        logit, gate = M.sb("logit", [P, 2, UNIT]), M.sb("gate", [P, 2, UNIT])
        gated = M.sb("gated", [P, 2, UNIT, P])
        view = lambda bank: bank[:, :].rearrange("p (k d) -> p k d", k=UNIT)
        turned_view = lambda u: K.bank[u.s % 2][:, :].bitcast(BF16)[:, 0:UNIT * P].rearrange("p (k d) -> p k d", k=UNIT)
        bank_q, bank_s = K.bank[2:4], K.bank[4:6]
        N = g.units
        opened = M.sem("opened")
        block = ctx.enter_context(nc.Block())

        @block.gpsimd
        def _(pool):
            pipeline(pool, N, RING, 0, stages(N, (0, gather_rows(nc, pool, K, g, x_table, D, staged, gathered, summed,
                                                                 opened))))

        @block.scalar
        def _(act):
            def copy_turned(u):
                after(act, turned, u)
                after(act, query_ready, u, 2)
                nc.scalar.copy(member_t[:, u.s % 2, :, :], turned_view(u)).then_inc(turned_out, 1)

            def sigmoid(u):
                after(act, logit_ready, u)
                after(act, gated_ready, u, 2)
                nc.scalar.activation(gate[:, u.s % 2, :], logit[:, u.s % 2, :], ACT.Sigmoid).then_inc(gate_ready, 1)

            pipeline(act, N, RING, 3, stages(N, (0, stage_rows(nc, act, K, g, K.src_row, staged, gathered)),
                                             (2, copy_turned), (3, sigmoid)))

        @block.vector
        def _(dve):
            nc.vector.memset(K.acc[:, :, :], 0.0).then_inc(cleared, 1)

            def members(u):
                after(dve, turned, u, RING)
                after(dve, gated_ready, u, RING)
                member(nc, K, u, member_b[:, u.s, :, :]).then_inc(member_ready, 1)

            def products(u):
                after(dve, query_ready, u)
                after_gather(dve, gathered, u)
                after(dve, logit_ready, u, 1)
                nc.vector.tensor_tensor(product[:, :, :], view(bank_q[u.s % 2]),
                                        K.ring[:, u.s * UNIT:(u.s + 1) * UNIT, 0:D], ALU.mult).then_inc(product_ready, 1)

            def logits(u):
                after(dve, product_ready, u)
                after(dve, gate_ready, u, 2)
                nc.vector.tensor_reduce(logit[:, u.s % 2, :], product[:, :, :], AX.X, ALU.add).then_inc(logit_ready, 1)

            def gates(u):
                after(dve, gate_ready, u)
                after(dve, summed, u, 2)
                nc.vector.tensor_tensor(gated[:, u.s % 2, :, :], member_b[:, u.s, :, :],
                                        gate[:, u.s % 2, :].unsqueeze(2).broadcast_to([P, UNIT, P]),
                                        ALU.mult).then_inc(gated_ready, 1)

            dve.wait_ge(cleared, 1)
            add = add_sums(nc, dve, K, g, summed, added, bank_s)
            pipeline(dve, N, RING, 4, stages(N, (4, add(0)), (0, members), (4, add(1)), (2, products), (4, add(2)),
                                             (2, logits), (4, add(3)), (2, gates)))

        @block.tensor
        def _(pe):
            def turn(u):
                after(pe, member_ready, u)
                after(pe, turned_out, u, 2)
                for k in range(UNIT):
                    last = nc.tensor.transpose(turned_view(u)[:, k, :], member_b[:, u.s, k, :], K.ident_b[:, :])
                last.then_inc(turned, 1)

            def queries(u):
                b = block_numbers(nc, mybir.EngineType.PE, K, g, u)
                after(pe, turned_out, u)
                after(pe, product_ready, u, 2)
                for k in range(UNIT):
                    last = nc.tensor.matmul(bank_q[u.s % 2][:, k * P:(k + 1) * P], member_t[:, u.s % 2, k, :],
                                            at_block(K.own, b[k], D), start=True, stop=True)
                last.then_inc(query_ready, 1)

            def sums(u):
                after(pe, gated_ready, u)
                after(pe, added, u, 2, per=UNIT)
                for k in range(UNIT):
                    last = nc.tensor.matmul(bank_s[u.s % 2][:, k * P:(k + 1) * P], gated[:, u.s % 2, k, :],
                                            K.ring[:, u.s * UNIT + k, 0:D], start=True, stop=True)
                last.then_inc(summed, 1)

            pipeline(pe, N, RING, 3, stages(N, (0, turn), (1, queries), (3, sums)))


def add_sums(nc, dve, K, g, summed, added, banks):
    registers = {}

    def add(k):
        def stage(u):
            if k == 0:
                registers[0] = block_numbers(nc, mybir.EngineType.DVE, K, g, u)
                after(dve, summed, u)
                after(dve, added, u, 1, per=UNIT)
            else:
                after(dve, added, u, per=UNIT, upto=k)
            into = at_block(K.acc, registers[0][k], D)
            nc.vector.tensor_tensor(into, into, banks[u.s % 2][:, k * P:(k + 1) * P], ALU.add).then_inc(added, 1)
        return stage
    return add


def sum_items(nc, g, K, name, table, index):
    with ExitStack() as ctx:
        M = Memory(nc, ctx, K, name)
        gathered = [M.sem(f"gathered{s}") for s in range(RING)]
        staged, member_ready, summed, added, cleared = (M.sem(n) for n in ("staged", "member", "summed", "added", "cleared"))
        banks = K.bank[0:2]
        N = g.units
        opened = M.sem("opened")
        block = ctx.enter_context(nc.Block())

        @block.gpsimd
        def _(pool):
            pipeline(pool, N, RING, 0, stages(N, (0, gather_rows(nc, pool, K, g, table, D, staged, gathered, summed,
                                                                 opened))))

        @block.scalar
        def _(act):
            pipeline(act, N, RING, 0, stages(N, (0, stage_rows(nc, act, K, g, index, staged, gathered))))

        @block.vector
        def _(dve):
            nc.vector.memset(K.acc[:, :, :], 0.0).then_inc(cleared, 1)

            def members(u):
                after(dve, summed, u, RING)
                member(nc, K, u).then_inc(member_ready, 1)

            dve.wait_ge(cleared, 1)
            add = add_sums(nc, dve, K, g, summed, added, banks)
            pipeline(dve, N, RING, 1, stages(N, (0, members), *((1, add(k)) for k in range(UNIT))))

        @block.tensor
        def _(pe):
            def sums(u):
                after(pe, member_ready, u)
                after_gather(pe, gathered, u)
                after(pe, added, u, 2, per=UNIT)
                for k in range(UNIT):
                    last = nc.tensor.matmul(banks[u.s % 2][:, k * P:(k + 1) * P], K.member[:, u.s, k, :],
                                            K.ring[:, u.s * UNIT + k, 0:D], start=True, stop=True)
                last.then_inc(summed, 1)

            pipeline(pe, N, RING, 0, stages(N, (0, sums)))


def softmax_items(nc, g, K, table):
    with ExitStack() as ctx:
        M = Memory(nc, ctx, K, "soft")
        N, R = g.units, LONG_RING
        C, W = UNIT * HEADS, HEADS * HZ
        gathered = [M.sem(f"gathered{s}") for s in range(R)]
        opened, taken = M.sem("opened"), M.sem("taken")
        staged, begun, scores_ready, starts_out, own_ready, turned_out, exp_ready = (
            M.sem(n) for n in ("staged", "begun", "scores", "starts_out", "own", "turned_out", "exp"))
        scores_turned, turned, run_back, tops_ready, picked, summed = (
            M.sem(n) for n in ("scores_turned", "turned", "run_back", "tops", "picked", "summed"))
        member_ready, run_ready, ends_ready, chain, max_ready, node_ready, edge_chain, over_ready = (
            M.sem(n) for n in ("member", "run_max", "ends", "chain", "max", "node", "edge_chain", "over"))
        message_ready, added, cleared = M.sem("message"), M.sem("added"), M.sem("cleared")
        bound_ready, leaky_ready, narrowed = M.sem("bound"), M.sem("leaky"), M.sem("narrowed")
        member_b = M.sb("member_b", [P, 2, UNIT, P], BF16)
        member_t = M.sb("member_t", [P, 2, UNIT, P])
        start_u = M.sb("start_u", [P, R, C])
        score_u = M.sb("score_u", [P, 2, C])
        starts_t = M.sb("starts_t", [C, 2, P])
        run_max = M.sb("run_max", [C, 2, P])
        run_end = M.sb("run_end", [P, 2, UNIT, HEADS + 1])
        absent = M.sb("absent", [P, UNIT])
        tops = M.sb("tops", [P, HEADS, UNIT + 1])
        peak = M.sb("peak", [P, 2, HEADS, UNIT + 1])
        old = M.sb("old", [P, HEADS, UNIT])
        node_u = M.sb("node_u", [P, RING, UNIT, 3, HEADS])
        edge_ad = M.sb("edge_ad", [P, UNIT, HEADS])
        both = M.sb("both", [P, 2, 2, 2, C])
        leaky = M.sb("leaky", [P, 2, 2, C])
        over = M.sb("over", [P, 2, 2, C])
        power = M.sb("power", [P, 2, 2, C])
        message = M.sb("message", [P, 2, UNIT, W])
        scaled = M.sb("scaled", [P, W])
        RUN, TOP, EDGE = 2 * P, 2 * P + C, 2 * P + C + UNIT * (HEADS + 1)
        small = lambda u: K.bank[4 + u.s % RING]
        turned_view = K.bank[0][:, :].bitcast(BF16)[:, 0:UNIT * P].rearrange("p (k d) -> p k d", k=UNIT)
        sum_of = lambda k: K.bank[1 + k // 3][:, (k % 3) * W:(k % 3 + 1) * W]
        top_of = lambda u: small(u)[:, TOP:EDGE].rearrange("p (k h) -> p k h", h=HEADS + 1)
        edge_of = lambda u: small(u)[:, EDGE:EDGE + 3 * C].rearrange("p (k j h) -> p k j h", k=UNIT, j=3)
        by_kh = lambda a: a.rearrange("p (k h) -> p k h", h=HEADS)
        by_hk = lambda a: a.rearrange("p (h k) -> p h k", h=HEADS)
        rows_of = lambda u, c0, c1: K.ring[:, u.s * UNIT:(u.s + 1) * UNIT, c0:c1]
        block = ctx.enter_context(nc.Block())

        @block.gpsimd
        def _(pool):
            pipeline(pool, N, R, 0, stages(N, (0, gather_rows(nc, pool, K, g, table, ROW1, staged, gathered,
                                                              message_ready, opened))))

        @block.scalar
        def _(act):
            rows = stage_rows(nc, act, K, g, K.src_row, staged, gathered)

            def inputs(u):
                rows(u)
                after(act, scores_turned, u, R)
                nc.scalar.copy(by_kh(start_u[:, u.s, :]), K.starts[:, bass.ds(u.at(UNIT), UNIT)].unsqueeze(2)
                               .broadcast_to([P, UNIT, HEADS])).then_inc(begun, 1)

            def copy_scores(u):
                after_gather(act, gathered, u)
                after(act, scores_turned, u, 2)
                nc.scalar.copy(by_kh(score_u[:, u.s % 2, :]), rows_of(u, W, W + HEADS)).then_inc(scores_ready, 1)

            def copy_own(u):
                b = block_numbers(nc, mybir.EngineType.Activation, K, g, u)
                after(act, picked, u, RING)
                for k in range(UNIT):
                    last = nc.scalar.copy(node_u[:, u.s % RING, k, 0:2, :].rearrange("p j h -> p (j h)"),
                                          at_block(K.own, b[k], 2 * HEADS))
                last.then_inc(own_ready, 1)

            def copy_starts(u):
                after(act, scores_turned, u)
                after(act, run_ready, u, 2)
                nc.scalar.copy(starts_t[:, u.s % 2, :], small(u)[0:C, P:2 * P]).then_inc(starts_out, 1)

            def copy_turned(u):
                after(act, turned, u)
                after(act, picked, u, 2)
                nc.scalar.copy(member_t[:, u.s % 2, :, :], turned_view).then_inc(turned_out, 1)

            def narrow(u):
                after(act, member_ready, u)
                after(act, turned, u, 2)
                nc.scalar.copy(member_b[:, u.s % 2, :, :], K.member[:, u.s % RING, :, :]).then_inc(narrowed, 1)

            def exponent(u):
                after(act, over_ready, u)
                after(act, added, u, 2, per=2 * UNIT)
                nc.scalar.activation(power[:, u.s % 2, :, :], over[:, u.s % 2, :, :], ACT.Exp).then_inc(exp_ready, 1)

            pipeline(act, N, R, 6, stages(N, (3, copy_scores), (3, copy_own), (3, copy_starts), (3, copy_turned),
                                          (5, exponent), (2, narrow), (0, inputs)))

        @block.tensor
        def _(pe):
            def turn_scores(u):
                after(pe, scores_ready, u)
                after(pe, begun, u)
                after(pe, over_ready, u, RING)
                nc.tensor.transpose(small(u)[0:C, 0:P], score_u[:, u.s % 2, :], K.ident[:, :])
                nc.tensor.transpose(small(u)[0:C, P:2 * P], start_u[:, u.s, :],
                                    K.ident[:, :]).then_inc(scores_turned, 1)

            def turn_runs(u):
                after(pe, run_ready, u)
                pe.sem_inc(taken, 1)
                nc.tensor.transpose(small(u)[:, RUN:TOP], run_max[:, u.s % 2, :],
                                    K.ident[0:C, 0:C]).then_inc(run_back, 1)

            def item_tops(u):
                after(pe, ends_ready, u, per=2)
                after(pe, member_ready, u)
                for k in range(UNIT):
                    last = nc.tensor.matmul(top_of(u)[:, k, :], K.member[:, u.s % RING, k, :],
                                            run_end[:, u.s % 2, k, :], start=True, stop=True)
                last.then_inc(tops_ready, 1)

            def pick(u):
                after(pe, max_ready, u, per=2)
                after(pe, turned_out, u)
                for k in range(UNIT):
                    last = nc.tensor.matmul(edge_of(u)[:, k, :, :], member_t[:, u.s % 2, k, :],
                                            node_u[:, u.s % RING, k, :, :], start=True, stop=True)
                last.then_inc(picked, 1)

            def turn(u):
                after(pe, narrowed, u)
                after(pe, turned_out, u, 1)
                for k in range(UNIT):
                    last = nc.tensor.transpose(turned_view[:, k, :], member_b[:, u.s % 2, k, :], K.ident_b[:, :])
                last.then_inc(turned, 1)

            def sums(u):
                after(pe, message_ready, u)
                after(pe, added, u, 1, per=2 * UNIT)
                for k in range(UNIT):
                    last = nc.tensor.matmul(sum_of(k), K.member[:, u.s % RING, k, :], message[:, u.s % 2, k, :],
                                            start=True, stop=True)
                last.then_inc(summed, 1)

            pipeline(pe, N, R, 4, stages(N, (1, turn_scores), (4, sums), (2, pick), (1, turn_runs), (1, item_tops),
                                         (0, turn)))

        @block.vector
        def _(dve):
            def run_maxima(u):
                after(dve, starts_out, u)
                after(dve, run_back, u, 2)
                nc.vector.tensor_tensor_scan(run_max[:, u.s % 2, :], starts_t[:, u.s % 2, :], small(u)[0:C, 0:P],
                                             -FAR, ALU.add, ALU.max).then_inc(run_ready, 1)

            def run_ends(u):
                ends = K.ends[:, bass.ds(u.at(UNIT), UNIT)]
                after(dve, tops_ready, u, 2)
                nc.vector.tensor_copy(run_end[:, u.s % 2, :, HEADS], ends).then_inc(ends_ready, 1)
                after(dve, run_back, u)
                nc.vector.tensor_tensor(run_end[:, u.s % 2, :, 0:HEADS], by_kh(small(u)[:, RUN:TOP]),
                                        ends.unsqueeze(2).broadcast_to([P, UNIT, HEADS]),
                                        ALU.mult).then_inc(ends_ready, 1)

            def new_maxima(u):
                own = node_u[:, u.s % RING, :, :, :]
                cut = K.cut[:, bass.ds(u.at(), 1), :]
                after(dve, tops_ready, u)
                nc.vector.tensor_scalar(absent[:, :], top_of(u)[:, :, HEADS], FAR, -FAR, ALU.mult,
                                        ALU.add).then_inc(chain, 1)
                nc.vector.tensor_copy(tops[:, :, 0], peak[:, 1 - u.s % 2, :, UNIT]).then_inc(chain, 1)
                after(dve, chain, u, per=6, upto=1)
                nc.vector.tensor_tensor(tops[:, :, 1:UNIT + 1], top_of(u)[:, :, 0:HEADS].rearrange("p k h -> p h k"),
                                        bcast(absent[:, :], 1, HEADS), ALU.add).then_inc(chain, 1)
                after(dve, own_ready, u)
                after(dve, chain, u, per=6, upto=3)
                nc.vector.tensor_tensor(tops[:, :, 1:UNIT + 1], tops[:, :, 1:UNIT + 1],
                                        own[:, :, 0, :].rearrange("p k h -> p h k"), ALU.max).then_inc(chain, 1)
                after(dve, chain, u, per=6, upto=4)
                nc.vector.tensor_tensor_scan(peak[:, u.s % 2, :, :].rearrange("p h k -> p (h k)"),
                                             cut.rearrange("p a c -> p (a c)"),
                                             tops[:, :, :].rearrange("p h k -> p (h k)"), -FAR, ALU.add,
                                             ALU.max).then_inc(max_ready, 1)
                after(dve, max_ready, u, per=2, upto=1)
                nc.vector.tensor_copy(own[:, :, 2, :].rearrange("p k h -> p h k"),
                                      peak[:, u.s % 2, :, 1:UNIT + 1]).then_inc(max_ready, 1)
                nc.vector.tensor_tensor(old[:, :, :], peak[:, u.s % 2, :, 0:UNIT],
                                        cut.rearrange("p a (h k) -> p (a h) k", h=HEADS)[:, :, 1:UNIT + 1],
                                        ALU.add).then_inc(chain, 1)
                ad = own[:, :, 1, :].rearrange("p k h -> p h k")
                after(dve, leaky_ready, u, 2)
                nc.vector.tensor_tensor(by_hk(both[:, u.s % 2, 0, 1, :]), peak[:, u.s % 2, :, 1:UNIT + 1], ad,
                                        ALU.add).then_inc(node_ready, 1)
                after(dve, chain, u, per=6, upto=5)
                nc.vector.tensor_tensor(old[:, :, :], old[:, :, :], own[:, :, 0, :].rearrange("p k h -> p h k"),
                                        ALU.max).then_inc(chain, 1)
                after(dve, chain, u, per=6)
                nc.vector.tensor_tensor(by_hk(both[:, u.s % 2, 0, 0, :]), old[:, :, :], ad, ALU.add).then_inc(node_ready, 1)

            def edge_values(u):
                after(dve, picked, u)
                edge = edge_of(u)
                nc.vector.tensor_copy(edge_ad[:, :, :], edge[:, :, 1, :]).then_inc(edge_chain, 1)
                after(dve, edge_chain, u, per=3, upto=1)
                nc.vector.tensor_tensor(by_kh(both[:, u.s % 2, 1, 1, :]), edge[:, :, 2, :], edge_ad[:, :, :],
                                        ALU.add).then_inc(edge_chain, 1)
                nc.vector.tensor_tensor(by_kh(both[:, u.s % 2, 1, 0, :]), rows_of(u, W, W + HEADS), edge_ad[:, :, :],
                                        ALU.add).then_inc(edge_chain, 1)

            def edge_bound(u):
                after(dve, edge_chain, u, per=3)
                nc.vector.tensor_tensor(both[:, u.s % 2, 1, 0, :], both[:, u.s % 2, 1, 0, :], both[:, u.s % 2, 1, 1, :],
                                        ALU.min).then_inc(bound_ready, 1)

            def edge_leaky(u):
                after(dve, bound_ready, u)
                after(dve, node_ready, u, per=2)
                nc.vector.scalar_tensor_tensor(leaky[:, :, :, :], both[:, u.s % 2, :, :, :], SLOPE,
                                               both[:, u.s % 2, :, :, :], ALU.mult, ALU.max).then_inc(leaky_ready, 1)

            def overs(u):
                after(dve, leaky_ready, u)
                after(dve, exp_ready, u, 2)
                nc.vector.tensor_tensor(over[:, u.s % 2, :, :], leaky[:, :, 0, :], leaky[:, :, 1, :],
                                        ALU.subtract).then_inc(over_ready, 1)

            def messages(u):
                after(dve, exp_ready, u)
                after(dve, summed, u, 2)
                nc.vector.tensor_tensor(
                    message[:, u.s % 2, :, :].rearrange("p k (h z) -> p k h z", h=HEADS),
                    rows_of(u, 0, W).rearrange("p k (h z) -> p k h z", h=HEADS),
                    by_kh(power[:, u.s % 2, 1, :]).unsqueeze(3).broadcast_to([P, UNIT, HEADS, HZ]),
                    ALU.mult).then_inc(message_ready, 1)

            registers = {}

            def rescale(k):
                def stage(u):
                    if k == 0:
                        registers[0] = block_numbers(nc, mybir.EngineType.DVE, K, g, u)
                        after(dve, added, u, 1, per=2 * UNIT)
                        after(dve, exp_ready, u)
                    else:
                        after(dve, added, u, per=2 * UNIT, upto=2 * k)
                    heads = lambda a: a.rearrange("p (h z) -> p h z", h=HEADS)
                    nc.vector.tensor_tensor(heads(scaled[:, :]), heads(at_block(K.acc, registers[0][k], W)),
                                            by_hk(power[:, u.s % 2, 0, :])[:, :, k].unsqueeze(2)
                                            .broadcast_to([P, HEADS, HZ]), ALU.mult).then_inc(added, 1)
                return stage

            def add(k):
                def stage(u):
                    if k == 0:
                        after(dve, summed, u)
                    after(dve, added, u, per=2 * UNIT, upto=2 * k + 1)
                    nc.vector.tensor_tensor(at_block(K.acc, registers[0][k], W), scaled[:, :], sum_of(k),
                                            ALU.add).then_inc(added, 1)
                return stage

            def members(u):
                after(dve, summed, u, RING)
                member(nc, K, u).then_inc(member_ready, 1)

            nc.vector.memset(peak[:, 1, :, :], -FAR).then_inc(cleared, 1)
            dve.wait_ge(cleared, 1)
            pipeline(dve, N, R, 4, stages(
                N, (2, new_maxima), (3, edge_values), (1, run_maxima), (4, rescale(0)), (3, edge_bound), (4, add(0)),
                (3, edge_leaky), (1, run_ends), (4, rescale(1)), (3, overs), (4, add(1)), (0, members),
                (4, rescale(2)), (3, messages), (4, add(2)), (4, rescale(3)), (4, add(3))))


ATTENTION, SOFTMAX, GIN, RELATIONS, LAST = range(5)


def node_pass(nc, g, K, kind, name, table, affine=None):
    with ExitStack() as ctx:
        M = Memory(nc, ctx, K, name)
        N = g.blocks
        inner = kind in (ATTENTION, GIN)
        tables = kind in (ATTENTION, GIN, RELATIONS)
        first = kind in (ATTENTION, SOFTMAX, GIN)
        second = kind != RELATIONS
        rel_w = K.rel_w[0 if kind == GIN else 1]
        width = ROW1 if kind == ATTENTION else REL * D
        S = {n: M.sem(n) for n in ("input", "turned", "turned_out", "product", "hidden", "product2", "layer", "stats1",
                                   "root1", "norm1", "joined", "stats2", "root2", "norm2", "row_turned",
                                   "row_turned_out", "rows", "rows_act", "rows_dve", "kept",
                                   "begun")
             if not (n.endswith("1") and not first)}
        stored = [M.sem("stored0"), M.sem("stored1")]
        taken, taken_pool, taken_sp = M.sem("taken"), M.sem("taken_pool"), M.sem("taken_sp")
        joins = {ATTENTION: 3, SOFTMAX: 3, GIN: 4}.get(kind, 1)
        row_stored = [M.sem(f"row_stored{s}") for s in range(RING)] if kind in (LAST, SOFTMAX) else None
        uses = lambda u: u.i * 2 + u.s // 2
        z_in = M.sb("z_in", [P, RING, D])
        z_t = M.sb("z_t", [P, 2, D])
        hidden = M.sb("hidden", [P, 2, D])
        layer = M.sb("layer", [P, RING, D])
        norm = M.sb("norm", [P, RING, D])
        joined = M.sb("joined", [P, RING, D])
        fresh = M.sb("fresh", [P, RING, D])
        stats = [M.sb(f"stats{j}", [P, RING, 6]) for j in range(2)]
        moments = [M.sb(f"moments{j}", [P, RING, 2]) for j in range(2)]
        root = [M.sb(f"root{j}", [P, RING, 1]) for j in range(2)]
        scale = [M.sb(f"scale{j}", [P, RING, 1]) for j in range(2)]
        inv_z = M.sb("inv_z", [P, RING, 2, HEADS])
        x_t = M.sb("x_t", [P, 2, D])
        rows = M.sb("rows", [P, 2, width])
        block = ctx.enter_context(nc.Block())

        def after_stored(eng, u):
            value = uses(u) * 16
            if not (isinstance(value, int) and value <= 0):
                eng.wait_ge(stored[u.s % 2], value)

        def moments_of(dve, j, src, u):
            sem = S[f"stats{j + 1}"]
            after(dve, S[f"norm{j + 1}"], u, RING, per=2)
            after(dve, S[f"root{j + 1}"], u, RING)
            nc.vector.bn_stats(stats[j][:, u.s, :], src).then_inc(sem, 1)
            after(dve, sem, u, per=2, upto=1)
            dve.sem_inc(taken, 1)
            nc.vector.bn_aggr(moments[j][:, u.s, :], stats[j][:, u.s, :]).then_inc(sem, 1)

        def root_of(act, j, u):
            after(act, S[f"stats{j + 1}"], u, per=2)
            after(act, S[f"norm{j + 1}"], u, RING, per=2)
            nc.scalar.activation(root[j][:, u.s, :], moments[j][:, u.s, 1:2], ACT.Sqrt,
                                 bias=K.eps[:, :]).then_inc(S[f"root{j + 1}"], 1)

        def normalize(dve, j, out, src, u):
            sem = S[f"norm{j + 1}"]
            after(dve, S[f"root{j + 1}"], u)
            nc.vector.reciprocal(scale[j][:, u.s, :], root[j][:, u.s, :]).then_inc(sem, 1)
            after(dve, sem, u, per=2, upto=1)
            nc.vector.tensor_scalar(out, src, moments[j][:, u.s, 0:1], scale[j][:, u.s, :], ALU.subtract,
                                    ALU.mult).then_inc(sem, 1)

        @block.vector
        def _(dve):
            def enter(u):
                if kind == GIN:
                    after(dve, S["turned"], u, RING)
                    nc.vector.scalar_tensor_tensor(z_in[:, u.s, :], blk(K.x, u, D), K.eta1[:, :], blk(K.acc, u, D),
                                                   ALU.mult, ALU.add).then_inc(S["input"], 1)
                if kind == SOFTMAX:
                    after(dve, S["layer"], u, RING, per=2)
                    z = K.acc[:, bass.ds(u.at(), 1), 0:HEADS * HZ].rearrange("p a (h z) -> p (a h) z", h=HEADS)[:, :, HC]
                    nc.vector.tensor_scalar(inv_z[:, u.s, 0, :], z, SOFTMAX_EPS, None, ALU.add).then_inc(S["input"], 1)
                    after(dve, S["input"], u, per=2, upto=1)
                    nc.vector.reciprocal(inv_z[:, u.s, 1, :], inv_z[:, u.s, 0, :]).then_inc(S["input"], 1)
                if kind == RELATIONS:
                    after(dve, S["layer"], u, RING)
                    nc.vector.tensor_tensor(joined[:, u.s, :], blk(K.acc, u, D), blk(K.own, u, D),
                                            ALU.add).then_inc(S["input"], 1)
                if kind == LAST:
                    after(dve, S["norm2"], u, RING, per=2)
                    nc.vector.tensor_tensor(joined[:, u.s, :], blk(K.acc, u, D), blk(K.own, u, D),
                                            ALU.add).then_inc(S["joined"], 1)

            def make_layer(u):
                if kind == ATTENTION:
                    after(dve, S["product"], u)
                    nc.vector.tensor_tensor(layer[:, u.s, :], K.bank[1 + u.s % 2][:, 0:D], blk(K.x, u, D),
                                            ALU.add).then_inc(S["layer"], 1)
                    after(dve, S["layer"], u)
                if kind == SOFTMAX:
                    after(dve, S["input"], u, per=2)
                    acc = K.acc[:, bass.ds(u.at(), 1), 0:HEADS * HZ].rearrange("p a (h z) -> p (a h) z", h=HEADS)
                    nc.vector.tensor_tensor(z_in[:, u.s, :].rearrange("p (h c) -> p h c", h=HEADS), acc[:, :, 0:HC],
                                            inv_z[:, u.s, 1, :].unsqueeze(2).broadcast_to([P, HEADS, HC]),
                                            ALU.mult).then_inc(S["layer"], 1)
                    after(dve, S["layer"], u, per=2, upto=1)
                    nc.vector.tensor_tensor(layer[:, u.s, :], z_in[:, u.s, :], blk(K.own, u, D, 2 * HEADS),
                                            ALU.add).then_inc(S["layer"], 1)
                    after(dve, S["layer"], u, per=2)
                if kind == GIN:
                    after(dve, S["layer"], u)
                if first:
                    moments_of(dve, 0, layer[:, u.s, :], u)
                if kind == RELATIONS:
                    after(dve, S["input"], u)
                    after(dve, S["row_turned"], u, RING)
                    nc.vector.scalar_tensor_tensor(z_in[:, u.s, :], joined[:, u.s, :], 0.0, K.rel_b1[:, :], ALU.max,
                                                   ALU.add).then_inc(S["layer"], 1)

            def norm_first(u):
                if first:
                    after(dve, S["joined"], u, RING, per=joins)
                    normalize(dve, 0, norm[:, u.s, :], layer[:, u.s, :], u)

            def stats_second(u):
                if second:
                    after(dve, S["joined"], u, per=joins)
                    moments_of(dve, 1, joined[:, u.s, :], u)

            def norm_second(u):
                if second:
                    if row_stored:
                        after_row_stored(dve, u)
                    if kind != LAST:
                        after(dve, S["kept"], u, RING)
                    if tables:
                        after(dve, S["row_turned"], u, RING)
                    if kind == GIN:
                        after(dve, S["rows_dve"], u, RING, per=2)
                    normalize(dve, 1, fresh[:, u.s, :], joined[:, u.s, :], u)

            def after_row_stored(eng, u):
                value = u.i * 16
                if not (isinstance(value, int) and value <= 0):
                    eng.wait_ge(row_stored[u.s], value)

            def copy_rows(u):
                if kind in (GIN, RELATIONS):
                    after(dve, S["rows"], u, per=3)
                    after_stored(dve, u)
                    nc.vector.tensor_copy(rows[:, u.s % 2, 4 * D:8 * D], K.bank[5][:, :]).then_inc(S["rows_dve"], 1)
                    nc.vector.tensor_tensor(blk(K.own, u, D), K.bank[6 + u.s % 2][:, 0:D],
                                            fresh[:, u.s, :] if kind == GIN else blk(K.x, u, D),
                                            ALU.add).then_inc(S["rows_dve"], 1)

            pipeline(dve, N, RING, 4, stages(N, (0, enter), (3, stats_second), (2, make_layer), (3, norm_second),
                                             (2, norm_first), (4, copy_rows)))


        @block.gpsimd
        def _(pool):
            def join(u):
                j = S["joined"]
                after(pool, S["norm1"], u, per=2)
                after(pool, S["stats2"], u, RING, per=2)
                after(pool, S["norm2"], u, RING, per=2)
                o = joined[:, u.s, :]
                nc.gpsimd.tensor_tensor(o, norm[:, u.s, :], affine[0][:, :], ALU.mult).then_inc(j, 1)
                after(pool, j, u, per=joins, upto=1)
                nc.gpsimd.tensor_tensor(o, o, affine[1][:, :], ALU.add).then_inc(j, 1)
                for n in range(2, joins):
                    after(pool, j, u, per=joins, upto=n)
                    pool.sem_inc(taken_pool, 1)
                    nc.gpsimd.tensor_tensor(o, o, blk(K.x, u, D), ALU.add).then_inc(j, 1)

            def bring(u):
                if kind == ATTENTION:
                    after(pool, S["turned"], u, RING)
                    pool.sem_inc(taken_pool, 1)
                    nc.gpsimd.tensor_copy(z_in[:, u.s, :], blk(K.acc, u, D)).then_inc(S["input"], 1)

            def keep(u):
                after(pool, S["norm2"], u, per=2)
                if kind == ATTENTION:
                    after(pool, S["layer"], u)
                pool.sem_inc(taken_pool, 1)
                nc.gpsimd.tensor_copy(blk(K.x, u, D), fresh[:, u.s, :]).then_inc(S["kept"], 1)

            def begin(u):
                if kind == ATTENTION:
                    after(pool, S["rows_act"], u, per=2, upto=1)
                    pool.sem_inc(taken_pool, 1)
                    nc.gpsimd.tensor_copy(blk(K.acc, u, HEADS * HZ),
                                          rows[:, u.s % 2, 0:HEADS * HZ]).then_inc(S["begun"], 1)

            if first:
                pipeline(pool, N, RING, 4, stages(N, (0, bring), (2, join), (4, keep), (4, begin)))

        @block.scalar
        def _(act):
            def copy_turned(u):
                if inner:
                    after(act, S["turned"], u)
                    after(act, S["product"], u, 2)
                    nc.scalar.copy(z_t[:, u.s % 2, :], K.bank[0][:, 0:D]).then_inc(S["turned_out"], 1)

            def hide(u):
                if kind == GIN:
                    after(act, S["product"], u)
                    after(act, S["product2"], u, 2)
                    nc.scalar.activation(hidden[:, u.s % 2, :], K.bank[1][:, 0:D], ACT.Relu,
                                         bias=K.gin_b1[:, :]).then_inc(S["hidden"], 1)

            def show(u):
                if kind == GIN:
                    after(act, S["product2"], u)
                    after(act, S["norm1"], u, RING, per=2)
                    nc.scalar.activation(layer[:, u.s, :], K.bank[2][:, 0:D], ACT.Relu).then_inc(S["layer"], 1)

            def root_first(u):
                if first:
                    root_of(act, 0, u)

            def root_second(u):
                if second:
                    root_of(act, 1, u)

            def copy_row(u):
                if tables:
                    after(act, S["row_turned"], u)
                    after(act, S["rows"], u, 2, per=3 if kind != ATTENTION else 1)
                    nc.scalar.copy(x_t[:, u.s % 2, :], K.bank[3][:, 0:D]).then_inc(S["row_turned_out"], 1)

            def copy_rows(u):
                if kind == ATTENTION:
                    bank = K.bank[4 + u.s % 2]
                    after(act, S["rows"], u)
                    after_stored(act, u)
                    after(act, S["begun"], u, 2)
                    nc.scalar.copy(rows[:, u.s % 2, :], bank[:, 0:ROW1]).then_inc(S["rows_act"], 1)
                    nc.scalar.copy(blk(K.own, u, OWN1), bank[:, ROW1 - HEADS:WIDE1]).then_inc(S["rows_act"], 1)
                elif tables:
                    after(act, S["rows"], u, per=3, upto=1)
                    after_stored(act, u)
                    nc.scalar.copy(rows[:, u.s % 2, 0:4 * D], K.bank[4][:, :]).then_inc(S["rows_act"], 1)

            pipeline(act, N, RING, 4, stages(N, (1, copy_turned), (3, root_second), (4, copy_row), (2, root_first),
                                             (1, hide), (4, copy_rows), (1, show)))

        @block.tensor
        def _(pe):
            def turn(u):
                if inner:
                    after(pe, S["input"], u)
                    after(pe, S["turned_out"], u, 1)
                    nc.tensor.transpose(K.bank[0][:, 0:D], z_in[:, u.s, :], K.ident[:, :]).then_inc(S["turned"], 1)

            def multiply(u):
                if kind == ATTENTION:
                    after(pe, S["turned_out"], u)
                    after(pe, S["layer"], u, 2)
                    out = K.bank[1 + u.s % 2][:, 0:D]
                    nc.tensor.matmul(out, z_t[:, u.s % 2, :], K.vo[:, :], start=True, stop=False)
                    nc.tensor.matmul(out, K.ones[0:1, :], K.b0[:, :], start=False, stop=True).then_inc(S["product"], 1)
                if kind == GIN:
                    after(pe, S["turned_out"], u)
                    after(pe, S["hidden"], u, 1)
                    nc.tensor.matmul(K.bank[1][:, 0:D], K.gin_w1[:, :], z_t[:, u.s % 2, :], start=True,
                                     stop=True).then_inc(S["product"], 1)

            def multiply2(u):
                if kind == GIN:
                    after(pe, S["hidden"], u)
                    after(pe, S["layer"], u, 1)
                    nc.tensor.matmul(K.bank[2][:, 0:D], hidden[:, u.s % 2, :], K.gin_w2[:, :], start=True, stop=False)
                    nc.tensor.matmul(K.bank[2][:, 0:D], K.ones[0:1, :], K.gin_b2[:, :], start=False,
                                     stop=True).then_inc(S["product2"], 1)

            def turn_row(u):
                if tables:
                    after(pe, S["layer"] if kind == RELATIONS else S["norm2"], u, per=1 if kind == RELATIONS else 2)
                    after(pe, S["row_turned_out"], u, 1)
                    src = z_in[:, u.s, :] if kind == RELATIONS else fresh[:, u.s, :]
                    nc.tensor.transpose(K.bank[3][:, 0:D], src, K.ident[:, :]).then_inc(S["row_turned"], 1)

            def make_rows(u):
                if kind == ATTENTION:
                    bank = K.bank[4 + u.s % 2]
                    after(pe, S["row_turned_out"], u)
                    after(pe, S["rows_act"], u, 2, per=2)
                    nc.tensor.matmul(bank[:, 0:WIDE1], x_t[:, u.s % 2, :], K.w1[:, :], start=True, stop=False)
                    nc.tensor.matmul(bank[:, 0:WIDE1], K.ones[0:1, :], K.b1[:, :], start=False,
                                     stop=True).then_inc(S["rows"], 1)
                elif tables:
                    after(pe, S["row_turned_out"], u)
                    after(pe, S["rows_act"], u, 1)
                    nc.tensor.matmul(K.bank[4][:, :], x_t[:, u.s % 2, :], rel_w[:, 0:4, :], start=True,
                                     stop=True).then_inc(S["rows"], 1)
                    after(pe, S["rows_dve"], u, 1, per=2)
                    nc.tensor.matmul(K.bank[5][:, :], x_t[:, u.s % 2, :], rel_w[:, 4:8, :], start=True,
                                     stop=True).then_inc(S["rows"], 1)
                    own = K.bank[6 + u.s % 2][:, 0:D]
                    last = nc.tensor.matmul(own, x_t[:, u.s % 2, :], rel_w[:, REL, :], start=True, stop=(kind == GIN))
                    if kind == RELATIONS:
                        last = nc.tensor.matmul(own, K.ones[0:1, :], K.rel_b2[:, :], start=False, stop=True)
                    last.then_inc(S["rows"], 1)

            pipeline(pe, N, RING, 4, stages(N, (1, turn), (4, turn_row), (1, multiply), (4, make_rows), (1, multiply2)))

        @block.sync
        def _(sp):
            def store(u):
                if tables:
                    after(sp, S["rows_act"], u, per=2 if kind == ATTENTION else 1)
                    if kind != ATTENTION:
                        sp.sem_inc(taken_sp, 1)
                        after(sp, S["rows_dve"], u, per=2)
                    sp.sem_inc(taken_sp, 1)
                    sp.dma_start(table[bass.ds(u.at(P), P), :], rows[:, u.s % 2, :]).then_inc(stored[u.s % 2], 16)
                if kind == SOFTMAX:
                    after(sp, S["norm2"], u, per=2)
                    sp.sem_inc(taken_sp, 1)
                    sp.dma_start(table[bass.ds(u.at(P), P), :], fresh[:, u.s, :]).then_inc(row_stored[u.s], 16)
                if kind == LAST:
                    after(sp, S["norm2"], u, per=2)
                    sp.sem_inc(taken_sp, 1)
                    n = g.tail if isinstance(u.i, int) and u.at() == N - 1 else P
                    sp.dma_start(table[bass.ds(u.at(P), n), :], fresh[0:n, u.s, :]).then_inc(row_stored[u.s], 16)

            pipeline(sp, N, RING, 0, stages(N, (0, store)))
            if row_stored:
                for s in range(RING):
                    sp.wait_ge(row_stored[s], 16 * ((N - s + RING - 1) // RING))
            else:
                for s in range(2):
                    sp.wait_ge(stored[s], 16 * ((N - s + 1) // 2))


class Kept:

    def __init__(self, nc, ctx, g):
        def sb(name, shape, dt=F32):
            return ctx.enter_context(nc.sbuf_tensor(name, shape, dt))

        self.semaphores = []
        NB, NI = g.blocks, g.items
        self.bank = [ctx.enter_context(nc.psum_tensor(f"bank{j}", [P, 512], F32)) for j in range(8)]
        self.x = sb("x_nodes", [P, NB, D])
        self.own = sb("own", [P, NB, OWN1])
        self.acc = sb("acc", [P, NB, HEADS * HZ])
        self.node = sb("node", [P, NI])
        self.src_row = sb("src_row", [P, NI], I32)
        self.rel_row = sb("rel_row", [P, NI], I32)
        self.ends = sb("ends", [P, NI])
        self.starts = sb("starts", [P, NI])
        self.cut = sb("cut", [P, g.units, HEADS * (UNIT + 1)])
        self.block_no = sb("block_no", [1, NI], I32)
        self.rows = sb("row_numbers", [P, LONG_RING, UNIT], I32)
        self.ring = sb("ring", [P, LONG_RING * UNIT, ROW1])
        self.member = sb("member", [P, RING, UNIT, P])
        self.ident, self.col, self.part = sb("ident", [P, P]), sb("col", [P, P]), sb("part", [P, 1])
        self.ident_b = sb("ident_b", [P, P], BF16)
        self.ones, self.eps = sb("ones", [P, P]), sb("eps", [P, 1])
        self.qk, self.vo = sb("qk", [P, P]), sb("vo", [P, P])
        self.w1, self.b1 = sb("w1", [P, WIDE1]), sb("b1", [1, WIDE1])
        self.b0 = sb("b0", [1, D])
        self.gin_w1, self.gin_w2 = sb("gin_w1", [P, D]), sb("gin_w2", [P, D])
        self.gin_b1, self.gin_b2 = sb("gin_b1", [P, 1]), sb("gin_b2", [1, D])
        self.eta1 = sb("eta1", [P, 1])
        self.affine = [sb(f"affine{j}", [P, D]) for j in range(6)]
        self.rel_w = [sb(f"rel_w{j}", [P, REL + 1, D]) for j in range(2)]
        self.rel_b1, self.rel_b2 = sb("rel_b1", [P, D]), sb("rel_b2", [1, D])


def gnn(nc, W, out, stop=99):
    g = Graph(W["x"].shape[0], W["src"].shape[0])
    rows = g.blocks * P
    with ExitStack() as ctx:
        K = Kept(nc, ctx, g)
        soft_table = nc.dram_tensor("soft_table", (rows, ROW1), F32).ap()
        records = nc.dram_tensor("records", (g.groups * P * P, 3), I32).ap()
        gin_table = nc.dram_tensor("gin_table", (rows, D), F32).ap()
        rel_tables = [nc.dram_tensor(f"rel_table{j}", (rows, REL * D), F32).ap() for j in range(2)]
        by_relation = lambda t: t.rearrange("n (r c) -> (n r) c", r=REL)
        parts = [
            lambda: load_and_fold(nc, g, K, W),
            lambda: order_edges(nc, g, K, W["src"], W["dst"], W["edge_type_8"], records),
            lambda: build_graph(nc, g, K),
            lambda: query_rows(nc, g, K),
            lambda: attention_items(nc, g, K, W["x"]),
            lambda: node_pass(nc, g, K, ATTENTION, "attn_nodes", soft_table, K.affine[0:2]),
            lambda: softmax_items(nc, g, K, soft_table),
            lambda: node_pass(nc, g, K, SOFTMAX, "soft_nodes", gin_table, K.affine[2:4]),
            lambda: sum_items(nc, g, K, "gin", gin_table, K.src_row),
            lambda: node_pass(nc, g, K, GIN, "gin_nodes", rel_tables[0], K.affine[4:6]),
            lambda: sum_items(nc, g, K, "rel1", by_relation(rel_tables[0]), K.rel_row),
            lambda: node_pass(nc, g, K, RELATIONS, "rel1_nodes", rel_tables[1]),
            lambda: sum_items(nc, g, K, "rel2", by_relation(rel_tables[1]), K.rel_row),
            lambda: node_pass(nc, g, K, LAST, "rel2_nodes", out),
        ]
        for part in parts[:stop]:
            part()
            nc.clear_and_free_semaphores(K.semaphores)
            nc.all_engine_barrier()
            K.semaphores = []
        return K


_INS = ["x", "src", "dst", "edge_type_8", "L0_gnn_Wq", "L0_gnn_Wk", "L0_gnn_Wv", "L0_gnn_Wo", "L0_gnn_bo",
        "L0_gnn_gamma", "L0_gnn_beta", "L1_gnn_W", "L1_gnn_att_src", "L1_gnn_att_dst", "L1_gnn_gat_bias",
        "L1_gnn_skip_W", "L1_gnn_skip_b", "L1_gnn_ln_g", "L1_gnn_ln_b", "L2_gnn_W1", "L2_gnn_b1", "L2_gnn_W2",
        "L2_gnn_b2", "L2_gnn_eta", "L2_gnn_ln_gamma", "L2_gnn_ln_beta", "L3_gnn_w1", "L3_gnn_sw1", "L3_gnn_b1",
        "L3_gnn_w2", "L3_gnn_sw2", "L3_gnn_b2"]


def kernel(**inputs):
    import numpy as np
    import concourse.bacc as bacc
    from concourse.bass_utils import run_bass_kernel_spmd

    nc = bacc.Bacc("TRN2", target_bir_lowering=False, num_devices=1)
    arrays, tensors = {}, {}
    for name in _INS:
        a = np.ascontiguousarray(inputs[name])
        arrays[f"in_{name}"] = a
        tensors[name] = nc.dram_tensor(f"in_{name}", a.shape, mybir.dt.from_np(a.dtype), kind="ExternalInput").ap()
    out = nc.dram_tensor("out_nodes", inputs["x"].shape, F32, kind="ExternalOutput").ap()
    gnn(nc, tensors, out)
    return run_bass_kernel_spmd(nc, [arrays], core_ids=[0]).results[0]["out_nodes"]
```

```python
import concourse.bass as bass
from concourse import mybir
from contextlib import ExitStack

P = 128
F32 = mybir.dt.float32
BF16 = mybir.dt.bfloat16
I32 = mybir.dt.int32
ALU = mybir.AluOpType
ACT = mybir.ActivationFunctionType
AX = mybir.AxisListType

D = 128
HEADS, HC = 4, 32
HZ = HC + 1
REL = 8
LN_EPS = 1e-05
SOFTMAX_EPS = 1e-16
SLOPE = 0.2
FAR = float(2.0 ** 100)
NO_NODE = (P - 1) * P

UNIT = 4
RING = 4
LONG_RING = 8
ROW1 = HEADS * HZ + HEADS
WIDE1 = ROW1 + HEADS + D
OWN1 = 2 * HEADS + D


class Step:

    def __init__(self, i, s, per):
        self.i, self.s, self.per = i, s, per

    def back(self, lag):
        s = self.s - lag
        return Step(self.i + s // self.per, s % self.per, self.per)

    def at(self, scale=1, offset=0):
        return self.i * (self.per * scale) + (self.s * scale + offset)

    def exists(self, total):
        return not isinstance(self.i, int) or 0 <= self.at() < total


def after(eng, sem, u, back=0, per=1, upto=None):
    value = u.at(per, (upto if upto is not None else per) - back * per)
    if isinstance(value, int) and value <= 0:
        return
    eng.wait_ge(sem, value)


def pipeline(eng, total, per, longest, step, peel=2):
    full = total // per
    for n in range(peel * per):
        step(Step(n // per, n % per, per))
    with eng.Fori(peel, full) as i:
        for s in range(per):
            step(Step(i, s, per))
    for n in range(full * per, total + longest):
        step(Step(n // per, n % per, per))


def stages(total, *parts):
    def step(u):
        for lag, stage in parts:
            v = u.back(lag)
            if v.exists(total):
                stage(v)
    return step


class Memory:

    def __init__(self, nc, ctx, K, name):
        self.nc, self.ctx, self.K, self.name = nc, ctx, K, name

    def sb(self, name, shape, dt=F32):
        return self.ctx.enter_context(self.nc.sbuf_tensor(f"{self.name}_{name}", shape, dt))

    def within(self, t, taken, shape, dt=F32):
        flat = t[:, :, :].rearrange("p b d -> p (b d)")
        count = 1
        for n in shape[1:]:
            count *= n
        flat = flat[:, taken:taken + count]
        if dt is not F32:
            flat = flat.bitcast(dt)
        return flat if len(shape) == 2 else flat.rearrange("p (g c) -> p g c", c=shape[2])

    def sem(self, name):
        one = self.nc.alloc_semaphore(f"{self.name}_{name}")
        self.K.semaphores.append(one)
        return one


def bcast(ap, axis, count):
    shape = list(ap.shape)
    ap = ap.unsqueeze(axis)
    shape.insert(axis, count)
    return ap.broadcast_to(shape)


def upper(ap):
    ap = ap.bitcast(BF16)
    free = [f"a{j}" for j in range(len(ap.shape) - 2)]
    lead = " ".join(["p"] + free)
    return ap.rearrange(f"{lead} (n half) -> {lead} n half", half=2)[(slice(None),) * (len(ap.shape)) + (1,)]


class Graph:

    def __init__(self, nodes, edges):
        self.nodes, self.edges = nodes, edges
        self.blocks = -(-nodes // P)
        self.tail = nodes - (self.blocks - 1) * P
        self.tiles = -(-edges // P)
        self.groups = -(-self.tiles // P)
        body = UNIT * RING
        self.items = -(-(self.tiles + self.blocks - 1) // body) * body
        self.units = self.items // UNIT
        assert self.items <= self.groups * P and nodes * REL < 1 << 24 and self.blocks < P


def edge_rows(g, K):
    flat = K.ring[:, :, :].rearrange("p b d -> p (b d)").bitcast(I32)
    n = g.groups * P
    return [flat[:, j * n:(j + 1) * n].rearrange("p (g c) -> p g c", c=P) for j in range(3)]


def order_edges(nc, g, K, records):
    G = g.groups
    NT = G * P
    low, high = 4, 3
    with ExitStack() as ctx:
        M = Memory(nc, ctx, K, "order")
        rows = edge_rows(g, K)
        first_dst = M.sb("first_dst", [P, G], I32)
        next_dst = M.sb("next_dst", [P, G], I32)
        bad, bad_sum = M.sb("bad", [P, 2]), M.sb("bad_sum", [P, 1])
        unsorted = M.sb("unsorted", [1, 1], I32)
        place_u = M.sb("place_u", [P, 2, UNIT], I32)
        record_u = M.sb("record_u", [P, 2, UNIT, 3], I32)
        row_f = M.within(K.acc, 0, [P, G, P])
        worse = M.within(K.acc, NT, [P, G, P])
        digit_f, place_f = M.within(K.acc, NT, [P, NT]), M.within(K.acc, 2 * NT, [P, NT])
        digit_i = M.within(K.acc, 3 * NT, [P, NT], I32)
        place_i = digit_i
        record = M.within(K.acc, 4 * NT, [P, NT, 3], I32)
        record_rows = M.within(K.own, 0, [P, G, 3 * P], I32)
        mask, product = K.member[:, 0, :, :], K.member[:, 1, :, :]
        before, carry, count = (K.member[:, 2, j, :] for j in range(3))
        firsts_ready = M.sem("firsts_ready")
        shifted, chain = M.sem("shifted"), M.sem("chain")
        bad_ready, bad_summed, flag_ready = M.sem("bad_ready"), M.sem("bad_summed"), M.sem("flag")
        row_ready, turned, masks_ready, ranked = M.sem("row"), M.sem("turned"), M.sem("masks"), M.sem("ranked")
        counted, counts_ready, based, based_out = M.sem("counted"), M.sem("counts"), M.sem("based"), M.sem("based_out")
        staged, sorted_out, reloaded = M.sem("staged"), M.sem("sorted_out"), M.sem("reloaded")
        scattered = [M.sem(f"scattered{j}") for j in range(2)]
        opened, rank_chain = M.sem("opened"), M.sem("rank_chain")
        units = NT // UNIT
        block = ctx.enter_context(nc.Block())

        def when_unsorted(eng, engine):
            eng.wait_ge(flag_ready, 1)
            flag = nc.values_load_multi_w_load_instructions(
                unsorted[0:1, 0:1], engines=(engine,), min_val=0, max_val=1,
                skip_runtime_bounds_check_because="it is the result of a comparison")[1][0]
            return eng.If(flag > 0)

        @block.sync
        def _(sp):
            with when_unsorted(sp, mybir.EngineType.SP):
                for digit in range(2):
                    sp.wait_ge(sorted_out, digit + 1)
                    sp.dma_start(record_rows[:, :, :], records.rearrange("(g r c) k -> r g (c k)", r=P, c=P)
                                 ).then_inc(reloaded, 16)

        @block.scalar
        def _(act):
            act.wait_ge(firsts_ready, 1)
            act.dma_start(next_dst[0:P - 1, :], first_dst[1:P, :]).then_inc(shifted, 16)
            act.dma_start(next_dst[P - 1:P, 0:G - 1], first_dst[0:1, 1:G]).then_inc(shifted, 16)

        @block.gpsimd
        def _(pool):
            with when_unsorted(pool, mybir.EngineType.Pool):
                for digit in range(2):
                    with pool.Fori(0, units // 2) as i:
                        for s in range(2):
                            pool.wait_ge(staged, i * 2 + (digit * units + s + 1))
                            pool.sem_inc(opened, 1)
                            for k in range(UNIT):
                                pool.indirect_dma_start(
                                    out=records, in_=record_u[:, s, k, :], in_offset=None,
                                    out_offset=bass.IndirectOffsetOnAxis(ap=place_u[:, s, k:k + 1], axis=0),
                                ).then_inc(scattered[s], 16)
                    for s in range(2):
                        pool.wait_ge(scattered[s], (digit + 1) * 16 * UNIT * (units // 2))
                    pool.sem_inc(sorted_out, 1)

        @block.vector
        def _(dve):
            link = [0]

            def chained(ins):
                link[0] += 1
                ins.then_inc(chain, 1)
                dve.wait_ge(chain, link[0])

            nc.vector.memset(next_dst[:, :], NO_NODE)
            dve.wait_ge(K.lists_loaded, 9 * 16)
            nc.vector.tensor_copy(first_dst[:, :], rows[0][:, :, 0]).then_inc(firsts_ready, 1)
            dve.wait_ge(shifted, 2 * 16)
            nc.vector.tensor_tensor(worse[:, :, 0:P - 1], rows[0][:, :, 0:P - 1], rows[0][:, :, 1:P], ALU.is_gt)
            chained(nc.vector.tensor_tensor(worse[:, :, P - 1], rows[0][:, :, P - 1], next_dst[:, :], ALU.is_gt))
            nc.vector.tensor_reduce(bad_sum[:, :], worse.rearrange("p g c -> p (g c)"), AX.X,
                                    ALU.add).then_inc(bad_ready, 1)
            dve.wait_ge(bad_summed, 1)
            nc.vector.tensor_scalar(unsorted[:, :], K.bank[0][0:1, 0:1], 0.0, None, ALU.is_gt).then_inc(flag_ready, 1)
            with when_unsorted(dve, mybir.EngineType.DVE):
                chained(nc.vector.tensor_scalar(before, K.col[:, :], K.part[:, :], None, ALU.is_gt))
                for digit in range(2):
                    for a in range(3):
                        if digit or a:
                            dve.wait_ge(turned, digit * 3 + a)
                        chained(nc.vector.tensor_copy(row_f[:, :, :], rows[a]))
                        dve.sem_inc(row_ready, 1)
                        dve.wait_ge(turned, digit * 3 + a + 1)
                        nc.vector.tensor_copy(record[:, 0:low * P, a], K.bank[0][:, :])
                        chained(nc.vector.tensor_copy(record[:, low * P:NT, a], K.bank[1][:, 0:high * P]))
                    if digit == 0:
                        chained(nc.vector.tensor_scalar(digit_i, record[:, :, 0], P - 1, None, ALU.bitwise_and))
                    else:
                        chained(nc.vector.tensor_scalar(digit_i, record[:, :, 0], P.bit_length() - 1, None,
                                                        ALU.logical_shift_right))
                    nc.vector.tensor_copy(digit_f, digit_i)
                    chained(nc.vector.memset(product, 0.0))
                    each = lambda i: digit_f[:, bass.ds(i * UNIT, UNIT)].unsqueeze(2).broadcast_to([P, UNIT, P])
                    seen, link_0 = masks_ready, digit * 2 * units
                    with dve.Fori(0, units) as i:
                        nc.vector.tensor_tensor(mask, bcast(K.col[:, :], 1, UNIT), each(i), ALU.is_equal).then_inc(seen, 1)
                        dve.wait_ge(seen, i * 2 + (link_0 + 1))
                        nc.vector.tensor_tensor(product, product, mask, ALU.add).then_inc(seen, 1)
                        dve.wait_ge(seen, i * 2 + (link_0 + 2))
                    dve.sem_inc(counted, 1)
                    dve.wait_ge(counts_ready, digit + 1)
                    chained(nc.vector.tensor_copy(count, K.bank[2][:, 0:P]))
                    dve.sem_inc(counted, 1)
                    dve.wait_ge(based, digit + 1)
                    chained(nc.vector.tensor_copy(carry, K.bank[3][:, 0:P]))
                    dve.sem_inc(based_out, 1)
                    with dve.Fori(0, units) as i:
                        rank = i * 4 + digit * 4 * units
                        nc.vector.tensor_tensor(mask, bcast(K.col[:, :], 1, UNIT), each(i), ALU.is_equal
                                                ).then_inc(based_out, 1)
                        dve.wait_ge(ranked, i + (digit * units + 1))
                        nc.vector.tensor_tensor(product, K.bank[2][:, :].rearrange("p (k d) -> p k d", k=UNIT),
                                                bcast(carry, 1, UNIT), ALU.add).then_inc(rank_chain, 1)
                        dve.wait_ge(rank_chain, rank + 1)
                        nc.vector.tensor_tensor(carry, carry, K.bank[3][:, 0:P], ALU.add).then_inc(rank_chain, 1)
                        nc.vector.tensor_tensor(product, product, mask, ALU.mult).then_inc(rank_chain, 1)
                        dve.wait_ge(rank_chain, rank + 3)
                        nc.vector.tensor_reduce(place_f[:, bass.ds(i * UNIT, UNIT)], product, AX.X,
                                                ALU.add).then_inc(rank_chain, 1)
                        dve.wait_ge(rank_chain, rank + 4)
                    chained(nc.vector.tensor_copy(place_i, place_f))

                    def stage(i, s):
                        nc.vector.tensor_copy(place_u[:, s, :], place_i[:, bass.ds(i * (2 * UNIT) + s * UNIT, UNIT)])
                        nc.vector.tensor_copy(record_u[:, s, :, :],
                                              record[:, bass.ds(i * (2 * UNIT) + s * UNIT, UNIT), :]).then_inc(staged, 1)

                    for s in range(2):
                        stage(0, s)
                    with dve.Fori(1, units // 2) as i:
                        for s in range(2):
                            dve.wait_ge(scattered[s], i * (16 * UNIT) + digit * 16 * UNIT * (units // 2))
                            stage(i, s)
                    dve.wait_ge(reloaded, 16 * (digit + 1))
                    for a in range(3):
                        last = nc.vector.tensor_copy(rows[a], record_rows.rearrange("p g (c k) -> p g c k", k=3)[:, :, :, a])
                    chained(last)

        @block.tensor
        def _(pe):
            pe.wait_ge(bad_ready, 1)
            nc.tensor.matmul(K.bank[0][0:1, 0:1], bad_sum[:, :], K.ones[:, 0:1], start=True,
                             stop=True).then_inc(bad_summed, 1)
            with when_unsorted(pe, mybir.EngineType.PE):
                for digit in range(2):
                    for a in range(3):
                        pe.wait_ge(row_ready, digit * 3 + a + 1)
                        for q in range(G):
                            last = nc.tensor.transpose(K.bank[q // low][:, (q % low) * P:(q % low + 1) * P],
                                                       row_f[:, q, :], K.ident[:, :])
                        last.then_inc(turned, 1)
                    pe.wait_ge(counted, 2 * digit + 1)
                    for k in range(UNIT):
                        last = nc.tensor.matmul(K.bank[2][:, 0:P], product[:, k, :], K.ones[:, :], start=(k == 0),
                                                stop=(k == UNIT - 1))
                    last.then_inc(counts_ready, 1)
                    pe.wait_ge(counted, 2 * digit + 2)
                    nc.tensor.matmul(K.bank[3][:, 0:P], count, before, start=True, stop=True).then_inc(based, 1)
                    pe.wait_ge(based_out, digit * (units + 1) + 1)
                    with pe.Fori(0, units) as i:
                        pe.wait_ge(based_out, i + (digit * (units + 1) + 2))
                        nc.tensor.matmul(K.bank[2][:, :], before, mask, start=True, stop=False)
                        for k in range(1, UNIT):
                            last = nc.tensor.matmul(K.bank[2][:, k * P:], K.ones[:, :], mask[:, 0:UNIT - k, :],
                                                    start=False, stop=(k == UNIT - 1))
                        for k in range(UNIT):
                            last = nc.tensor.matmul(K.bank[3][:, 0:P], K.ones[:, :], mask[:, k, :], start=(k == 0),
                                                    stop=(k == UNIT - 1))
                        last.then_inc(ranked, 1)


def build_graph(nc, g, K, x):
    G, NB, NI = g.groups, g.blocks, g.items
    NT = G * P
    with ExitStack() as ctx:
        M = Memory(nc, ctx, K, "prep")
        dst_rows, src_rows, type_rows = edge_rows(g, K)
        dst_f, src_f, rel_f, end_f, start_f = (M.within(K.acc, j * NT, [P, G, P]) for j in range(5))
        limit = M.sb("limit", [P, NB - 1, 1])
        before = M.sb("before", [P, NB - 1, G])
        tiles_before = M.sb("tiles_before", [P, NB - 1])
        rank = M.sb("rank", [P, 1])
        item_no, item_mod, block_past, block_of, place, pick_own, pick_prev = (
            M.within(K.own, j * NT, [P, NT]) for j in range(7))
        change = item_no
        consts = M.sem("consts")
        chain, rank_sum, rank_ready = M.sem("chain"), M.sem("rank_sum"), M.sem("rank_ready")
        mask_ready, blocks_ready, picks_ready = M.sem("mask_ready"), M.sem("blocks_ready"), M.sem("picks_ready")
        table_ready, table_out = M.sem("table_ready"), M.sem("table_out")
        block = ctx.enter_context(nc.Block())
        half = NT // 2
        arrays = [dst_f, src_f, rel_f, end_f, start_f]

        def load_nodes(eng, first, last):
            with eng.Fori(first, last) as b:
                eng.dma_start(K.x[:, bass.ds(b, 1), :].rearrange("p a d -> p (a d)"),
                              x[bass.ds(b * P, P), :]).then_inc(K.x_loaded, 16)

        @block.sync
        def _(sp):
            load_nodes(sp, 0, NB // 2)

        @block.scalar
        def _(act):
            load_nodes(act, NB // 2, NB - 1)
            act.dma_start(K.x[0:g.tail, NB - 1, :], x[(NB - 1) * P:g.nodes, :]).then_inc(K.x_loaded, 16)

        @block.gpsimd
        def _(pool):
            nc.gpsimd.iota(limit[:, :, :], [[P, NB - 1]], base=P, channel_multiplier=0,
                           allow_small_or_imprecise_dtypes=True).then_inc(consts, 1)
            nc.gpsimd.iota(item_no[:, :], [[1, NT]], base=0, channel_multiplier=0,
                           allow_small_or_imprecise_dtypes=True).then_inc(consts, 1)
            nc.gpsimd.iota(item_mod[:, :], [[0, G], [1, P]], base=0, channel_multiplier=0,
                           allow_small_or_imprecise_dtypes=True).then_inc(consts, 1)

        @block.vector
        def _(dve):
            link = [0]

            def chained(ins):
                link[0] += 1
                ins.then_inc(chain, 1)
                dve.wait_ge(chain, link[0])

            dve.wait_ge(consts, 3)
            nc.vector.tensor_copy(dst_f[:, :, :], dst_rows[:, :, :])
            nc.vector.tensor_copy(src_f[:, :, :], src_rows[:, :, :])
            chained(nc.vector.tensor_copy(rel_f[:, :, :], type_rows[:, :, :]))
            chained(nc.vector.tensor_tensor(before[:, :, :], bcast(dst_f[:, :, P - 1], 1, NB - 1),
                                            limit[:, :, :].broadcast_to([P, NB - 1, G]), ALU.is_lt))
            nc.vector.tensor_reduce(tiles_before[:, :], before[:, :, :], AX.X, ALU.add).then_inc(rank_ready, 1)
            chained(nc.vector.scalar_tensor_tensor(rel_f[:, :, :], src_f[:, :, :], float(REL), rel_f[:, :, :],
                                                   ALU.mult, ALU.add))
            nc.vector.memset(end_f[:, :, :], 1.0)
            chained(nc.vector.memset(start_f[:, :, :], -FAR))
            chained(nc.vector.tensor_tensor(end_f[:, :, 0:P - 1], dst_f[:, :, 0:P - 1], dst_f[:, :, 1:P],
                                            ALU.not_equal))
            chained(nc.vector.tensor_scalar(start_f[:, :, 1:P], end_f[:, :, 0:P - 1], -FAR, None, ALU.mult))
            dve.wait_ge(rank_sum, 1)
            chained(nc.vector.tensor_tensor(rank[0:NB - 1, :], K.bank[0][0:NB - 1, 0:1], K.part[0:NB - 1, :],
                                            ALU.add))
            nc.vector.tensor_scalar(block_past[0:NB - 1, :], item_no[0:NB - 1, :], rank[0:NB - 1, :], None,
                                    ALU.is_gt).then_inc(mask_ready, 1)
            dve.wait_ge(blocks_ready, 1)
            for h in range(2):
                last = nc.vector.tensor_copy(block_of[:, h * half:(h + 1) * half], K.bank[1 + h][:, 0:half])
            chained(last)
            nc.vector.tensor_copy(K.block_no[:, :], block_of[0:1, 0:NI])
            chained(nc.vector.tensor_tensor(place[:, :], item_mod[:, :], block_of[:, :], ALU.subtract))
            nc.vector.tensor_scalar(pick_own[:, :], place[:, :], K.part[:, :], None, ALU.is_equal)
            nc.vector.tensor_scalar(pick_prev[:, :], place[:, :], float(P), K.part[:, :], ALU.add,
                                    ALU.is_equal).then_inc(picks_ready, 1)
            nc.vector.memset(change[:, 0:1], -FAR)
            chained(nc.vector.tensor_tensor(change[:, 1:NT], block_of[:, 1:NT], block_of[:, 0:NT - 1],
                                            ALU.not_equal))
            chained(nc.vector.tensor_scalar(change[:, 1:NT], change[:, 1:NT], -FAR, None, ALU.mult))
            cut = K.cut[:, :, :].rearrange("p u (h k) -> p u h k", h=HEADS)
            nc.vector.memset(cut[:, :, :, 0], -FAR)
            for h in range(HEADS):
                nc.vector.tensor_copy(cut[:, :, h, 1:UNIT + 1],
                                      change[:, 0:NI].rearrange("p (u k) -> p u k", k=UNIT))
            for a in range(5):
                dve.wait_ge(table_ready, a + 1)
                lo, hi = K.bank[3 + 2 * (a % 2)], K.bank[4 + 2 * (a % 2)]
                for bank, c0, n in ((lo, 0, half), (hi, half, NI - half)):
                    if a == 0:
                        last = nc.vector.scalar_tensor_tensor(K.node[:, c0:c0 + n], block_of[:, c0:c0 + n], float(-P),
                                                              bank[:, 0:n], ALU.mult, ALU.add)
                    else:
                        into = (K.src_row, K.rel_row, K.ends, K.starts)[a - 1]
                        last = nc.vector.tensor_copy(into[:, c0:c0 + n], bank[:, 0:n])
                last.then_inc(table_out, 1)

        @block.tensor
        def _(pe):
            pe.wait_ge(rank_ready, 1)
            nc.tensor.matmul(K.bank[0][0:NB - 1, 0:1], tiles_before[:, :], K.ones[:, 0:1], start=True,
                             stop=True).then_inc(rank_sum, 1)
            pe.wait_ge(mask_ready, 1)
            for h in range(2):
                last = nc.tensor.matmul(K.bank[1 + h][:, 0:half], K.ones[0:NB - 1, :],
                                        block_past[0:NB - 1, h * half:(h + 1) * half], start=True, stop=True)
            last.then_inc(blocks_ready, 1)
            pe.wait_ge(picks_ready, 1)
            pe.wait_ge(chain, 7)
            for a, rows in enumerate(arrays):
                if a >= 2:
                    pe.wait_ge(table_out, a - 1)
                for q in range(G):
                    for c0, n in ((q * P, min(P, max(0, half - q * P))), (max(q * P, half), min(P, (q + 1) * P - half))):
                        if n <= 0 or c0 >= (q + 1) * P:
                            continue
                        bank, at = (K.bank[3 + 2 * (a % 2)], c0) if c0 < half else (K.bank[4 + 2 * (a % 2)], c0 - half)
                        last = nc.tensor.matmul(bank[:, at:at + n], rows[:, q, :], pick_own[:, c0:c0 + n],
                                                start=True, stop=(q == 0))
                        if q:
                            last = nc.tensor.matmul(bank[:, at:at + n], rows[:, q - 1, :], pick_prev[:, c0:c0 + n],
                                                    start=False, stop=True)
                last.then_inc(table_ready, 1)


def load_and_fold(nc, g, K, W):
    with ExitStack() as ctx:
        M = Memory(nc, ctx, K, "fold")
        part_no = M.sb("part_no", [P, 1], I32)
        col_no = M.sb("col_no", [P, P], I32)
        wq, wk, wv, wo = (M.sb(n, [P, P]) for n in ("wq", "wk", "wv", "wo"))
        wo_t = M.sb("wo_t", [P, P])
        w1, w1_t, att = M.sb("w1", [P, P]), M.sb("w1_t", [P, P]), M.sb("att", [P, 2 * HEADS])
        gin1, gin2 = M.sb("gin1", [P, P]), M.sb("gin2", [P, P])
        skip_b = M.sb("skip_b", [1, D])
        eta = M.sb("eta", [P, 1])
        zeroed, iotas, loaded = M.sem("zeroed"), M.sem("iotas"), M.sem("loaded")
        chain, ident_ready = M.sem("chain"), M.sem("ident_ready")
        turned, turned_out, folded, folded_out = M.sem("turned"), M.sem("turned_out"), M.sem("folded"), M.sem("folded_out")
        loads = [0]
        lists = edge_rows(g, K)
        block = ctx.enter_context(nc.Block())

        @block.sync
        def _(sp):
            def load(out, in_):
                loads[0] += 16
                sp.dma_start(out, in_).then_inc(loaded, 16)

            row = lambda v: v.rearrange("(a d) -> a d", a=1)
            sp.wait_ge(zeroed, 1)
            for t, n in ((wq, "L0_gnn_Wq"), (wk, "L0_gnn_Wk"), (wv, "L0_gnn_Wv"), (wo, "L0_gnn_Wo"), (w1, "L1_gnn_W"),
                         (gin1, "L2_gnn_W1"), (gin2, "L2_gnn_W2")):
                load(t[:, :], W[n])
            for h in range(HEADS):
                for j, n in enumerate(("L1_gnn_att_src", "L1_gnn_att_dst")):
                    load(att[h * HC:(h + 1) * HC, j * HEADS + h:j * HEADS + h + 1],
                         W[n][h:h + 1, :].rearrange("a c -> c a"))
            load(K.w1[:, ROW1 + HEADS:], W["L1_gnn_skip_W"])
            load(K.b0[:, 0, :], row(W["L0_gnn_bo"]))
            load(K.b1[:, 0, ROW1 + HEADS:], row(W["L1_gnn_gat_bias"]))
            load(skip_b[:, :], row(W["L1_gnn_skip_b"]))
            load(K.gin_b1[:, :], W["L2_gnn_b1"].rearrange("(d a) -> d a", a=1))
            load(K.gin_b2[:, 0, :], row(W["L2_gnn_b2"]))
            load(eta[:, :], W["L2_gnn_eta"].broadcast_to([P, 1]))
            for t, n in zip(K.affine, ("L0_gnn_gamma", "L0_gnn_beta", "L1_gnn_ln_g", "L1_gnn_ln_b", "L2_gnn_ln_gamma",
                                       "L2_gnn_ln_beta")):
                load(t[:, :], row(W[n]).broadcast_to([P, D]))
            load(K.rel_b1[:, :], row(W["L3_gnn_b1"]).broadcast_to([P, D]))
            load(K.rel_b2[:, 0, :], row(W["L3_gnn_b2"]))
            for t, n, m in ((K.rel_w[0], "L3_gnn_w1", "L3_gnn_sw1"), (K.rel_w[1], "L3_gnn_w2", "L3_gnn_sw2")):
                load(t[:, 0:REL, :], W[n].rearrange("r c o -> c r o"))
                load(t[:, REL, :], W[m])
            G, whole = g.groups, (g.groups - 1) * P * P
            full, rest = (g.edges // P) % P, g.edges % P
            for into, n in zip(lists, ("dst", "src", "edge_type_8")):
                sp.dma_start(into[:, 0:G - 1, :],
                             W[n][0:whole].rearrange("(g r c) -> r g c", r=P, c=P)).then_inc(K.lists_loaded, 16)
                sp.dma_start(into[0:full, G - 1, :],
                             W[n][whole:whole + full * P].rearrange("(r c) -> r c", c=P)).then_inc(K.lists_loaded, 16)
                sp.dma_start(into[full:full + 1, G - 1, 0:rest],
                             W[n][whole + full * P:g.edges].rearrange("(r c) -> r c", r=1)).then_inc(K.lists_loaded, 16)

        @block.gpsimd
        def _(pool):
            nc.gpsimd.iota(part_no[:, :], [[0, 1]], base=0, channel_multiplier=1).then_inc(iotas, 1)
            nc.gpsimd.iota(col_no[:, :], [[1, P]], base=0, channel_multiplier=0).then_inc(iotas, 1)

        @block.vector
        def _(dve):
            nc.vector.memset(K.x[:, g.blocks - 1, :], 0.0)
            for t, value in zip(lists, (NO_NODE, 0, 0)):
                nc.vector.memset(t[:, g.groups - 1, :], value)
            nc.vector.memset(K.w1[:, :], 0.0)
            nc.vector.memset(K.b1[:, :, :], 0.0).then_inc(chain, 1)
            nc.vector.memset(K.ones[:, :], 1.0)
            nc.vector.memset(K.eps[:, :], LN_EPS)
            dve.wait_ge(chain, 1)
            nc.vector.memset(K.b1[:, 0, 0:HEADS * HZ].rearrange("p (h z) -> p h z", h=HEADS)[:, :, HC], 1.0)
            nc.vector.memset(att[:, :], 0.0).then_inc(zeroed, 1)
            dve.wait_ge(iotas, 2)
            nc.vector.tensor_copy(K.col[:, :], col_no[:, :])
            nc.vector.tensor_copy(K.part[:, :], part_no[:, :]).then_inc(chain, 1)
            dve.wait_ge(chain, 2)
            nc.vector.tensor_scalar(K.ident[:, :], K.col[:, :], K.part[:, :], None,
                                    ALU.is_equal).then_inc(ident_ready, 1)
            nc.vector.tensor_scalar(K.ident_b[:, :], K.col[:, :], K.part[:, :], None, ALU.is_equal)
            dve.wait_ge(loaded, loads[0])
            nc.vector.tensor_copy(K.w1[:, 0:HEADS * HZ].rearrange("p (h z) -> p h z", h=HEADS)[:, :, 0:HC],
                                  w1[:, :].rearrange("p (h c) -> p h c", h=HEADS))
            nc.vector.tensor_scalar(K.eta1[:, :], eta[:, :], 1.0, None, ALU.add)
            nc.vector.tensor_tensor(K.b1[:, 0, ROW1 + HEADS:], K.b1[:, 0, ROW1 + HEADS:], skip_b[:, :],
                                    ALU.add).then_inc(chain, 1)
            for j in range(1, 3):
                dve.wait_ge(chain, j + 2)
                for bias in (K.b0, K.gin_b2, K.rel_b2, K.b1):
                    last = nc.vector.tensor_tensor(bias[:, j, :], bias[:, j - 1, :], upper(bias[:, j - 1, :]), ALU.subtract)
                last.then_inc(chain, 1)
            dve.wait_ge(turned, 1)
            for j, t in enumerate((wo_t, w1_t, K.gin_w1, K.gin_w2)):
                last = nc.vector.tensor_copy(t[:, :], K.bank[0][:, j * P:(j + 1) * P])
            last.then_inc(turned_out, 1)
            dve.wait_ge(folded, 1)
            nc.vector.tensor_scalar(K.qk[:, :], K.bank[1][:, 0:P], float(D) ** -0.5, None, ALU.mult)
            nc.vector.tensor_copy(K.vo[:, :], K.bank[1][:, P:2 * P])
            nc.vector.tensor_copy(K.w1[:, ROW1 - HEADS:ROW1 + HEADS],
                                  K.bank[1][:, 2 * P:2 * P + 2 * HEADS]).then_inc(folded_out, 1)

        @block.tensor
        def _(pe):
            pe.wait_ge(loaded, loads[0])
            pe.wait_ge(ident_ready, 1)
            for j, t in enumerate((wo, w1, gin1, gin2)):
                last = nc.tensor.transpose(K.bank[0][:, j * P:(j + 1) * P], t[:, :], K.ident[:, :])
            last.then_inc(turned, 1)
            nc.tensor.matmul(K.bank[1][:, 0:P], wq[:, :], wk[:, :], start=True, stop=True)
            pe.wait_ge(turned_out, 1)
            nc.tensor.matmul(K.bank[1][:, P:2 * P], wv[:, :], wo_t[:, :], start=True, stop=True)
            nc.tensor.matmul(K.bank[1][:, 2 * P:2 * P + 2 * HEADS], w1_t[:, :], att[:, :], start=True,
                             stop=True).then_inc(folded, 1)


def query_rows(nc, g, K):
    with ExitStack() as ctx:
        M = Memory(nc, ctx, K, "query")
        x_t = M.sb("x_t", [P, RING, P])
        x_u = M.sb("x_u", [P, RING, P])
        brought, taken = M.sem("brought"), M.sem("taken")
        turned, turned_out, made, made_out = M.sem("turned"), M.sem("turned_out"), M.sem("made"), M.sem("made_out")
        block = ctx.enter_context(nc.Block())

        @block.gpsimd
        def _(pool):
            def bring(u):
                after(pool, turned, u, RING)
                pool.sem_inc(taken, 1)
                nc.gpsimd.tensor_copy(x_u[:, u.s, :], blk(K.x, u, D)).then_inc(brought, 1)

            pool.wait_ge(K.x_loaded, 16 * g.blocks)
            pipeline(pool, g.blocks, RING, 0, stages(g.blocks, (0, bring)))

        @block.tensor
        def _(pe):
            def turn(u):
                after(pe, turned_out, u, 2)
                after(pe, brought, u)
                nc.tensor.transpose(K.bank[u.s % 2][:, 0:P], x_u[:, u.s, :], K.ident[:, :]).then_inc(turned, 1)

            def make(u):
                after(pe, turned_out, u)
                after(pe, made_out, u, 2)
                nc.tensor.matmul(K.bank[2 + u.s % 2][:, 0:P], x_t[:, u.s, :], K.qk[:, :], start=True,
                                 stop=True).then_inc(made, 1)

            pipeline(pe, g.blocks, RING, 1, stages(g.blocks, (0, turn), (1, make)))

        @block.scalar
        def _(act):
            def copy(u):
                after(act, turned, u)
                after(act, made, u, RING)
                nc.scalar.copy(x_t[:, u.s, :], K.bank[u.s % 2][:, 0:P]).then_inc(turned_out, 1)

            pipeline(act, g.blocks, RING, 0, stages(g.blocks, (0, copy)))

        @block.vector
        def _(dve):
            def copy(u):
                after(dve, made, u)
                nc.vector.tensor_copy(blk(K.own, u, D), K.bank[2 + u.s % 2][:, 0:P]).then_inc(made_out, 1)

            pipeline(dve, g.blocks, RING, 0, stages(g.blocks, (0, copy)))


def blk(t, u, n, start=0):
    return t[:, bass.ds(u.at(), 1), start:start + n].rearrange("p a d -> p (a d)")


def block_numbers(nc, engine, K, g, u, units=1):
    return nc.values_load_multi_w_load_instructions(
        K.block_no[0:1, bass.ds(u.at(UNIT), units * UNIT)], engines=(engine,), min_val=0, max_val=g.blocks - 1,
        skip_runtime_bounds_check_because="items are numbered within the blocks")[1]


def at_block(t, b, n, start=0):
    return t[:, bass.ds(b, 1), start:start + n].rearrange("p a d -> p (a d)")


def stage_rows(nc, act, K, g, index, staged, gathered):
    def stage(u):
        after_gather(act, gathered, u, u.per)
        nc.scalar.copy(K.rows[:, u.s, :], index[:, bass.ds(u.at(UNIT), UNIT)]).then_inc(staged, 1)
    return stage


def after_gather(eng, gathered, u, back=0):
    v = u.back(back)
    value = v.i * (16 * UNIT) + 16 * UNIT
    if isinstance(value, int) and value <= 0:
        return
    eng.wait_ge(gathered[u.s], value)


def gather_rows(nc, pool, K, g, table, width, staged, gathered, used, opened):
    def gather(u):
        after(pool, staged, u)
        after(pool, used, u, u.per)
        pool.sem_inc(opened, 1)
        for k in range(UNIT):
            pool.indirect_dma_start(out=K.ring[:, u.s * UNIT + k, 0:width], out_offset=None, in_=table,
                                    in_offset=bass.IndirectOffsetOnAxis(ap=K.rows[:, u.s, k:k + 1], axis=0),
                                    ).then_inc(gathered[u.s], 16)
    return gather


def member(nc, K, u, out=None):
    shape = [P, UNIT, P]
    return nc.vector.tensor_tensor(K.member[:, u.s % RING, :, :] if out is None else out, bcast(K.col[:, :], 1, UNIT),
                                   K.node[:, bass.ds(u.at(UNIT), UNIT)].unsqueeze(2).broadcast_to(shape), ALU.is_equal)


def attention_items(nc, g, K, x_table):
    with ExitStack() as ctx:
        M = Memory(nc, ctx, K, "attn")
        gathered = [M.sem(f"gathered{s}") for s in range(RING)]
        staged, member_ready, turned, turned_out = (M.sem(n) for n in ("staged", "member", "turned", "turned_out"))
        query_ready, product_ready, logit_ready, gate_ready = (M.sem(n) for n in ("query", "product", "logit", "gate"))
        gated_ready, summed, added, cleared = (M.sem(n) for n in ("gated", "summed", "added", "cleared"))
        member_b = M.sb("member_b", [P, RING, UNIT, P], BF16)
        member_t = M.sb("member_t", [P, 2, UNIT, P])
        product = M.sb("product", [P, UNIT, P])
        logit, gate = M.sb("logit", [P, 2, UNIT]), M.sb("gate", [P, 2, UNIT])
        gated = M.sb("gated", [P, 2, UNIT, P])
        view = lambda bank: bank[:, :].rearrange("p (k d) -> p k d", k=UNIT)
        turned_view = lambda u: K.bank[u.s % 2][:, :].bitcast(BF16)[:, 0:UNIT * P].rearrange("p (k d) -> p k d", k=UNIT)
        bank_q, bank_s = K.bank[2:4], K.bank[4:6]
        N = g.units
        opened = M.sem("opened")
        block = ctx.enter_context(nc.Block())

        @block.gpsimd
        def _(pool):
            pipeline(pool, N, RING, 0, stages(N, (0, gather_rows(nc, pool, K, g, x_table, D, staged, gathered, summed,
                                                                 opened))))

        @block.scalar
        def _(act):
            def copy_turned(u):
                after(act, turned, u)
                after(act, query_ready, u, 2)
                nc.scalar.copy(member_t[:, u.s % 2, :, :], turned_view(u)).then_inc(turned_out, 1)

            def sigmoid(u):
                after(act, logit_ready, u)
                after(act, gated_ready, u, 2)
                nc.scalar.activation(gate[:, u.s % 2, :], logit[:, u.s % 2, :], ACT.Sigmoid).then_inc(gate_ready, 1)

            pipeline(act, N, RING, 3, stages(N, (0, stage_rows(nc, act, K, g, K.src_row, staged, gathered)),
                                             (2, copy_turned), (3, sigmoid)))

        @block.vector
        def _(dve):
            nc.vector.memset(K.acc[:, :, :], 0.0).then_inc(cleared, 1)

            def members(u):
                after(dve, turned, u, RING)
                after(dve, gated_ready, u, RING)
                member(nc, K, u, member_b[:, u.s, :, :]).then_inc(member_ready, 1)

            def products(u):
                after(dve, query_ready, u)
                after_gather(dve, gathered, u)
                after(dve, logit_ready, u, 1)
                nc.vector.tensor_tensor(product[:, :, :], view(bank_q[u.s % 2]),
                                        K.ring[:, u.s * UNIT:(u.s + 1) * UNIT, 0:D], ALU.mult).then_inc(product_ready, 1)

            def logits(u):
                after(dve, product_ready, u)
                after(dve, gate_ready, u, 2)
                nc.vector.tensor_reduce(logit[:, u.s % 2, :], product[:, :, :], AX.X, ALU.add).then_inc(logit_ready, 1)

            def gates(u):
                after(dve, gate_ready, u)
                after(dve, summed, u, 2)
                nc.vector.tensor_tensor(gated[:, u.s % 2, :, :], member_b[:, u.s, :, :],
                                        gate[:, u.s % 2, :].unsqueeze(2).broadcast_to([P, UNIT, P]),
                                        ALU.mult).then_inc(gated_ready, 1)

            dve.wait_ge(cleared, 1)
            add = add_sums(nc, dve, K, g, summed, added, bank_s)
            pipeline(dve, N, RING, 4, stages(N, (4, add(0)), (0, members), (4, add(1)), (2, products), (4, add(2)),
                                             (2, logits), (4, add(3)), (2, gates)))

        @block.tensor
        def _(pe):
            def turn(u):
                after(pe, member_ready, u)
                after(pe, turned_out, u, 2)
                for k in range(UNIT):
                    last = nc.tensor.transpose(turned_view(u)[:, k, :], member_b[:, u.s, k, :], K.ident_b[:, :])
                last.then_inc(turned, 1)

            def queries(u):
                b = block_numbers(nc, mybir.EngineType.PE, K, g, u)
                after(pe, turned_out, u)
                after(pe, product_ready, u, 2)
                for k in range(UNIT):
                    last = nc.tensor.matmul(bank_q[u.s % 2][:, k * P:(k + 1) * P], member_t[:, u.s % 2, k, :],
                                            at_block(K.own, b[k], D), start=True, stop=True)
                last.then_inc(query_ready, 1)

            def sums(u):
                after(pe, gated_ready, u)
                after(pe, added, u, 2, per=UNIT)
                for k in range(UNIT):
                    last = nc.tensor.matmul(bank_s[u.s % 2][:, k * P:(k + 1) * P], gated[:, u.s % 2, k, :],
                                            K.ring[:, u.s * UNIT + k, 0:D], start=True, stop=True)
                last.then_inc(summed, 1)

            pipeline(pe, N, RING, 3, stages(N, (0, turn), (1, queries), (3, sums)))


def add_sums(nc, dve, K, g, summed, added, banks):
    registers = {}

    def add(k):
        def stage(u):
            if k == 0:
                registers[0] = block_numbers(nc, mybir.EngineType.DVE, K, g, u)
                after(dve, summed, u)
                after(dve, added, u, 1, per=UNIT)
            else:
                after(dve, added, u, per=UNIT, upto=k)
            into = at_block(K.acc, registers[0][k], D)
            nc.vector.tensor_tensor(into, into, banks[u.s % 2][:, k * P:(k + 1) * P], ALU.add).then_inc(added, 1)
        return stage
    return add


def sum_items(nc, g, K, name, table, index):
    with ExitStack() as ctx:
        M = Memory(nc, ctx, K, name)
        gathered = [M.sem(f"gathered{s}") for s in range(RING)]
        staged, member_ready, summed, added, cleared = (M.sem(n) for n in ("staged", "member", "summed", "added", "cleared"))
        banks = K.bank[0:2]
        N = g.units
        opened = M.sem("opened")
        block = ctx.enter_context(nc.Block())

        @block.gpsimd
        def _(pool):
            pipeline(pool, N, RING, 0, stages(N, (0, gather_rows(nc, pool, K, g, table, D, staged, gathered, summed,
                                                                 opened))))

        @block.scalar
        def _(act):
            pipeline(act, N, RING, 0, stages(N, (0, stage_rows(nc, act, K, g, index, staged, gathered))))

        @block.vector
        def _(dve):
            nc.vector.memset(K.acc[:, :, :], 0.0).then_inc(cleared, 1)

            def members(u):
                after(dve, summed, u, RING)
                member(nc, K, u).then_inc(member_ready, 1)

            dve.wait_ge(cleared, 1)
            add = add_sums(nc, dve, K, g, summed, added, banks)
            pipeline(dve, N, RING, 1, stages(N, (0, members), *((1, add(k)) for k in range(UNIT))))

        @block.tensor
        def _(pe):
            def sums(u):
                after(pe, member_ready, u)
                after_gather(pe, gathered, u)
                after(pe, added, u, 2, per=UNIT)
                for k in range(UNIT):
                    last = nc.tensor.matmul(banks[u.s % 2][:, k * P:(k + 1) * P], K.member[:, u.s, k, :],
                                            K.ring[:, u.s * UNIT + k, 0:D], start=True, stop=True)
                last.then_inc(summed, 1)

            pipeline(pe, N, RING, 0, stages(N, (0, sums)))


def softmax_items(nc, g, K, table):
    with ExitStack() as ctx:
        M = Memory(nc, ctx, K, "soft")
        N, R = g.units, LONG_RING
        C, W = UNIT * HEADS, HEADS * HZ
        gathered = [M.sem(f"gathered{s}") for s in range(R)]
        opened, taken = M.sem("opened"), M.sem("taken")
        staged, begun, scores_ready, starts_out, own_ready, turned_out, exp_ready = (
            M.sem(n) for n in ("staged", "begun", "scores", "starts_out", "own", "turned_out", "exp"))
        scores_turned, turned, run_back, tops_ready, picked, summed = (
            M.sem(n) for n in ("scores_turned", "turned", "run_back", "tops", "picked", "summed"))
        member_ready, run_ready, ends_ready, chain, max_ready, node_ready, edge_chain, over_ready = (
            M.sem(n) for n in ("member", "run_max", "ends", "chain", "max", "node", "edge_chain", "over"))
        message_ready, added, cleared = M.sem("message"), M.sem("added"), M.sem("cleared")
        bound_ready, leaky_ready, narrowed = M.sem("bound"), M.sem("leaky"), M.sem("narrowed")
        member_b = M.sb("member_b", [P, RING, UNIT, P], BF16)
        member_t = M.sb("member_t", [P, 2, UNIT, P], BF16)
        start_u = M.sb("start_u", [P, R, C])
        score_u = M.sb("score_u", [P, 2, C])
        starts_t = M.sb("starts_t", [C, 2, P])
        run_max = M.sb("run_max", [C, 2, P])
        run_end = M.sb("run_end", [P, 2, 3, UNIT, HEADS])
        far_end = M.sb("far_end", [P, R, UNIT, HEADS])
        minus_far = M.sb("minus_far", [1, C])
        tops = M.sb("tops", [P, HEADS, UNIT + 1])
        peak = M.sb("peak", [P, 2, HEADS, UNIT + 1])
        old = M.sb("old", [P, HEADS, UNIT])
        AS, AD, TOPMOST = 0, 1, 4
        node_own = M.sb("node_own", [P, g.blocks, TOPMOST, HEADS])
        node_u = M.sb("node_u", [P, RING, UNIT, TOPMOST + 3, HEADS])
        both = M.sb("both", [P, 2, 2, 2, C])
        leaky = M.sb("leaky", [P, 2, 2, C])
        over = M.sb("over", [P, 2, 2, C])
        power = M.sb("power", [P, 2, 2, C])
        message = M.sb("message", [P, 2, UNIT, W])
        scaled = M.sb("scaled", [P, W])
        RUN, TOP, EDGE = 2 * P, 2 * P + C, 2 * P + 2 * C
        small = lambda u: K.bank[4 + u.s % RING]
        turned_view = K.bank[0][:, :].bitcast(BF16)[:, 0:UNIT * P].rearrange("p (k d) -> p k d", k=UNIT)
        sum_of = lambda k: K.bank[1 + k // 3][:, (k % 3) * W:(k % 3 + 1) * W]
        top_of = lambda u: by_kh(small(u)[:, TOP:EDGE])
        edge_of = lambda u: small(u)[:, EDGE:EDGE + 2 * C].rearrange("p (k j h) -> p k j h", k=UNIT, j=2)
        by_kh = lambda a: a.rearrange("p (k h) -> p k h", h=HEADS)
        by_hk = lambda a: a.rearrange("p (h k) -> p h k", h=HEADS)
        rows_of = lambda u, c0, c1: K.ring[:, u.s * UNIT:(u.s + 1) * UNIT, c0:c1]
        block = ctx.enter_context(nc.Block())

        @block.gpsimd
        def _(pool):
            pipeline(pool, N, R, 0, stages(N, (0, gather_rows(nc, pool, K, g, table, ROW1, staged, gathered,
                                                              message_ready, opened))))

        @block.scalar
        def _(act):
            act.wait_ge(cleared, 3)
            rows = stage_rows(nc, act, K, g, K.src_row, staged, gathered)

            def inputs(u):
                rows(u)
                after(act, scores_turned, u, R)
                after(act, tops_ready, u, R)
                nc.scalar.activation(far_end[:, u.s, :, :], K.ends[:, bass.ds(u.at(UNIT), UNIT)].unsqueeze(2)
                                     .broadcast_to([P, UNIT, HEADS]), ACT.Copy, scale=FAR)
                nc.scalar.copy(by_kh(start_u[:, u.s, :]), K.starts[:, bass.ds(u.at(UNIT), UNIT)].unsqueeze(2)
                               .broadcast_to([P, UNIT, HEADS])).then_inc(begun, 1)

            def copy_scores(u):
                after_gather(act, gathered, u)
                after(act, scores_turned, u, 2)
                nc.scalar.copy(by_kh(score_u[:, u.s % 2, :]), rows_of(u, W, W + HEADS)).then_inc(scores_ready, 1)

            def copy_own(u):
                b = block_numbers(nc, mybir.EngineType.Activation, K, g, u)
                after(act, picked, u, RING)
                for k in range(UNIT):
                    last = nc.scalar.copy(node_u[:, u.s % RING, k, 0:TOPMOST, :].rearrange("p j h -> p (j h)"),
                                          node_own[:, bass.ds(b[k], 1), :, :].rearrange("p a j h -> p (a j h)"))
                last.then_inc(own_ready, 1)

            def copy_starts(u):
                after(act, scores_turned, u)
                after(act, run_ready, u, 2)
                nc.scalar.copy(starts_t[:, u.s % 2, :], small(u)[0:C, P:2 * P]).then_inc(starts_out, 1)

            def copy_turned(u):
                after(act, turned, u)
                after(act, picked, u, 2)
                nc.scalar.copy(member_t[:, u.s % 2, :, :], turned_view).then_inc(turned_out, 1)

            def narrow(u):
                after(act, member_ready, u)
                after(act, turned, u, RING)
                after(act, tops_ready, u, RING)
                nc.scalar.copy(member_b[:, u.s % RING, :, :], K.member[:, u.s % RING, :, :]).then_inc(narrowed, 1)

            def exponent(u):
                after(act, over_ready, u)
                after(act, added, u, 2, per=2 * UNIT)
                nc.scalar.activation(power[:, u.s % 2, :, :], over[:, u.s % 2, :, :], ACT.Exp).then_inc(exp_ready, 1)

            pipeline(act, N, R, 5, stages(
                N, (3, copy_scores), (3, copy_own), (3, copy_starts), (3, copy_turned), (5, exponent),
                (0, inputs), (2, narrow)))

        @block.tensor
        def _(pe):
            def turn_scores(u):
                after(pe, scores_ready, u)
                after(pe, begun, u)
                after(pe, over_ready, u, RING)
                nc.tensor.transpose(small(u)[0:C, 0:P], score_u[:, u.s % 2, :], K.ident[:, :])
                nc.tensor.transpose(small(u)[0:C, P:2 * P], start_u[:, u.s, :],
                                    K.ident[:, :]).then_inc(scores_turned, 1)

            def turn_runs(u):
                after(pe, run_ready, u)
                pe.sem_inc(taken, 1)
                nc.tensor.transpose(small(u)[:, RUN:TOP], run_max[:, u.s % 2, :],
                                    K.ident[0:C, 0:C]).then_inc(run_back, 1)

            def item_tops(u):
                after(pe, ends_ready, u, per=3)
                after(pe, narrowed, u)
                nc.tensor.matmul(small(u)[:, TOP:EDGE], upper(K.ones[0:1, :]), upper(minus_far[:, :]), start=True,
                                 stop=False)
                for k in range(UNIT):
                    top, ones = top_of(u)[:, k, :], member_b[:, u.s % RING, k, :]
                    nc.tensor.matmul(top, ones, upper(far_end[:, u.s, k, :]), start=False, stop=False)
                    for j in range(3):
                        last = nc.tensor.matmul(top, ones, upper(run_end[:, u.s % 2, j, k, :]), start=False,
                                                stop=(k == UNIT - 1 and j == 2))
                last.then_inc(tops_ready, 1)

            def pick(u):
                after(pe, max_ready, u, per=4)
                after(pe, turned_out, u)
                for k in range(UNIT):
                    for j in range(3):
                        last = nc.tensor.matmul(edge_of(u)[:, k, :, :], member_t[:, u.s % 2, k, :],
                                                upper(node_u[:, u.s % RING, k, AD + j:TOPMOST + j + 1:TOPMOST - AD, :]),
                                                start=(j == 0), stop=(j == 2))
                last.then_inc(picked, 1)

            def turn(u):
                after(pe, narrowed, u)
                after(pe, turned_out, u, 1)
                for k in range(UNIT):
                    last = nc.tensor.transpose(turned_view[:, k, :], member_b[:, u.s % RING, k, :], K.ident_b[:, :])
                last.then_inc(turned, 1)

            def sums(u):
                after(pe, message_ready, u)
                after(pe, added, u, 1, per=2 * UNIT)
                for k in range(UNIT):
                    last = nc.tensor.matmul(sum_of(k), K.member[:, u.s % RING, k, :], message[:, u.s % 2, k, :],
                                            start=True, stop=True)
                last.then_inc(summed, 1)

            pipeline(pe, N, R, 4, stages(
                N, (1, turn_scores), (4, sums), (1, turn_runs), (2, pick), (1, item_tops), (0, turn)))

        @block.vector
        def _(dve):
            def run_maxima(u):
                after(dve, starts_out, u)
                after(dve, run_back, u, 2)
                nc.vector.tensor_tensor_scan(run_max[:, u.s % 2, :], starts_t[:, u.s % 2, :], small(u)[0:C, 0:P],
                                             -FAR, ALU.add, ALU.max).then_inc(run_ready, 1)

            def run_ends(u):
                ends = K.ends[:, bass.ds(u.at(UNIT), UNIT)]
                after(dve, tops_ready, u, 2)
                after(dve, run_back, u)
                nc.vector.tensor_tensor(run_end[:, u.s % 2, 0, :, :], by_kh(small(u)[:, RUN:TOP]),
                                        ends.unsqueeze(2).broadcast_to([P, UNIT, HEADS]),
                                        ALU.mult).then_inc(ends_ready, 1)

            def leave(u, n, sem, part, first, per):
                after(dve, sem, u, per=per, upto=first + n - 1)
                nc.vector.tensor_tensor(part[n], part[n - 1], upper(part[n - 1]), ALU.subtract).then_inc(sem, 1)

            def run_left(n):
                return lambda u: leave(u, n, ends_ready, [run_end[:, u.s % 2, j, :, :] for j in range(3)], 1, 3)

            own_of = lambda u: node_u[:, u.s % RING, :, :, :]
            own_hk = lambda u, j: own_of(u)[:, :, j, :].rearrange("p k h -> p h k")
            cut_of = lambda u: K.cut[:, bass.ds(u.at(), 1), :]

            def tops_in(u):
                nc.vector.tensor_copy(tops[:, :, 0], peak[:, 1 - u.s % 2, :, UNIT]).then_inc(chain, 1)

            def tops_self(u):
                after(dve, tops_ready, u)
                after(dve, own_ready, u)
                nc.vector.tensor_tensor(tops[:, :, 1:UNIT + 1], top_of(u).rearrange("p k h -> p h k"), own_hk(u, AS),
                                        ALU.max).then_inc(chain, 1)

            def peaks(u):
                after(dve, chain, u, per=4, upto=2)
                nc.vector.tensor_tensor_scan(peak[:, u.s % 2, :, :].rearrange("p h k -> p (h k)"),
                                             cut_of(u).rearrange("p a c -> p (a c)"),
                                             tops[:, :, :].rearrange("p h k -> p (h k)"), -FAR, ALU.add,
                                             ALU.max).then_inc(max_ready, 1)

            def peaks_out(u):
                after(dve, max_ready, u, per=4, upto=1)
                nc.vector.tensor_tensor(own_hk(u, TOPMOST), peak[:, u.s % 2, :, 1:UNIT + 1], own_hk(u, AD),
                                        ALU.add).then_inc(max_ready, 1)
                nc.vector.tensor_tensor(old[:, :, :], peak[:, u.s % 2, :, 0:UNIT],
                                        cut_of(u).rearrange("p a (h k) -> p (a h) k", h=HEADS)[:, :, 1:UNIT + 1],
                                        ALU.add).then_inc(chain, 1)
                after(dve, leaky_ready, u, 2)
                nc.vector.tensor_tensor(by_hk(both[:, u.s % 2, 0, 1, :]), peak[:, u.s % 2, :, 1:UNIT + 1],
                                        own_hk(u, AD), ALU.add).then_inc(node_ready, 1)

            peak_parts = lambda u: [own_of(u)[:, :, TOPMOST + j, :] for j in range(3)]

            def peaks_left(u):
                leave(u, 1, max_ready, peak_parts(u), 2, 4)
                after(dve, chain, u, per=4, upto=3)
                nc.vector.tensor_tensor(old[:, :, :], old[:, :, :], own_hk(u, AS), ALU.max).then_inc(chain, 1)

            def peaks_last(u):
                leave(u, 2, max_ready, peak_parts(u), 2, 4)
                after(dve, chain, u, per=4)
                nc.vector.tensor_tensor(by_hk(both[:, u.s % 2, 0, 0, :]), old[:, :, :], own_hk(u, AD),
                                        ALU.add).then_inc(node_ready, 1)

            def edge_values(u):
                after(dve, picked, u)
                edge = edge_of(u)
                nc.vector.tensor_tensor(by_kh(both[:, u.s % 2, 1, 0, :]), rows_of(u, W, W + HEADS), edge[:, :, 0, :],
                                        ALU.add).then_inc(edge_chain, 1)
                nc.vector.tensor_copy(by_kh(both[:, u.s % 2, 1, 1, :]), edge[:, :, 1, :]).then_inc(edge_chain, 1)

            def edge_bound(u):
                after(dve, edge_chain, u, per=2)
                nc.vector.tensor_tensor(both[:, u.s % 2, 1, 0, :], both[:, u.s % 2, 1, 0, :], both[:, u.s % 2, 1, 1, :],
                                        ALU.min).then_inc(bound_ready, 1)

            def edge_leaky(u):
                after(dve, bound_ready, u)
                after(dve, node_ready, u, per=2)
                nc.vector.scalar_tensor_tensor(leaky[:, :, :, :], both[:, u.s % 2, :, :, :], SLOPE,
                                               both[:, u.s % 2, :, :, :], ALU.mult, ALU.max).then_inc(leaky_ready, 1)

            def overs(u):
                after(dve, leaky_ready, u)
                after(dve, exp_ready, u, 2)
                nc.vector.tensor_tensor(over[:, u.s % 2, :, :], leaky[:, :, 0, :], leaky[:, :, 1, :],
                                        ALU.subtract).then_inc(over_ready, 1)

            def messages(u):
                after(dve, exp_ready, u)
                after(dve, summed, u, 2)
                nc.vector.tensor_tensor(
                    message[:, u.s % 2, :, :].rearrange("p k (h z) -> p k h z", h=HEADS),
                    rows_of(u, 0, W).rearrange("p k (h z) -> p k h z", h=HEADS),
                    by_kh(power[:, u.s % 2, 1, :]).unsqueeze(3).broadcast_to([P, UNIT, HEADS, HZ]),
                    ALU.mult).then_inc(message_ready, 1)

            registers = {}

            def blocks(u):
                if u.s % 2 == 0:
                    registers[0] = block_numbers(nc, mybir.EngineType.DVE, K, g, u, 2)

            def block_of(u, k):
                return registers[0][u.s % 2 * UNIT + k]

            def rescale(k):
                def stage(u):
                    if k == 0:
                        after(dve, added, u, 1, per=2 * UNIT)
                        after(dve, exp_ready, u)
                    else:
                        after(dve, added, u, per=2 * UNIT, upto=2 * k)
                    heads = lambda a: a.rearrange("p (h z) -> p h z", h=HEADS)
                    nc.vector.tensor_tensor(heads(scaled[:, :]), heads(at_block(K.acc, block_of(u, k), W)),
                                            by_hk(power[:, u.s % 2, 0, :])[:, :, k].unsqueeze(2)
                                            .broadcast_to([P, HEADS, HZ]), ALU.mult).then_inc(added, 1)
                return stage

            def add(k):
                def stage(u):
                    if k == 0:
                        after(dve, summed, u)
                    after(dve, added, u, per=2 * UNIT, upto=2 * k + 1)
                    nc.vector.tensor_tensor(at_block(K.acc, block_of(u, k), W), scaled[:, :], sum_of(k),
                                            ALU.add).then_inc(added, 1)
                return stage

            def members(u):
                after(dve, summed, u, RING)
                member(nc, K, u).then_inc(member_ready, 1)

            nc.vector.memset(peak[:, 1, :, :], -FAR)
            nc.vector.memset(minus_far[:, :], -FAR)
            split = [node_own[:, :, AD + j, :] for j in range(3)]
            nc.vector.tensor_copy(node_own[:, :, AS, :], K.own[:, :, 0:HEADS])
            nc.vector.tensor_copy(split[0], K.own[:, :, HEADS:2 * HEADS]).then_inc(cleared, 1)
            for j in range(2):
                dve.wait_ge(cleared, j + 1)
                nc.vector.tensor_tensor(split[j + 1], split[j], upper(split[j]), ALU.subtract).then_inc(cleared, 1)
            pipeline(dve, N, R, 4, stages(
                N, (4, blocks), (2, tops_in), (3, edge_values), (1, run_maxima),
                (2, tops_self), (3, edge_bound), (4, rescale(0)), (2, peaks), (2, peaks_out),
                (3, edge_leaky), (4, add(0)), (2, peaks_left), (4, rescale(1)), (3, overs),
                (2, peaks_last), (4, add(1)), (1, run_ends), (0, members), (1, run_left(1)),
                (4, rescale(2)), (1, run_left(2)), (4, add(2)), (3, messages), (4, rescale(3)),
                (4, add(3))))


ATTENTION, SOFTMAX, GIN, RELATIONS, LAST = range(5)


def add_bias(nc, K, out, bias):
    for j in range(3):
        last = nc.tensor.matmul(out, upper(K.ones[0:1, :]), upper(bias[0:1, j, :]), start=False, stop=(j == 2))
    return last


def node_pass(nc, g, K, kind, name, table, affine=None):
    with ExitStack() as ctx:
        M = Memory(nc, ctx, K, name)
        N, R = g.blocks, LONG_RING
        inner = kind in (ATTENTION, GIN)
        tables = kind in (ATTENTION, GIN, RELATIONS)
        first = kind in (ATTENTION, SOFTMAX, GIN)
        second = kind != RELATIONS
        rel_w = K.rel_w[0 if kind == GIN else 1]
        width = ROW1 if kind == ATTENTION else REL * D
        S = {n: M.sem(n) for n in ("input", "turned", "turned_out", "product", "hidden", "product2", "layer", "stats1",
                                   "root1", "norm1", "joined", "stats2", "root2", "norm2", "row_turned",
                                   "row_turned_out", "rows", "rows_act", "rows_dve", "kept")
             if not (n.endswith("1") and not first)}
        stored = [M.sem("stored0"), M.sem("stored1")]
        taken, taken_pool, taken_sp = M.sem("taken"), M.sem("taken_pool"), M.sem("taken_sp")
        joins = {ATTENTION: 2, SOFTMAX: 2, GIN: 3}.get(kind, 1)
        norms = {1: 3, 2: 2}
        row_stored = [M.sem(f"row_stored{s}") for s in range(R)] if kind in (LAST, SOFTMAX) else None
        MK = {ATTENTION: 2, SOFTMAX: 1, GIN: 2, RELATIONS: 1, LAST: 0}[kind]
        N2 = 2 if kind == LAST else MK + 3
        RT = MK + 1 if kind == RELATIONS else N2
        uses = lambda u: u.i * (u.per // 2) + u.s // 2
        z_in = M.sb("z_in", [P, R, D])
        z_t = M.sb("z_t", [P, 2, D])
        hidden = M.sb("hidden", [P, 2, D])
        layer = M.sb("layer", [P, R, D])
        norm = M.sb("norm", [P, R, D])
        joined = M.sb("joined", [P, R, D])
        fresh = M.sb("fresh", [P, R, D])
        stats = [M.sb(f"stats{j}", [P, R, 6]) for j in range(2)]
        moments = [M.sb(f"moments{j}", [P, R, 2]) for j in range(2)]
        root = [M.sb(f"root{j}", [P, R, 1]) for j in range(2)]
        scale = [M.sb(f"scale{j}", [P, R, 1]) for j in range(2)]
        inv_z = M.sb("inv_z", [P, R, 2, HEADS])
        x_t = M.sb("x_t", [P, 2, D])
        rows = M.sb("rows", [P, 2, width])
        block = ctx.enter_context(nc.Block())

        def after_stored(eng, u):
            value = uses(u) * 16
            if not (isinstance(value, int) and value <= 0):
                eng.wait_ge(stored[u.s % 2], value)

        def moments_of(dve, j, src, u):
            after(dve, S[f"norm{j + 1}"], u, R, per=norms[j + 1])
            after(dve, S[f"root{j + 1}"], u, R)
            nc.vector.bn_stats(stats[j][:, u.s, :], src).then_inc(S[f"stats{j + 1}"], 1)

        def moments_out(dve, j, u):
            after(dve, S[f"stats{j + 1}"], u, per=2, upto=1)
            dve.sem_inc(taken, 1)
            nc.vector.bn_aggr(moments[j][:, u.s, :], stats[j][:, u.s, :]).then_inc(S[f"stats{j + 1}"], 1)

        def root_of(act, j, u):
            after(act, S[f"stats{j + 1}"], u, per=2)
            after(act, S[f"norm{j + 1}"], u, R, per=norms[j + 1])
            nc.scalar.activation(root[j][:, u.s, :], moments[j][:, u.s, 1:2], ACT.Sqrt,
                                 bias=K.eps[:, :]).then_inc(S[f"root{j + 1}"], 1)

        def invert(dve, j, u):
            after(dve, S[f"root{j + 1}"], u)
            nc.vector.reciprocal(scale[j][:, u.s, :], root[j][:, u.s, :]).then_inc(S[f"norm{j + 1}"], 1)

        def normalize(dve, j, out, src, u):
            sem = S[f"norm{j + 1}"]
            after(dve, sem, u, per=norms[j + 1], upto=1)
            nc.vector.tensor_scalar(out, src, moments[j][:, u.s, 0:1], scale[j][:, u.s, :], ALU.subtract,
                                    ALU.mult).then_inc(sem, 1)

        @block.vector
        def _(dve):
            def enter(u):
                if kind == GIN:
                    after(dve, S["turned"], u, R)
                    nc.vector.scalar_tensor_tensor(z_in[:, u.s, :], blk(K.x, u, D), K.eta1[:, :], blk(K.acc, u, D),
                                                   ALU.mult, ALU.add).then_inc(S["input"], 1)
                if kind == SOFTMAX:
                    after(dve, S["layer"], u, R, per=2)
                    z = K.acc[:, bass.ds(u.at(), 1), 0:HEADS * HZ].rearrange("p a (h z) -> p (a h) z", h=HEADS)[:, :, HC]
                    nc.vector.tensor_scalar(inv_z[:, u.s, 0, :], z, SOFTMAX_EPS, None, ALU.add).then_inc(S["input"], 1)
                if kind == RELATIONS:
                    after(dve, S["layer"], u, R)
                    nc.vector.tensor_tensor(joined[:, u.s, :], blk(K.acc, u, D), blk(K.own, u, D),
                                            ALU.add).then_inc(S["input"], 1)
                if kind == LAST:
                    after(dve, S["norm2"], u, R, per=2)
                    nc.vector.tensor_tensor(joined[:, u.s, :], blk(K.acc, u, D), blk(K.own, u, D),
                                            ALU.add).then_inc(S["joined"], 1)

            def enter_more(u):
                if kind == SOFTMAX:
                    after(dve, S["input"], u, per=2, upto=1)
                    nc.vector.reciprocal(inv_z[:, u.s, 1, :], inv_z[:, u.s, 0, :]).then_inc(S["input"], 1)

            def make_layer(u):
                if kind == ATTENTION:
                    after(dve, S["product"], u)
                    nc.vector.tensor_tensor(layer[:, u.s, :], K.bank[1 + u.s % 2][:, 0:D], blk(K.x, u, D),
                                            ALU.add).then_inc(S["layer"], 1)
                if kind == SOFTMAX:
                    after(dve, S["input"], u, per=2)
                    acc = K.acc[:, bass.ds(u.at(), 1), 0:HEADS * HZ].rearrange("p a (h z) -> p (a h) z", h=HEADS)
                    nc.vector.tensor_tensor(z_in[:, u.s, :].rearrange("p (h c) -> p h c", h=HEADS), acc[:, :, 0:HC],
                                            inv_z[:, u.s, 1, :].unsqueeze(2).broadcast_to([P, HEADS, HC]),
                                            ALU.mult).then_inc(S["layer"], 1)
                if kind == RELATIONS:
                    after(dve, S["input"], u)
                    after(dve, S["row_turned"], u, R)
                    nc.vector.scalar_tensor_tensor(z_in[:, u.s, :], joined[:, u.s, :], 0.0, K.rel_b1[:, :], ALU.max,
                                                   ALU.add).then_inc(S["layer"], 1)

            def make_more(u):
                if kind == SOFTMAX:
                    after(dve, S["layer"], u, per=2, upto=1)
                    nc.vector.tensor_tensor(layer[:, u.s, :], z_in[:, u.s, :], blk(K.own, u, D, 2 * HEADS),
                                            ALU.add).then_inc(S["layer"], 1)

            def stats_first(u):
                if first:
                    after(dve, S["layer"], u, per=2 if kind == SOFTMAX else 1)
                    moments_of(dve, 0, layer[:, u.s, :], u)

            def stats_first_out(u):
                if first:
                    moments_out(dve, 0, u)

            def invert_first(u):
                if first:
                    invert(dve, 0, u)

            def invert_second(u):
                if second:
                    if kind in (ATTENTION, GIN):
                        after(dve, S["kept"], u, R)
                    invert(dve, 1, u)

            def stats_second_out(u):
                if second:
                    moments_out(dve, 1, u)

            def norm_first(u):
                if first:
                    after(dve, S["joined"], u, R, per=joins)
                    normalize(dve, 0, norm[:, u.s, :], layer[:, u.s, :], u)

            def weigh(u):
                if first:
                    after(dve, S["norm1"], u, per=3, upto=2)
                    nc.vector.tensor_tensor(norm[:, u.s, :], norm[:, u.s, :], affine[0][:, :],
                                            ALU.mult).then_inc(S["norm1"], 1)

            def stats_second(u):
                if second:
                    after(dve, S["joined"], u, per=joins)
                    moments_of(dve, 1, joined[:, u.s, :], u)

            def norm_second(u):
                if second:
                    if kind == LAST:
                        after_row_stored(dve, u)
                    if tables:
                        after(dve, S["row_turned"], u, R)
                    if kind == GIN:
                        after(dve, S["rows_dve"], u, R, per=2)
                    normalize(dve, 1, blk(K.x, u, D) if kind == SOFTMAX else fresh[:, u.s, :], joined[:, u.s, :], u)

            def after_row_stored(eng, u):
                value = u.i * 16
                if not (isinstance(value, int) and value <= 0):
                    eng.wait_ge(row_stored[u.s], value)

            def copy_rows(u):
                if kind in (GIN, RELATIONS):
                    after(dve, S["rows"], u, per=3)
                    after_stored(dve, u)
                    nc.vector.tensor_copy(rows[:, u.s % 2, 4 * D:8 * D], K.bank[5][:, :]).then_inc(S["rows_dve"], 1)
                    nc.vector.tensor_tensor(blk(K.own, u, D), K.bank[6 + u.s % 2][:, 0:D],
                                            fresh[:, u.s, :] if kind == GIN else blk(K.x, u, D),
                                            ALU.add).then_inc(S["rows_dve"], 1)

            pipeline(dve, N, R, RT + 2, stages(
                N, (N2, invert_second), (0, enter), (MK + 1, invert_first), (MK + 1, norm_first), (N2, norm_second),
                (N2 - 1, stats_second), (MK + 1, weigh), (MK, make_layer), (N2 - 1, stats_second_out),
                (MK, make_more), (RT + 2, copy_rows), (MK, stats_first), (0, enter_more),
                (MK, stats_first_out)))

        @block.gpsimd
        def _(pool):
            def join(u):
                j = S["joined"]
                after(pool, S["norm1"], u, per=3)
                after(pool, S["stats2"], u, R, per=2)
                after(pool, S["norm2"], u, R, per=2)
                o = joined[:, u.s, :]
                nc.gpsimd.tensor_tensor(o, norm[:, u.s, :], affine[1][:, :], ALU.add).then_inc(j, 1)
                for n in range(1, joins):
                    after(pool, j, u, per=joins, upto=n)
                    pool.sem_inc(taken_pool, 1)
                    nc.gpsimd.tensor_tensor(o, o, blk(K.x, u, D), ALU.add).then_inc(j, 1)

            def bring(u):
                if kind == ATTENTION:
                    after(pool, S["turned"], u, R)
                    pool.sem_inc(taken_pool, 1)
                    nc.gpsimd.tensor_copy(z_in[:, u.s, :], blk(K.acc, u, D)).then_inc(S["input"], 1)

            if first:
                pipeline(pool, N, R, MK + 1, stages(N, (0, bring), (MK + 1, join)))

        @block.scalar
        def _(act):
            def copy_turned(u):
                if inner:
                    after(act, S["turned"], u)
                    after(act, S["product"], u, 2)
                    nc.scalar.copy(z_t[:, u.s % 2, :], K.bank[0][:, 0:D]).then_inc(S["turned_out"], 1)

            def hide(u):
                if kind == GIN:
                    after(act, S["product"], u)
                    after(act, S["product2"], u, 2)
                    nc.scalar.activation(hidden[:, u.s % 2, :], K.bank[1][:, 0:D], ACT.Relu,
                                         bias=K.gin_b1[:, :]).then_inc(S["hidden"], 1)

            def show(u):
                if kind == GIN:
                    after(act, S["product2"], u)
                    after(act, S["norm1"], u, R, per=3)
                    nc.scalar.activation(layer[:, u.s, :], K.bank[2][:, 0:D], ACT.Relu).then_inc(S["layer"], 1)

            def keep(u):
                if kind in (ATTENTION, GIN):
                    after(act, S["norm2"], u, per=2)
                    if kind == ATTENTION:
                        after(act, S["layer"], u)
                    nc.scalar.copy(blk(K.x, u, D), fresh[:, u.s, :]).then_inc(S["kept"], 1)

            def root_first(u):
                if first:
                    root_of(act, 0, u)

            def root_second(u):
                if second:
                    root_of(act, 1, u)

            def copy_row(u):
                if tables:
                    after(act, S["row_turned"], u)
                    after(act, S["rows"], u, 2, per=3 if kind != ATTENTION else 1)
                    nc.scalar.copy(x_t[:, u.s % 2, :], K.bank[3][:, 0:D]).then_inc(S["row_turned_out"], 1)

            def copy_rows(u):
                if kind == ATTENTION:
                    bank = K.bank[4 + u.s % 2]
                    after(act, S["rows"], u)
                    after_stored(act, u)
                    nc.scalar.copy(rows[:, u.s % 2, :], bank[:, 0:ROW1]).then_inc(S["rows_act"], 1)
                    nc.scalar.copy(blk(K.acc, u, HEADS * HZ), bank[:, 0:HEADS * HZ]).then_inc(S["rows_act"], 1)
                    nc.scalar.copy(blk(K.own, u, OWN1), bank[:, ROW1 - HEADS:WIDE1]).then_inc(S["rows_act"], 1)
                elif tables:
                    after(act, S["rows"], u, per=3, upto=1)
                    after_stored(act, u)
                    nc.scalar.copy(rows[:, u.s % 2, 0:4 * D], K.bank[4][:, :]).then_inc(S["rows_act"], 1)

            pipeline(act, N, R, RT + 1, stages(
                N, (0, copy_turned), (N2 - 1, root_second), (MK, root_first), (RT, copy_row), (1, show),
                (RT + 1, copy_rows), (0, hide), (RT, keep)))

        @block.tensor
        def _(pe):
            def turn(u):
                if inner:
                    after(pe, S["input"], u)
                    after(pe, S["turned_out"], u, 1)
                    nc.tensor.transpose(K.bank[0][:, 0:D], z_in[:, u.s, :], K.ident[:, :]).then_inc(S["turned"], 1)

            def multiply(u):
                if kind == ATTENTION:
                    after(pe, S["turned_out"], u)
                    after(pe, S["layer"], u, 2)
                    out = K.bank[1 + u.s % 2][:, 0:D]
                    nc.tensor.matmul(out, z_t[:, u.s % 2, :], K.vo[:, :], start=True, stop=False)
                    add_bias(nc, K, out, K.b0).then_inc(S["product"], 1)
                if kind == GIN:
                    after(pe, S["turned_out"], u)
                    after(pe, S["hidden"], u, 1)
                    nc.tensor.matmul(K.bank[1][:, 0:D], K.gin_w1[:, :], z_t[:, u.s % 2, :], start=True,
                                     stop=True).then_inc(S["product"], 1)

            def multiply2(u):
                if kind == GIN:
                    after(pe, S["hidden"], u)
                    after(pe, S["layer"], u, 1)
                    nc.tensor.matmul(K.bank[2][:, 0:D], hidden[:, u.s % 2, :], K.gin_w2[:, :], start=True, stop=False)
                    add_bias(nc, K, K.bank[2][:, 0:D], K.gin_b2).then_inc(S["product2"], 1)

            def turn_row(u):
                if tables:
                    after(pe, S["layer"] if kind == RELATIONS else S["norm2"], u, per=1 if kind == RELATIONS else 2)
                    after(pe, S["row_turned_out"], u, 1)
                    src = z_in[:, u.s, :] if kind == RELATIONS else fresh[:, u.s, :]
                    nc.tensor.transpose(K.bank[3][:, 0:D], src, K.ident[:, :]).then_inc(S["row_turned"], 1)

            def make_rows(u):
                if kind == ATTENTION:
                    bank = K.bank[4 + u.s % 2]
                    after(pe, S["row_turned_out"], u)
                    after(pe, S["rows_act"], u, 2, per=3)
                    nc.tensor.matmul(bank[:, 0:WIDE1], x_t[:, u.s % 2, :], K.w1[:, :], start=True, stop=False)
                    add_bias(nc, K, bank[:, 0:WIDE1], K.b1).then_inc(S["rows"], 1)
                elif tables:
                    after(pe, S["row_turned_out"], u)
                    after(pe, S["rows_act"], u, 1)
                    nc.tensor.matmul(K.bank[4][:, :], x_t[:, u.s % 2, :], rel_w[:, 0:4, :], start=True,
                                     stop=True).then_inc(S["rows"], 1)
                    after(pe, S["rows_dve"], u, 1, per=2)
                    nc.tensor.matmul(K.bank[5][:, :], x_t[:, u.s % 2, :], rel_w[:, 4:8, :], start=True,
                                     stop=True).then_inc(S["rows"], 1)
                    own = K.bank[6 + u.s % 2][:, 0:D]
                    last = nc.tensor.matmul(own, x_t[:, u.s % 2, :], rel_w[:, REL, :], start=True, stop=(kind == GIN))
                    if kind == RELATIONS:
                        last = add_bias(nc, K, own, K.rel_b2)
                    last.then_inc(S["rows"], 1)

            if kind == ATTENTION:
                pipeline(pe, N, R, RT + 1, stages(
                    N, (0, turn), (RT + 1, make_rows), (RT, turn_row), (0, multiply)))
            else:
                pipeline(pe, N, R, RT + 1, stages(
                    N, (0, turn), (1, multiply2), (RT, turn_row), (0, multiply), (RT + 1, make_rows)))

        @block.sync
        def _(sp):
            def store(u):
                if tables:
                    after(sp, S["rows_act"], u, per=3 if kind == ATTENTION else 1)
                    if kind != ATTENTION:
                        sp.sem_inc(taken_sp, 1)
                        after(sp, S["rows_dve"], u, per=2)
                    sp.sem_inc(taken_sp, 1)
                    sp.dma_start(table[bass.ds(u.at(P), P), :], rows[:, u.s % 2, :]).then_inc(stored[u.s % 2], 16)
                if kind == SOFTMAX:
                    after(sp, S["norm2"], u, per=2)
                    sp.sem_inc(taken_sp, 1)
                    sp.dma_start(table[bass.ds(u.at(P), P), :], blk(K.x, u, D)).then_inc(row_stored[u.s], 16)
                if kind == LAST:
                    after(sp, S["norm2"], u, per=2)
                    sp.sem_inc(taken_sp, 1)
                    n = g.tail if isinstance(u.i, int) and u.at() == N - 1 else P
                    sp.dma_start(table[bass.ds(u.at(P), n), :], fresh[0:n, u.s, :]).then_inc(row_stored[u.s], 16)

            pipeline(sp, N, R, 0, stages(N, (0, store)))
            if row_stored:
                for s in range(R):
                    sp.wait_ge(row_stored[s], 16 * ((N - s + R - 1) // R))
            else:
                for s in range(2):
                    sp.wait_ge(stored[s], 16 * ((N - s + 1) // 2))


class Kept:

    def __init__(self, nc, ctx, g):
        def sb(name, shape, dt=F32):
            return ctx.enter_context(nc.sbuf_tensor(name, shape, dt))

        self.semaphores = []
        self.lists_loaded, self.x_loaded = nc.alloc_semaphore("lists_loaded"), nc.alloc_semaphore("x_loaded")
        NB, NI = g.blocks, g.items
        self.bank = [ctx.enter_context(nc.psum_tensor(f"bank{j}", [P, 512], F32)) for j in range(8)]
        self.x = sb("x_nodes", [P, NB, D])
        self.own = sb("own", [P, NB, OWN1])
        self.acc = sb("acc", [P, NB, HEADS * HZ])
        self.node = sb("node", [P, NI])
        self.src_row = sb("src_row", [P, NI], I32)
        self.rel_row = sb("rel_row", [P, NI], I32)
        self.ends = sb("ends", [P, NI])
        self.starts = sb("starts", [P, NI])
        self.cut = sb("cut", [P, g.units, HEADS * (UNIT + 1)])
        self.block_no = sb("block_no", [1, NI], I32)
        self.rows = sb("row_numbers", [P, LONG_RING, UNIT], I32)
        self.ring = sb("ring", [P, LONG_RING * UNIT, ROW1])
        self.member = sb("member", [P, RING, UNIT, P])
        self.ident, self.col, self.part = sb("ident", [P, P]), sb("col", [P, P]), sb("part", [P, 1])
        self.ident_b = sb("ident_b", [P, P], BF16)
        self.ones, self.eps = sb("ones", [P, P]), sb("eps", [P, 1])
        self.qk, self.vo = sb("qk", [P, P]), sb("vo", [P, P])
        self.w1, self.b1 = sb("w1", [P, WIDE1]), sb("b1", [1, 3, WIDE1])
        self.b0 = sb("b0", [1, 3, D])
        self.gin_w1, self.gin_w2 = sb("gin_w1", [P, D]), sb("gin_w2", [P, D])
        self.gin_b1, self.gin_b2 = sb("gin_b1", [P, 1]), sb("gin_b2", [1, 3, D])
        self.eta1 = sb("eta1", [P, 1])
        self.affine = [sb(f"affine{j}", [P, D]) for j in range(6)]
        self.rel_w = [sb(f"rel_w{j}", [P, REL + 1, D]) for j in range(2)]
        self.rel_b1, self.rel_b2 = sb("rel_b1", [P, D]), sb("rel_b2", [1, 3, D])


def gnn(nc, W, out, stop=99):
    g = Graph(W["x"].shape[0], W["src"].shape[0])
    rows = g.blocks * P
    with ExitStack() as ctx:
        K = Kept(nc, ctx, g)
        soft_table = nc.dram_tensor("soft_table", (rows, ROW1), F32).ap()
        records = nc.dram_tensor("records", (g.groups * P * P, 3), I32).ap()
        gin_table = nc.dram_tensor("gin_table", (rows, D), F32).ap()
        rel_tables = [nc.dram_tensor(f"rel_table{j}", (rows, REL * D), F32).ap() for j in range(2)]
        by_relation = lambda t: t.rearrange("n (r c) -> (n r) c", r=REL)
        parts = [
            lambda: load_and_fold(nc, g, K, W),
            lambda: order_edges(nc, g, K, records),
            lambda: build_graph(nc, g, K, W["x"]),
            lambda: query_rows(nc, g, K),
            lambda: attention_items(nc, g, K, W["x"]),
            lambda: node_pass(nc, g, K, ATTENTION, "attn_nodes", soft_table, K.affine[0:2]),
            lambda: softmax_items(nc, g, K, soft_table),
            lambda: node_pass(nc, g, K, SOFTMAX, "soft_nodes", gin_table, K.affine[2:4]),
            lambda: sum_items(nc, g, K, "gin", gin_table, K.src_row),
            lambda: node_pass(nc, g, K, GIN, "gin_nodes", rel_tables[0], K.affine[4:6]),
            lambda: sum_items(nc, g, K, "rel1", by_relation(rel_tables[0]), K.rel_row),
            lambda: node_pass(nc, g, K, RELATIONS, "rel1_nodes", rel_tables[1]),
            lambda: sum_items(nc, g, K, "rel2", by_relation(rel_tables[1]), K.rel_row),
            lambda: node_pass(nc, g, K, LAST, "rel2_nodes", out),
        ]
        for part in parts[:stop]:
            part()
            nc.clear_and_free_semaphores(K.semaphores)
            nc.all_engine_barrier()
            K.semaphores = []
        return K


_INS = ["x", "src", "dst", "edge_type_8", "L0_gnn_Wq", "L0_gnn_Wk", "L0_gnn_Wv", "L0_gnn_Wo", "L0_gnn_bo",
        "L0_gnn_gamma", "L0_gnn_beta", "L1_gnn_W", "L1_gnn_att_src", "L1_gnn_att_dst", "L1_gnn_gat_bias",
        "L1_gnn_skip_W", "L1_gnn_skip_b", "L1_gnn_ln_g", "L1_gnn_ln_b", "L2_gnn_W1", "L2_gnn_b1", "L2_gnn_W2",
        "L2_gnn_b2", "L2_gnn_eta", "L2_gnn_ln_gamma", "L2_gnn_ln_beta", "L3_gnn_w1", "L3_gnn_sw1", "L3_gnn_b1",
        "L3_gnn_w2", "L3_gnn_sw2", "L3_gnn_b2"]


def kernel(**inputs):
    import numpy as np
    import concourse.bacc as bacc
    from concourse.bass_utils import run_bass_kernel_spmd

    nc = bacc.Bacc("TRN2", target_bir_lowering=False, num_devices=1)
    arrays, tensors = {}, {}
    for name in _INS:
        a = np.ascontiguousarray(inputs[name])
        arrays[f"in_{name}"] = a
        tensors[name] = nc.dram_tensor(f"in_{name}", a.shape, mybir.dt.from_np(a.dtype), kind="ExternalInput").ap()
    out = nc.dram_tensor("out_nodes", inputs["x"].shape, F32, kind="ExternalOutput").ap()
    gnn(nc, tensors, out)
    return run_bass_kernel_spmd(nc, [arrays], core_ids=[0]).results[0]["out_nodes"]
```
